# Optimizing a Trainium2 kernel written in Bass

```python
import numpy as np
import jax
import jax.numpy as jnp

def _softmax(x, axis=-1):
    return jax.nn.softmax(x, axis=axis)

def _gelu(x):
    return jax.nn.gelu(x, approximate=True)

def _silu(x):
    return jax.nn.silu(x)

def _sigmoid(x):
    return jax.nn.sigmoid(x)

def _layernorm(x, axis=-1, eps=1e-05):
    m = jnp.mean(x, axis=axis, keepdims=True)
    v = jnp.var(x, axis=axis, keepdims=True)
    return (x - m) / jnp.sqrt(v + eps)

def _scatter_add(tgt, idx, src, axis=0):
    return tgt.at[idx].add(src)

def _segment_sum(src, seg, n):
    return jax.ops.segment_sum(src, seg, n)
kernel_name = 'mk_xattn_ffn_d4_seqx_r8_6f5333'

def setup_inputs(seed: int=0):
    np.random.seed(seed)
    _w = jnp.asarray

    def _rec_inputs():
        import jax
        import jax.numpy as jnp
        _rk = jax.random.key(seed)
        x = -0.0005207 + 1.001 * jax.random.normal(jax.random.fold_in(_rk, 1), (64, 128, 128), jnp.float32)
        _lenS = 128 - jax.random.randint(jax.random.fold_in(_rk, 7), (64,), 0, max(1, 128 // 4) + 1, jnp.int32)
        _lenS2 = 77 - jax.random.randint(jax.random.fold_in(_rk, 8), (64,), 0, max(1, 77 // 4) + 1, jnp.int32)
        _ctx_1024P = jax.random.normal(jax.random.fold_in(_rk, 12), (64, 16, 128), jnp.float32)
        _ctx_1024c = jax.random.dirichlet(jax.random.fold_in(_rk, 512), 0.3 * jnp.ones((16,), jnp.float32), (64, 77))
        _ctx_1024t = jnp.einsum('bsk,bkd->bsd', _ctx_1024c, _ctx_1024P)
        _ctx_1024t = _ctx_1024t * jax.lax.rsqrt(jnp.mean(jnp.square(_ctx_1024t)) + 1e-12) * 0.953939
        ctx_1024 = 0.00191187 + 0.999416 * (_ctx_1024t + 0.3 * jax.random.normal(jax.random.fold_in(_rk, 612), (64, 77, 128), jnp.float32))
        _validS = jnp.arange(128)[None, :] < _lenS[:, None]
        _validS2 = jnp.arange(77)[None, :] < _lenS2[:, None]
        _causal = jnp.tril(jnp.ones((128, 128), dtype=bool))
        mask_BxS_ff1 = jnp.where(jnp.ones((64, 128), dtype=bool), 1.0, 0.0).astype(jnp.float32)
        mask_BxS2_ik0 = jnp.where(jnp.broadcast_to(_validS2[:, :], (64, 77)), 0, 1).astype(jnp.int32)
        mask_Bx1xSxS2_fk0 = jnp.where(jnp.broadcast_to(_validS2[:, None, None, :], (64, 1, 128, 77)), 0.0, 1.0).astype(jnp.float32)
        return (x, ctx_1024, mask_BxS_ff1, mask_BxS2_ik0, mask_Bx1xSxS2_fk0)
    x, ctx_1024, mask_BxS_ff1, mask_BxS2_ik0, mask_Bx1xSxS2_fk0 = _rec_inputs()

    def _L0_xattn_setup():
        import jax, jax.numpy as jnp
        import numpy as np
        B, F, T, D = (8, 32, 32, 128)
        NEG = -1e+30
        key = jax.random.key(seed)
        ks = jax.random.split(key, 10)
        s = 1.0 / np.sqrt(D)
        return {'features': jax.random.normal(ks[0], (B, F, D), jnp.float32), 'masks': jnp.ones((B, F), jnp.float32), 'textual_features': jax.random.normal(ks[1], (B, T, D), jnp.float32), 'q_masks': jax.random.randint(ks[2], (B, T), 0, 2, jnp.int32), 'Ws': jax.random.normal(ks[3], (D, D), jnp.float32) * s, 'W': jax.random.normal(ks[4], (D, D), jnp.float32) * s, 'w': jax.random.normal(ks[5], (D, 1), jnp.float32) * s, 'b': jax.random.normal(ks[6], (1, D), jnp.float32) * s, 'Wcw': jax.random.normal(ks[7], (1, D), jnp.float32) * s, 'bcw': jnp.zeros((1,), jnp.float32), 'Wcb': jax.random.normal(ks[8], (1, D), jnp.float32) * s, 'bcb': jnp.zeros((1,), jnp.float32)}
    _L0_xattn_all = _L0_xattn_setup()
    _L0_xattn_in = {k: v for k, v in _L0_xattn_all.items() if k in ('Ws', 'W', 'w', 'b', 'Wcw', 'bcw', 'Wcb', 'bcb')}
    del _L0_xattn_all

    def _L0_ffn_setup():
        import jax, jax.numpy as jnp
        import numpy as np
        N_EXPERTS = 16
        TOP_K = 4
        HIDDEN = 128
        INTER = 64
        B, S = (2, 128)
        key = jax.random.key(seed)
        k1, k2, k3, k4, k5 = jax.random.split(key, 5)
        return {'hidden_states': jax.random.normal(k1, (B, S, HIDDEN), dtype=jnp.float32), 'gate_w': jax.random.normal(k2, (N_EXPERTS, HIDDEN), dtype=jnp.float32) * 0.02, 'w1': jax.random.normal(k3, (N_EXPERTS, HIDDEN, INTER), dtype=jnp.float32) * 0.02, 'w3': jax.random.normal(k4, (N_EXPERTS, HIDDEN, INTER), dtype=jnp.float32) * 0.02, 'w2': jax.random.normal(k5, (N_EXPERTS, INTER, HIDDEN), dtype=jnp.float32) * 0.02}
    _L0_ffn_all = _L0_ffn_setup()
    _L0_ffn_in = {k: v for k, v in _L0_ffn_all.items() if k in ('gate_w', 'w1', 'w3', 'w2')}
    del _L0_ffn_all

    def _L1_xattn_setup():
        import jax, jax.numpy as jnp
        import numpy as np
        EMBED_DIM = 128
        N_HEADS = 16
        HEAD_DIM = EMBED_DIM // N_HEADS
        key = jax.random.key(seed)
        ks = jax.random.split(key, 8)
        B, Tq, Tk, C = (2, 256, 256, EMBED_DIM)
        s = 1.0 / np.sqrt(C)
        return {'query': jax.random.normal(ks[0], (B, Tq, C), jnp.float32), 'context': jax.random.normal(ks[1], (B, Tk, C), jnp.float32), 'Wq': jax.random.normal(ks[2], (C, C), jnp.float32) * s, 'bq': jnp.zeros((C,), jnp.float32), 'Wkv': jax.random.normal(ks[3], (C, 2 * C), jnp.float32) * s, 'bkv': jnp.zeros((2 * C,), jnp.float32), 'Wo': jax.random.normal(ks[4], (C, C), jnp.float32) * s, 'bo': jnp.zeros((C,), jnp.float32)}
    _L1_xattn_all = _L1_xattn_setup()
    _L1_xattn_in = {k: v for k, v in _L1_xattn_all.items() if k in ('Wq', 'bq', 'Wkv', 'bkv', 'Wo', 'bo')}
    del _L1_xattn_all

    def _L1_ffn_setup():
        import jax, jax.numpy as jnp
        import numpy as np
        D = 128
        H = 128
        E = 8
        K = 2
        I = 2 * 128
        ROUTE_SCALE = 1.0
        key = jax.random.key(seed)
        ks = jax.random.split(key, 12)
        s = lambda *sh: 1.0 / np.sqrt(sh[-1])
        return {'x': jax.random.normal(ks[0], (1, 256, D), jnp.float32), 'gate_w': jax.random.normal(ks[1], (E, D), jnp.float32) * s(E, D), 'w1': jax.random.normal(ks[2], (E, H, D), jnp.float32) * s(H, D), 'b1': jax.random.normal(ks[3], (E, H), jnp.float32) * 0.01, 'w2': jax.random.normal(ks[4], (E, D, H), jnp.float32) * s(D, H), 'b2': jax.random.normal(ks[5], (E, D), jnp.float32) * 0.01, 'w3': jax.random.normal(ks[6], (E, H, D), jnp.float32) * s(H, D), 'b3': jax.random.normal(ks[7], (E, H), jnp.float32) * 0.01, 'sw1': jax.random.normal(ks[8], (I, D), jnp.float32) * s(I, D), 'sw2': jax.random.normal(ks[9], (I, D), jnp.float32) * s(I, D), 'sw3': jax.random.normal(ks[10], (D, I), jnp.float32) * s(D, I)}
    _L1_ffn_all = _L1_ffn_setup()
    _L1_ffn_in = {k: v for k, v in _L1_ffn_all.items() if k in ('gate_w', 'w1', 'b1', 'w2', 'b2', 'w3', 'b3', 'sw1', 'sw2', 'sw3')}
    del _L1_ffn_all

    def _L2_xattn_setup():
        import jax, jax.numpy as jnp
        import numpy as np
        D_MODEL = 128
        N_HEADS = 16
        DEPTH = D_MODEL // N_HEADS
        B, S = (2, 256)

        def _split_heads(x):
            b, s, _ = x.shape
            return x.reshape(b, s, N_HEADS, DEPTH).transpose(0, 2, 1, 3)
        key = jax.random.key(seed)
        ks = jax.random.split(key, 13)
        scale = 1.0 / np.sqrt(D_MODEL)
        inp = {'query': jax.random.normal(ks[0], (B, S, D_MODEL), jnp.float32), 'key': jax.random.normal(ks[1], (B, S, D_MODEL), jnp.float32), 'value': jax.random.normal(ks[2], (B, S, D_MODEL), jnp.float32), 'mask': (jax.random.uniform(ks[3], (B, 1, S, S)) < 0.1).astype(jnp.float32), 'Wq': jax.random.normal(ks[4], (D_MODEL, D_MODEL), jnp.float32) * scale, 'bq': jnp.zeros((D_MODEL,), jnp.float32), 'Wk': jax.random.normal(ks[5], (D_MODEL, D_MODEL), jnp.float32) * scale, 'bk': jnp.zeros((D_MODEL,), jnp.float32), 'Wv': jax.random.normal(ks[6], (D_MODEL, D_MODEL), jnp.float32) * scale, 'bv': jnp.zeros((D_MODEL,), jnp.float32), 'Wo': jax.random.normal(ks[7], (D_MODEL, D_MODEL), jnp.float32) * scale, 'bo': jnp.zeros((D_MODEL,), jnp.float32)}
        return inp
    _L2_xattn_all = _L2_xattn_setup()
    _L2_xattn_in = {k: v for k, v in _L2_xattn_all.items() if k in ('Wq', 'bq', 'Wk', 'bk', 'Wv', 'bv', 'Wo', 'bo')}
    del _L2_xattn_all

    def _L2_ffn_setup():
        import jax, jax.numpy as jnp
        import numpy as np
        B, T, D, E, H = (4, 256, 128, 4, 8)
        EPS = 1e-05

        def _uniform(k, shape, bound):
            return jax.random.uniform(k, shape, jnp.float32, -bound, bound)

        def _layernorm(x, w, b):
            mu = jnp.mean(x, axis=-1, keepdims=True)
            var = jnp.mean(jnp.square(x - mu), axis=-1, keepdims=True)
            return (x - mu) * jax.lax.rsqrt(var + EPS) * w + b
        key = jax.random.key(seed)
        ks = jax.random.split(key, 12)
        wb = np.sqrt(6.0 / D) / np.sqrt(6.0)
        wb = 1.0 / np.sqrt(D)
        return {'x': jax.random.normal(ks[0], (B, T, D), jnp.float32), 'router_prob': jax.random.uniform(ks[1], (B, T, E), jnp.float32), 'norm_w': jnp.ones((D,), jnp.float32), 'norm_b': jnp.zeros((D,), jnp.float32), 'q_w': _uniform(ks[2], (D, D), wb), 'q_b': _uniform(ks[3], (D,), wb), 'k_w': _uniform(ks[4], (D, D), wb), 'k_b': _uniform(ks[5], (D,), wb), 'v_w': _uniform(ks[6], (D, D), wb), 'v_b': _uniform(ks[7], (D,), wb), 'o_w': _uniform(ks[8], (D, D), wb), 'o_b': _uniform(ks[9], (D,), wb)}
    _L2_ffn_all = _L2_ffn_setup()
    _L2_ffn_in = {k: v for k, v in _L2_ffn_all.items() if k in ('router_prob', 'norm_w', 'norm_b', 'q_w', 'q_b', 'k_w', 'k_b', 'v_w', 'v_b', 'o_w', 'o_b')}
    del _L2_ffn_all

    def _L3_xattn_setup():
        import jax, jax.numpy as jnp
        import numpy as np
        D_MODEL = 128
        N_HEADS = 16
        RANK = 128
        TOPK = 64
        D_HEAD = D_MODEL // N_HEADS
        SCALE = D_HEAD ** (-0.5)
        INIT_SCALE = 0.05

        def _lowrank_proj(x, U, V, b):
            return jnp.einsum('btr,dr->btd', jnp.einsum('btd,dr->btr', x, U), V) + b

        def _heads(x, B, T):
            return x.reshape(B, T, N_HEADS, D_HEAD).transpose(0, 2, 1, 3)

        def _topk_softmax(scores, k):
            B, H, L, S = scores.shape
            flat = scores.reshape(-1, S)
            vals, idx = jax.lax.top_k(flat, k)
            p = jax.nn.softmax(vals, axis=-1)
            rows = jnp.arange(flat.shape[0])[:, None]
            attn = jnp.zeros_like(flat).at[rows, idx].set(p)
            return attn.reshape(B, H, L, S)
        key = jax.random.key(seed)
        ks = jax.random.split(key, 11)
        B, L, S = (2, 256, 256)
        inp = {'q': jax.random.normal(ks[0], (B, L, D_MODEL), jnp.float32), 'k': jax.random.normal(ks[1], (B, S, D_MODEL), jnp.float32), 'v': jax.random.normal(ks[2], (B, S, D_MODEL), jnp.float32)}
        names = ['q', 'k', 'v', 'o']
        for i, n in enumerate(names):
            inp[f'U{n}'] = jax.random.normal(ks[3 + 2 * i], (D_MODEL, RANK), jnp.float32) * INIT_SCALE
            inp[f'V{n}'] = jax.random.normal(ks[4 + 2 * i], (D_MODEL, RANK), jnp.float32) * INIT_SCALE
            inp[f'b{n}'] = jnp.zeros((D_MODEL,), jnp.float32)
        return inp
    _L3_xattn_all = _L3_xattn_setup()
    _L3_xattn_in = {k: v for k, v in _L3_xattn_all.items() if k in ('Uq', 'Vq', 'bq', 'Uk', 'Vk', 'bk', 'Uv', 'Vv', 'bv', 'Uo', 'Vo', 'bo')}
    del _L3_xattn_all

    def _L3_ffn_setup():
        import jax, jax.numpy as jnp
        import numpy as np
        S, B, H = (256, 4, 128)
        E = 64
        K = 4
        I = 64
        CAP = 128
        key = jax.random.key(seed)
        k1, k2, k3, k4 = jax.random.split(key, 4)
        return {'hidden_states': jax.random.normal(k1, (S, B, H), dtype=jnp.float32), 'router_w': jax.random.normal(k2, (H, E), dtype=jnp.float32) * 0.02, 'w1': jax.random.normal(k3, (E, H, 2 * I), dtype=jnp.float32) * 0.02, 'w2': jax.random.normal(k4, (E, I, H), dtype=jnp.float32) * 0.02}
    _L3_ffn_all = _L3_ffn_setup()
    _L3_ffn_in = {k: v for k, v in _L3_ffn_all.items() if k in ('router_w', 'w1', 'w2')}
    del _L3_ffn_all
    return {'x': x, 'ctx_1024': ctx_1024, 'mask_BxS_ff1': mask_BxS_ff1, 'mask_BxS2_ik0': mask_BxS2_ik0, 'mask_Bx1xSxS2_fk0': mask_Bx1xSxS2_fk0, 'L0_xattn_Ws': _L0_xattn_in['Ws'], 'L0_xattn_W': _L0_xattn_in['W'], 'L0_xattn_w': _L0_xattn_in['w'], 'L0_xattn_b': _L0_xattn_in['b'], 'L0_xattn_Wcw': _L0_xattn_in['Wcw'], 'L0_xattn_bcw': _L0_xattn_in['bcw'], 'L0_xattn_Wcb': _L0_xattn_in['Wcb'], 'L0_xattn_bcb': _L0_xattn_in['bcb'], 'L0_ffn_gate_w': _L0_ffn_in['gate_w'], 'L0_ffn_w1': _L0_ffn_in['w1'], 'L0_ffn_w3': _L0_ffn_in['w3'], 'L0_ffn_w2': _L0_ffn_in['w2'], 'L1_xattn_Wq': _L1_xattn_in['Wq'], 'L1_xattn_bq': _L1_xattn_in['bq'], 'L1_xattn_Wkv': _L1_xattn_in['Wkv'], 'L1_xattn_bkv': _L1_xattn_in['bkv'], 'L1_xattn_Wo': _L1_xattn_in['Wo'], 'L1_xattn_bo': _L1_xattn_in['bo'], 'L1_ffn_gate_w': _L1_ffn_in['gate_w'], 'L1_ffn_w1': _L1_ffn_in['w1'], 'L1_ffn_b1': _L1_ffn_in['b1'], 'L1_ffn_w2': _L1_ffn_in['w2'], 'L1_ffn_b2': _L1_ffn_in['b2'], 'L1_ffn_w3': _L1_ffn_in['w3'], 'L1_ffn_b3': _L1_ffn_in['b3'], 'L1_ffn_sw1': _L1_ffn_in['sw1'], 'L1_ffn_sw2': _L1_ffn_in['sw2'], 'L1_ffn_sw3': _L1_ffn_in['sw3'], 'L2_xattn_Wq': _L2_xattn_in['Wq'], 'L2_xattn_bq': _L2_xattn_in['bq'], 'L2_xattn_Wk': _L2_xattn_in['Wk'], 'L2_xattn_bk': _L2_xattn_in['bk'], 'L2_xattn_Wv': _L2_xattn_in['Wv'], 'L2_xattn_bv': _L2_xattn_in['bv'], 'L2_xattn_Wo': _L2_xattn_in['Wo'], 'L2_xattn_bo': _L2_xattn_in['bo'], 'L2_ffn_router_prob': _L2_ffn_in['router_prob'], 'L2_ffn_norm_w': _L2_ffn_in['norm_w'], 'L2_ffn_norm_b': _L2_ffn_in['norm_b'], 'L2_ffn_q_w': _L2_ffn_in['q_w'], 'L2_ffn_q_b': _L2_ffn_in['q_b'], 'L2_ffn_k_w': _L2_ffn_in['k_w'], 'L2_ffn_k_b': _L2_ffn_in['k_b'], 'L2_ffn_v_w': _L2_ffn_in['v_w'], 'L2_ffn_v_b': _L2_ffn_in['v_b'], 'L2_ffn_o_w': _L2_ffn_in['o_w'], 'L2_ffn_o_b': _L2_ffn_in['o_b'], 'L3_xattn_Uq': _L3_xattn_in['Uq'], 'L3_xattn_Vq': _L3_xattn_in['Vq'], 'L3_xattn_bq': _L3_xattn_in['bq'], 'L3_xattn_Uk': _L3_xattn_in['Uk'], 'L3_xattn_Vk': _L3_xattn_in['Vk'], 'L3_xattn_bk': _L3_xattn_in['bk'], 'L3_xattn_Uv': _L3_xattn_in['Uv'], 'L3_xattn_Vv': _L3_xattn_in['Vv'], 'L3_xattn_bv': _L3_xattn_in['bv'], 'L3_xattn_Uo': _L3_xattn_in['Uo'], 'L3_xattn_Vo': _L3_xattn_in['Vo'], 'L3_xattn_bo': _L3_xattn_in['bo'], 'L3_ffn_router_w': _L3_ffn_in['router_w'], 'L3_ffn_w1': _L3_ffn_in['w1'], 'L3_ffn_w2': _L3_ffn_in['w2']}

def reference(x, ctx_1024, mask_BxS_ff1, mask_BxS2_ik0, mask_Bx1xSxS2_fk0, L0_xattn_Ws, L0_xattn_W, L0_xattn_w, L0_xattn_b, L0_xattn_Wcw, L0_xattn_bcw, L0_xattn_Wcb, L0_xattn_bcb, L0_ffn_gate_w, L0_ffn_w1, L0_ffn_w3, L0_ffn_w2, L1_xattn_Wq, L1_xattn_bq, L1_xattn_Wkv, L1_xattn_bkv, L1_xattn_Wo, L1_xattn_bo, L1_ffn_gate_w, L1_ffn_w1, L1_ffn_b1, L1_ffn_w2, L1_ffn_b2, L1_ffn_w3, L1_ffn_b3, L1_ffn_sw1, L1_ffn_sw2, L1_ffn_sw3, L2_xattn_Wq, L2_xattn_bq, L2_xattn_Wk, L2_xattn_bk, L2_xattn_Wv, L2_xattn_bv, L2_xattn_Wo, L2_xattn_bo, L2_ffn_router_prob, L2_ffn_norm_w, L2_ffn_norm_b, L2_ffn_q_w, L2_ffn_q_b, L2_ffn_k_w, L2_ffn_k_b, L2_ffn_v_w, L2_ffn_v_b, L2_ffn_o_w, L2_ffn_o_b, L3_xattn_Uq, L3_xattn_Vq, L3_xattn_bq, L3_xattn_Uk, L3_xattn_Vk, L3_xattn_bk, L3_xattn_Uv, L3_xattn_Vv, L3_xattn_bv, L3_xattn_Uo, L3_xattn_Vo, L3_xattn_bo, L3_ffn_router_w, L3_ffn_w1, L3_ffn_w2):
    import jax
    import jax.numpy as jnp

    def _L0_xattn_ref(features, masks, textual_features, q_masks, Ws, W, w, b, Wcw, bcw, Wcb, bcb):
        import jax, jax.numpy as jnp
        import numpy as np
        B, F, T, D = (8, 32, 32, 128)
        NEG = -1e+30
        txt_proj = jnp.einsum('btd,de->bte', textual_features, Ws)
        feat_proj = jnp.einsum('bfd,de->bfe', features, W)
        h = jnp.tanh(txt_proj[:, None, :, :] + feat_proj[:, :, None, :] + b[None, None, :, :][..., 0, :])
        rho = jnp.einsum('bftd,d->bft', h, w[:, 0])
        qm = q_masks.astype(jnp.float32)
        rho = rho + (1.0 - qm)[:, None, :] * NEG
        att = jax.nn.softmax(rho, axis=-1)
        txt_h = jnp.einsum('bft,btd->bfd', att, textual_features)
        w_s = jnp.tanh(jnp.einsum('bfd,od->bfo', txt_h, Wcw) + bcw)
        b_s = jnp.tanh(jnp.einsum('bfd,od->bfo', txt_h, Wcb) + bcb)
        return w_s * features + b_s

    def _L0_ffn_ref(hidden_states, gate_w, w1, w3, w2):
        import jax, jax.numpy as jnp
        import numpy as np
        N_EXPERTS = 16
        TOP_K = 4
        HIDDEN = 128
        INTER = 64
        B, S = (2, 128)
        'DeepseekV3 MoE adapter forward: router -> sparse scores -> expert GLU MLP -> combine.'
        b, s, h = hidden_states.shape
        x = hidden_states.reshape(-1, h)
        logits = jnp.einsum('th,eh->te', x, gate_w)
        probs = jax.nn.softmax(logits, axis=-1)
        topk_w, topk_idx = jax.lax.top_k(probs, TOP_K)
        topk_w = topk_w / jnp.sum(topk_w, axis=-1, keepdims=True)
        one_hot = (topk_idx[..., None] == jnp.arange(N_EXPERTS)).astype(topk_w.dtype)
        scores = jnp.einsum('tk,tke->te', topk_w, one_hot)
        g = jnp.einsum('th,ehi->tei', x, w1)
        u = jnp.einsum('th,ehi->tei', x, w3)
        act = jax.nn.silu(g) * u
        expert_out = jnp.einsum('tei,eih->teh', act, w2)
        out = jnp.einsum('teh,te->th', expert_out, scores)
        return out.reshape(b, s, h)

    def _L1_xattn_ref(query, context, Wq, bq, Wkv, bkv, Wo, bo):
        import jax, jax.numpy as jnp
        import numpy as np
        EMBED_DIM = 128
        N_HEADS = 16
        HEAD_DIM = EMBED_DIM // N_HEADS
        B, Tq, C = query.shape
        Tk = context.shape[1]
        H, D = (N_HEADS, HEAD_DIM)
        q = (query @ Wq + bq).reshape(B, Tq, H, D)
        kv = (context @ Wkv + bkv).reshape(B, Tk, 2, H, D)
        k = kv[:, :, 0]
        v = kv[:, :, 1]
        scale = D ** (-0.5)
        attn = jnp.einsum('bqhd,bkhd->bhqk', q, k) * scale
        attn = jax.nn.softmax(attn, axis=-1)
        out = jnp.einsum('bhqk,bkhd->bqhd', attn, v).reshape(B, Tq, C)
        return out @ Wo + bo

    def _L1_ffn_ref(x, gate_w, w1, b1, w2, b2, w3, b3, sw1, sw2, sw3):
        import jax, jax.numpy as jnp
        import numpy as np
        D = 128
        H = 128
        E = 8
        K = 2
        I = 2 * 128
        ROUTE_SCALE = 1.0
        B, S, _ = x.shape
        xt = x.reshape(-1, D)
        logits = xt @ gate_w.T
        scores = jax.nn.softmax(logits.astype(jnp.float32), axis=-1)
        top_vals, idx = jax.lax.top_k(scores, K)
        weights = jnp.take_along_axis(scores, idx, axis=1).astype(x.dtype) * ROUTE_SCALE
        xs = xt[:, None, :] * weights[:, :, None]
        y = jnp.zeros_like(xt)
        for e in range(E):
            mask = (idx == e).astype(x.dtype)
            h = jax.nn.silu(jnp.einsum('tkd,hd->tkh', xs, w1[e]) + b1[e])
            x2 = jnp.einsum('tkh,dh->tkd', h, w2[e]) + b2[e]
            x3 = jnp.einsum('tkd,hd->tkh', xs, w3[e]) + b3[e]
            y = y + jnp.sum(x2 * x3 * mask[:, :, None], axis=1)
        z = jax.nn.silu(xt @ sw1.T) * (xt @ sw2.T) @ sw3.T
        return (y + z).reshape(B, S, D)

    def _L2_xattn_ref(query, key, value, mask, Wq, bq, Wk, bk, Wv, bv, Wo, bo):
        import jax, jax.numpy as jnp
        import numpy as np
        D_MODEL = 128
        N_HEADS = 16
        DEPTH = D_MODEL // N_HEADS
        B, S = (2, 256)

        def _split_heads(x):
            b, s, _ = x.shape
            return x.reshape(b, s, N_HEADS, DEPTH).transpose(0, 2, 1, 3)
        q = _split_heads(query @ Wq.T + bq)
        k = _split_heads(key @ Wk.T + bk)
        v = _split_heads(value @ Wv.T + bv)
        scores = jnp.einsum('bhqd,bhkd->bhqk', q, k) / jnp.sqrt(jnp.float32(DEPTH))
        scores = scores + mask * jnp.float32(-1000000000.0)
        weights = jax.nn.softmax(scores, axis=-1)
        ctx = jnp.einsum('bhqk,bhkd->bhqd', weights, v)
        ctx = ctx.transpose(0, 2, 1, 3).reshape(query.shape[0], -1, D_MODEL)
        return ctx @ Wo.T + bo

    def _L2_ffn_ref(x, router_prob, norm_w, norm_b, q_w, q_b, k_w, k_b, v_w, v_b, o_w, o_b):
        import jax, jax.numpy as jnp
        import numpy as np
        B, T, D, E, H = (4, 256, 128, 4, 8)
        EPS = 1e-05

        def _uniform(k, shape, bound):
            return jax.random.uniform(k, shape, jnp.float32, -bound, bound)

        def _layernorm(x, w, b):
            mu = jnp.mean(x, axis=-1, keepdims=True)
            var = jnp.mean(jnp.square(x - mu), axis=-1, keepdims=True)
            return (x - mu) * jax.lax.rsqrt(var + EPS) * w + b
        e_cnt = router_prob.shape[2]
        b, t, d = x.shape
        n = t // e_cnt
        h = H
        scale = d ** (-0.5)
        qs, ks_, vs = ([], [], [])
        for e in range(e_cnt):
            xe = x[:, e * n:(e + 1) * n, :]
            xn = _layernorm(xe, norm_w, norm_b)
            m = d // 2 ** e
            xm = xn[..., :m]
            qs.append(jnp.einsum('bnm,dm->bnd', xm, q_w[:, :m]) + q_b)
            ks_.append(jnp.einsum('bnm,dm->bnd', xm, k_w[:, :m]) + k_b)
            vs.append(jnp.einsum('bnm,dm->bnd', xm, v_w[:, :m]) + v_b)
        q = jnp.concatenate(qs, axis=1)
        k = jnp.concatenate(ks_, axis=1)
        v = jnp.concatenate(vs, axis=1)
        dh = d // h
        q = q.reshape(b, t, h, dh).transpose(0, 2, 1, 3)
        k = k.reshape(b, t, h, dh).transpose(0, 2, 1, 3)
        v = v.reshape(b, t, h, dh).transpose(0, 2, 1, 3)
        attn = jnp.einsum('bhqd,bhkd->bhqk', q, k) * scale
        attn = jax.nn.softmax(attn, axis=-1)
        attn_out = jnp.einsum('bhqk,bhkd->bhqd', attn, v)
        attn_out = attn_out.transpose(0, 2, 1, 3).reshape(b, t, d)
        outs = []
        for e in range(e_cnt):
            sl = slice(e * n, (e + 1) * n)
            m = d // 2 ** e
            xm = attn_out[:, sl, :m]
            out = jnp.einsum('bnm,om->bno', xm, o_w[:m, :m]) + o_b[:m]
            pad = d - m
            if pad:
                out = jnp.pad(out, ((0, 0), (0, 0), (0, pad)))
            outs.append(out + x[:, sl, :])
        return jnp.concatenate(outs, axis=1)

    def _L3_xattn_ref(q, k, v, Uq, Vq, bq, Uk, Vk, bk, Uv, Vv, bv, Uo, Vo, bo):
        import jax, jax.numpy as jnp
        import numpy as np
        D_MODEL = 128
        N_HEADS = 16
        RANK = 128
        TOPK = 64
        D_HEAD = D_MODEL // N_HEADS
        SCALE = D_HEAD ** (-0.5)
        INIT_SCALE = 0.05

        def _lowrank_proj(x, U, V, b):
            return jnp.einsum('btr,dr->btd', jnp.einsum('btd,dr->btr', x, U), V) + b

        def _heads(x, B, T):
            return x.reshape(B, T, N_HEADS, D_HEAD).transpose(0, 2, 1, 3)

        def _topk_softmax(scores, k):
            B, H, L, S = scores.shape
            flat = scores.reshape(-1, S)
            vals, idx = jax.lax.top_k(flat, k)
            p = jax.nn.softmax(vals, axis=-1)
            rows = jnp.arange(flat.shape[0])[:, None]
            attn = jnp.zeros_like(flat).at[rows, idx].set(p)
            return attn.reshape(B, H, L, S)
        B, L, _ = q.shape
        S = k.shape[1]
        qh = _heads(_lowrank_proj(q, Uq, Vq, bq), B, L)
        kh = _heads(_lowrank_proj(k, Uk, Vk, bk), B, S)
        vh = _heads(_lowrank_proj(v, Uv, Vv, bv), B, S)
        scores = jnp.einsum('bhld,bhsd->bhls', qh, kh) * SCALE
        dyn_k = min(TOPK, S)
        attn = _topk_softmax(scores, dyn_k)
        out = jnp.einsum('bhls,bhsd->bhld', attn, vh)
        out = out.transpose(0, 2, 1, 3).reshape(B, L, D_MODEL)
        return _lowrank_proj(out, Uo, Vo, bo)

    def _L3_ffn_ref(hidden_states, router_w, w1, w2):
        import jax, jax.numpy as jnp
        import numpy as np
        S, B, H = (256, 4, 128)
        E = 64
        K = 4
        I = 64
        CAP = 128
        s, b, h = hidden_states.shape
        x = hidden_states.reshape(-1, h)
        T = x.shape[0]
        P = T * K
        logits = x @ router_w
        probs_all = jax.nn.softmax(logits, axis=-1)
        top_p, top_i = jax.lax.top_k(probs_all, K)
        rows = jnp.arange(T)[:, None]
        routing_map = jnp.zeros((T, E), dtype=bool).at[rows, top_i].set(True)
        probs = jnp.zeros((T, E), dtype=x.dtype).at[rows, top_i].set(top_p)
        flat = routing_map.T.reshape(-1)
        order = jnp.argsort((~flat).astype(jnp.int32), stable=True)[:P]
        expert_id = order // T
        token_idx = order % T
        group_sizes = routing_map.sum(axis=0)
        starts = jnp.cumsum(group_sizes) - group_sizes
        pos = jnp.arange(P) - starts[expert_id]
        perm_x = x[token_idx]
        buf = jnp.zeros((E, CAP, h), dtype=x.dtype).at[expert_id, pos].set(perm_x)
        h1 = jnp.einsum('ech,ehf->ecf', buf, w1)
        g = jax.nn.silu(h1[..., :I]) * h1[..., I:]
        y = jnp.einsum('eci,eih->ech', g, w2)
        perm_y = y[expert_id, pos]
        perm_probs = probs.T.reshape(-1)[order]
        out = jnp.zeros((T, h), dtype=x.dtype).at[token_idx].add(perm_y * perm_probs[:, None])
        return out.reshape(s, b, h)
    x = x + _L0_xattn_ref(_layernorm(x, axis=-1), mask_BxS_ff1, ctx_1024, mask_BxS2_ik0, L0_xattn_Ws, L0_xattn_W, L0_xattn_w, L0_xattn_b, L0_xattn_Wcw, L0_xattn_bcw, L0_xattn_Wcb, L0_xattn_bcb)
    x = x + _L0_ffn_ref(_layernorm(x, axis=-1), L0_ffn_gate_w, L0_ffn_w1, L0_ffn_w3, L0_ffn_w2)
    x = x + _L1_xattn_ref(_layernorm(x, axis=-1), ctx_1024, L1_xattn_Wq, L1_xattn_bq, L1_xattn_Wkv, L1_xattn_bkv, L1_xattn_Wo, L1_xattn_bo)
    x = x + _L1_ffn_ref(_layernorm(x, axis=-1), L1_ffn_gate_w, L1_ffn_w1, L1_ffn_b1, L1_ffn_w2, L1_ffn_b2, L1_ffn_w3, L1_ffn_b3, L1_ffn_sw1, L1_ffn_sw2, L1_ffn_sw3)
    x = x + _L2_xattn_ref(_layernorm(x, axis=-1), ctx_1024, ctx_1024, mask_Bx1xSxS2_fk0, L2_xattn_Wq, L2_xattn_bq, L2_xattn_Wk, L2_xattn_bk, L2_xattn_Wv, L2_xattn_bv, L2_xattn_Wo, L2_xattn_bo)
    x = x + _L2_ffn_ref(_layernorm(x, axis=-1), L2_ffn_router_prob, L2_ffn_norm_w, L2_ffn_norm_b, L2_ffn_q_w, L2_ffn_q_b, L2_ffn_k_w, L2_ffn_k_b, L2_ffn_v_w, L2_ffn_v_b, L2_ffn_o_w, L2_ffn_o_b)
    x = x + _L3_xattn_ref(_layernorm(x, axis=-1), ctx_1024, ctx_1024, L3_xattn_Uq, L3_xattn_Vq, L3_xattn_bq, L3_xattn_Uk, L3_xattn_Vk, L3_xattn_bk, L3_xattn_Uv, L3_xattn_Vv, L3_xattn_bv, L3_xattn_Uo, L3_xattn_Vo, L3_xattn_bo)
    x = x + _L3_ffn_ref(_layernorm(x, axis=-1), L3_ffn_router_w, L3_ffn_w1, L3_ffn_w2)
    return x

_drawn_inputs = setup_inputs


def setup_inputs(seed=0):
    import zlib

    import numpy as np

    out = dict(_drawn_inputs(seed))
    spreads = {'L1_xattn_bq': (0.0, 0.354),
     'L1_xattn_bkv': (0.0, 0.1),
     'L1_xattn_bo': (0.0, 0.1),
     'L2_xattn_bq': (0.0, 0.48),
     'L2_xattn_bk': (0.0, 0.8),
     'L2_xattn_bv': (0.0, 0.1),
     'L2_xattn_bo': (0.0, 0.1),
     'L2_ffn_norm_w': (1.0, 0.6),
     'L2_ffn_norm_b': (0.0, 0.8),
     'L3_xattn_bq': (0.0, 0.8),
     'L3_xattn_bk': (0.0, 0.8),
     'L3_xattn_bv': (0.0, 0.574),
     'L3_xattn_bo': (0.0, 0.1)}
    factors = {'L0_xattn_b': 8.0,
     'L0_ffn_gate_w': 8.0,
     'L0_ffn_w1': 8.0,
     'L0_ffn_w3': 8.0,
     'L0_ffn_w2': 8.0,
     'L1_ffn_b1': 8.0,
     'L1_ffn_b2': 8.0,
     'L1_ffn_b3': 8.0,
     'L2_ffn_q_w': 8.0,
     'L2_ffn_q_b': 8.0,
     'L2_ffn_k_w': 8.0,
     'L2_ffn_k_b': 8.0,
     'L2_ffn_v_b': 8.0,
     'L2_ffn_o_b': 3.808,
     'L3_xattn_Uq': 8.0,
     'L3_xattn_Vq': 8.0,
     'L3_xattn_Uk': 8.0,
     'L3_xattn_Vk': 8.0,
     'L3_xattn_Vv': 2.708,
     'L3_ffn_router_w': 8.0,
     'L3_ffn_w1': 8.0,
     'L3_ffn_w2': 8.0}
    for name, (base, spread) in spreads.items():
        noise = np.random.default_rng([zlib.crc32(name.encode()), seed]).standard_normal(out[name].shape)
        drawn = base * np.exp(spread * noise) if base else spread * noise
        out[name] = jnp.asarray(drawn.astype(out[name].dtype))
    for name, factor in factors.items():
        out[name] = (out[name] * factor).astype(out[name].dtype)
    return out
```

```python
from contextlib import ExitStack

import concourse.bass as bass
from concourse import mybir

F32 = mybir.dt.float32
BF16 = mybir.dt.bfloat16
I32 = mybir.dt.int32
U32 = mybir.dt.uint32
ALU = mybir.AluOpType
ACT = mybir.ActivationFunctionType
AX = mybir.AxisListType.X

PHASES = range(0, 8)

B = 64
S = 128
D = 128
C = 77
EPS = 1e-5
BANK = 512
FAR = -3.0e38



class Named:
    pass

def real(i, n=B):
    return not isinstance(i, int) or 0 <= i < n


def past(i, back):
    return not isinstance(i, int) or i >= back


def nth_part(i, p, per, back=0):
    return i * per + (p + 1 - back)


def past_part(i, p, per, back):
    return not isinstance(i, int) or nth_part(i, p, per, back) > 0


def run_slots(eng, step, lead, tail, n=B):
    first, last = 4, (n - max(lead, 2)) // 2 * 2
    for s in range(-lead, first):
        step(s, s % 2, s // 2)
    with eng.Fori(0, (last - first) // 2) as j:
        h = eng.snap(j + first // 2)
        s0 = eng.snap(2 * h)
        for u in range(2):
            step(s0 + u, u, h)
    for s in range(last, n + tail):
        step(s, s % 2, s // 2)


class Signals(dict):

    def __init__(self, ctx, nc, prefix, names):
        super().__init__((n, nc.alloc_semaphore(f"{prefix}_{n}")) for n in names)
        self.done = {n: 0 for n in names}
        ctx.callback(self.give_back, nc)

    def nth(self, name, i, back=0, n=B):
        if isinstance(i, int):
            i = min(i - back, n - 1) + back
        return i + (self.done[name] + 1 - back)

    def give_back(self, nc):
        nc.clear_and_free_semaphores(list(self.values()))
        nc.all_engine_barrier()


def bcast(ap, axis, n):
    a = ap.unsqueeze(axis)
    shape = list(a.shape)
    shape[axis] = n
    return a.broadcast_to(shape)



def norm_stats(nc, m):
    k = m.norms
    m.norms += 1
    with ExitStack() as ctx:
        t = ctx.enter_context(nc.sbuf_tensor(f"norm_tmp{k}", [S, 4, B], F32))
        block = ctx.enter_context(nc.Block())
        mean_even, var_even = m.STATS[:, :, 1], m.STATS[:, :, 2]
        mean_odd, var_odd = m.STATS[:, :, 4], m.STATS[:, :, 5]

        @block.vector
        def _(dve):
            dve.tensor_tensor(t[:, 0, :], mean_even, mean_odd, ALU.add)
            dve.tensor_tensor(t[:, 1, :], mean_even, mean_odd, ALU.subtract)
            dve.tensor_tensor(t[:, 2, :], var_even, var_odd, ALU.add).then_inc(m.s_norm_a, 1)
            dve.wait_ge(m.s_norm_a, 4 * k + 1)
            dve.tensor_scalar(m.MEAN[:, :], t[:, 0, :], 0.5, None, ALU.mult)
            dve.tensor_tensor(t[:, 3, :], t[:, 1, :], t[:, 1, :], ALU.mult).then_inc(m.s_norm_a, 1)
            dve.wait_ge(m.s_norm_a, 4 * k + 2)
            dve.tensor_scalar(t[:, 1, :], t[:, 3, :], 0.25, EPS, ALU.mult, ALU.add).then_inc(m.s_norm_a, 1)
            dve.wait_ge(m.s_norm_a, 4 * k + 3)
            dve.scalar_tensor_tensor(out=t[:, 0, :], in0=t[:, 2, :], scalar=1.0 / D, in1=t[:, 1, :],
                                     op0=ALU.mult, op1=ALU.add).then_inc(m.s_norm_a, 1)

        @block.gpsimd
        def _(pool):
            pool.wait_ge(m.s_norm_a, 4 * k + 4)
            pool.tensor_tensor(m.RSTD[:, :], t[:, 0, :], m.MINUS_HALF[:, :], ALU.pow).then_inc(m.s_norm_b, 1)



def attention_layer(nc, m, k, w, heads, keys, scale, context=None, mask=None, topk=0, lowrank=False,
                    inner=None):
    dh = D // heads
    hpg = 32 // dh
    groups = heads // 4
    less_max = "T" if mask is not None or topk else "sfree"
    kv_base = m.ctx_loads
    mask_base = m.mask_loads
    q = m.at
    with ExitStack() as ctx:
        def sb(name, shape, dt=F32):
            return ctx.enter_context(nc.sbuf_tensor(f"a{k}_{name}", shape, dt))

        Wq, Wk, Wv, Wo = (sb(n, [D, D]) for n in ("Wq", "Wk", "Wv", "Wo"))
        bq = sb("bq", [D, 1])
        bqs = sb("bqs", [D, 1])
        bk = sb("bk", [D, 1])
        bv = sb("bv", [D, D])
        bo = sb("bo", [D, D])
        y = sb("y", [S, 2, D])
        yT = sb("yT", [D, 2, S])
        cT = sb("cT", [D, 2, C])
        qT = sb("qT", [D, 2, S])
        kblk = sb("kblk", [D, 2, hpg * keys])
        vaug = sb("vaug", [keys, 2, heads * 32])
        mx = sb("mx", [S, 2, heads])
        T = sb("T", [S, 2, heads * keys])
        Pr = sb("Pr", [keys, 2, heads * S])
        oT = sb("oT", [D, 2, groups * S])
        rec = sb("rec", [S, 2, heads])
        O = sb("O", [S, 2, D])
        OT = sb("OT", [D, 2, S])
        if mask is not None:
            mk = sb("mk", [S, 2, C])
        if topk:
            r1 = sb("r1", [S, 2, heads * 8])
            r2 = sb("r2", [S, 2, heads * 8])
        if lowrank:
            U = sb("U", [D, 4, D])
            V = sb("V", [D, 4, D])
        if inner is not None:
            nw = sb("nw", [D, 1])
            nb = sb("nb", [D, 1])
            y0 = sb("y0", [S, 2, D])
            in_stats = sb("in_stats", [S, 2, 6])
            in_mv = sb("in_mv", [S, 2, 2])
            in_var = sb("in_var", [S, 2, 1])
            in_rstd = sb("in_rstd", [S, 2, 1])
            xw = sb("xw", [D, 2, S])
            tmp = sb("tmp", [S, 2, D])

        PS = m.PS
        yT_ps = PS[:, 5, 0:128]
        qT_ps = PS[:, 5, 128:256]
        OT_ps = PS[:, 5, 256:384]
        kT_ps = PS[:, 7, 0:keys]
        v_ps = PS[0:keys, 7, 128:256]
        out_ps = PS[:, 7, 256:384]

        with nc.Block() as block:
            nload = [0]

            @block.sync
            def _(sp):
                def load(dst, src):
                    sp.dma_start(dst, src).then_inc(m.s_weights, 16)
                    nload[0] += 1
                if lowrank:
                    for n in range(4):
                        load(U[:, n, :], w.U[n])
                        load(V[:, n, :], w.V[n])
                else:
                    load(Wq[:, :], w.Wq)
                    load(Wk[:, :], w.Wk)
                    load(Wv[:, :], w.Wv)
                    load(Wo[:, :], w.Wo)
                load(bq[:, :], w.bq.unsqueeze(1))
                load(bk[:, :], w.bk.unsqueeze(1))
                load(bv[:, :], w.bv.partition_broadcast(D))
                load(bo[:, :], w.bo.partition_broadcast(D))
                if inner is not None:
                    load(nw[:, :], w.nw.unsqueeze(1))
                    load(nb[:, :], w.nb.unsqueeze(1))
            loaded = m.weight_loads + 16 * nload[0]

            @block.vector
            def _(dve):
                dve.memset(vaug[:, :, :], 0.0).then_inc(q["prep"], 1)
                dve.wait_ge(m.s_weights, loaded)
                dve.wait_ge(q["prep"], m.preps + 1)
                dve.memset(vaug[:, :, :].rearrange("p u (h e) -> p (u h) e", e=32)[:, :, dh:dh + 1], 1.0)
                if inner is not None:
                    dve.tensor_tensor(bo[:, :], bo[:, :], m.WIDTH_TOKENS[:, :], ALU.mult)
                dve.tensor_scalar(bqs[:, :], bq[:, :], scale, None, ALU.mult).then_inc(q["prep"], 1)
                if lowrank:
                    dve.wait_ge(q["fold"], 1)
                    for n, W in enumerate((Wq, Wk, Wv, Wo)):
                        last = dve.tensor_copy(W[:, :], PS[:, 0, n * D:(n + 1) * D])
                    last.then_inc(q["prep"], 1)

            @block.tensor
            def _(pe):
                if lowrank:
                    pe.wait_ge(m.s_weights, loaded)
                    for n in range(4):
                        last = pe.matmul(PS[:, 0, n * D:(n + 1) * D], U[:, n, :], V[:, n, :],
                                         start=True, stop=True)
                    last.then_inc(q["fold"], 1)
            m.weight_loads = loaded
            m.preps += 3 if lowrank else 2

        norm_stats(nc, m)

        block = ctx.enter_context(nc.Block())

        @block.sync
        def _(sp):
            def step(i, u, h):
                if context is not None:
                    if past(i, 2):
                        sp.wait_ge(q["proj"], q.nth("proj", i, 2))
                    sp.dma_start(cT[:, u, :], context[:, bass.ds(i, 1), :].rearrange("p a c -> p (a c)")) \
                        .then_inc(q[f"ctx{u}"], 16)
                if mask is not None:
                    if past(i, 2):
                        sp.wait_ge(q["sfree"], q.nth("sfree", i, 2))
                    sp.dma_start(mk[:, u, :], mask[:, bass.ds(i, 1), :].rearrange("p a c -> p (a c)")) \
                        .then_inc(q[f"mask{u}"], 16)
            if context is not None:
                run_slots(sp, step, 0, 0)

        @block.tensor
        def _(pe):
            def scores(i, u, g):
                if g == 0:
                    pe.wait_ge(q["q"], q.nth("q", i))
                    pe.wait_ge(q["k"], q.nth("k", i))
                    if past(i, 1):
                        pe.wait_ge(q["sfree"], q.nth("sfree", i, 1))
                last = pe.matmul(PS[:, g, 0:hpg * keys], qT[32 * g:32 * g + 32, u, :],
                                 kblk[32 * g:32 * g + 32, u, :], start=True, stop=True,
                                 tile_position=(32 * g, 0))
                if g == 3:
                    last.then_inc(q["scores"], 1)

            def turn_y(i, u):
                pe.wait_ge(q["y"], q.nth("y", i))
                if past(i, 4):
                    pe.wait_ge(q["OT"], q.nth("OT", i, 4))
                pe.transpose(yT_ps, y[:, u, :], m.IDENT[:, :]).then_inc(q["yTps"], 1)

            def project(i, u, h):
                pe.wait_ge(q["yT"], q.nth("yT", i))
                if inner is not None:
                    pe.wait_ge(q["xT"], q.nth("xT", i))
                kv = yT
                if context is not None:
                    pe.wait_ge(q[f"ctx{u}"], h * 16 + (16 + kv_base))
                    kv = cT
                pe.matmul(qT_ps, Wq[:, :], yT[:, u, :], start=True, stop=True)
                if past(i, 4):
                    pe.wait_ge(q["x"], q.nth("x", i, 4))
                pe.matmul(kT_ps, Wk[:, :], kv[:, u, :], start=True, stop=True)
                pe.matmul(v_ps, kv[:, u, :], Wv[:, :], start=True, stop=True).then_inc(q["proj"], 1)

            def turn_scores(i, u, g):
                if g == 0:
                    pe.wait_ge(q[less_max], q.nth(less_max, i))
                    if past(i, 1):
                        pe.wait_ge(q[f"P{groups - 1}"], q.nth(f"P{groups - 1}", i, 1))
                else:
                    pe.wait_ge(q[f"P{g - 1}"], q.nth(f"P{g - 1}", i))
                for j in range(4):
                    c = (4 * g + j) * keys
                    last = pe.transpose(PS[0:keys, 4, j * S:(j + 1) * S], T[:, u, c:c + keys],
                                        m.IDENT[:, :])
                last.then_inc(q[f"PT{g}"], 1)

            def weigh_values(i, u):
                pe.wait_ge(q["v"], q.nth("v", i))
                if past(i, 1):
                    pe.wait_ge(q["O"], q.nth("O", i, 1))
                for g in range(groups):
                    pe.wait_ge(q[f"P{g}"], q.nth(f"P{g}", i))
                    for j in range(4):
                        c = 4 * g + j
                        last = pe.matmul(PS[32 * j:32 * j + 32, 6, g * S:(g + 1) * S],
                                         vaug[:, u, c * 32:c * 32 + 32],
                                         Pr[:, u, c * S:(c + 1) * S], start=True, stop=True,
                                         tile_position=(0, 32 * j))
                last.then_inc(q["pv"], 1)

            def turn_back(i, u):
                pe.wait_ge(q["oT"], q.nth("oT", i))
                for g in range(groups):
                    last = pe.transpose(PS[:, 6, g * S:(g + 1) * S], oT[:, u, g * S:(g + 1) * S],
                                        m.IDENT[:, :])
                last.then_inc(q["back"], 1)

            def turn_out(i, u):
                pe.wait_ge(q["O"], q.nth("O", i))
                pe.wait_ge(q["q"], q.nth("q", i, -3))
                pe.transpose(OT_ps, O[:, u, :], m.IDENT[:, :]).then_inc(q["OTps"], 1)

            def project_out(i, u):
                pe.wait_ge(q["OT"], q.nth("OT", i))
                pe.wait_ge(q["k"], q.nth("k", i, -3))
                pe.wait_ge(q["v"], q.nth("v", i, -3))
                pe.matmul(out_ps, OT[:, u, :], Wo[:, :], start=True, stop=True).then_inc(q["out"], 1)

            def step(s, u, h):
                a = (u + 1) % 2
                for g in range(4):
                    if real(s):
                        scores(s, u, g)
                    if real(s - 1) and g < groups:
                        turn_scores(s - 1, a, g)
                    if real(s - 2) and g == 0:
                        turn_back(s - 2, u)
                    if real(s + 1) and g == 1:
                        turn_y(s + 1, a)
                if real(s + 1):
                    project(s + 1, a, h + u)
                if real(s - 2):
                    turn_out(s - 2, u)
                if real(s - 1):
                    weigh_values(s - 1, a)
                if real(s - 2):
                    project_out(s - 2, u)
            run_slots(pe, step, 1, 2)

        @block.scalar
        def _(act):
            act.activation(m.scratch[:, 0:1], m.scratch[:, 1:2], ACT.Exp)

            def copy_pv(i, u):
                act.wait_ge(q["pv"], q.nth("pv", i))
                if past(i, 2):
                    act.wait_ge(q["back"], q.nth("back", i, 2))
                act.activation(oT[:, u, :], PS[:, 6, 0:groups * S], ACT.Copy).then_inc(q["oT"], 1)

            def copy_yT(i, u):
                act.wait_ge(q["yTps"], q.nth("yTps", i))
                if inner is not None:
                    if past(i, 2):
                        act.wait_ge(q["xT"], q.nth("xT", i, 2))
                    act.activation(xw[:, u, :], yT_ps, ACT.Identity, bias=nb[:, :], scale=nw[:, :]) \
                        .then_inc(q["yT"], 1)
                else:
                    if past(i, 2):
                        act.wait_ge(q["proj"], q.nth("proj", i, 2))
                    act.activation(yT[:, u, :], yT_ps, ACT.Copy).then_inc(q["yT"], 1)

            def probabilities(i, u, g):
                act.wait_ge(q[f"PT{g}"], q.nth(f"PT{g}", i))
                if past(i, 2):
                    act.wait_ge(q["pv"], q.nth("pv", i, 2))
                part = Pr[:, u, g * BANK:(g + 1) * BANK]
                if topk:
                    act.activation(part, PS[0:keys, 4, :], ACT.Abs).then_inc(q[f"abs{g}"], 1)
                    act.wait_ge(q[f"abs{g}"], q.nth(f"abs{g}", i))
                    act.activation(part, part, ACT.Exp, scale=-1.0).then_inc(q[f"P{g}"], 1)
                else:
                    act.activation(part, PS[0:keys, 4, :], ACT.Exp).then_inc(q[f"P{g}"], 1)

            def copy_q(i, u):
                act.wait_ge(q["proj"], q.nth("proj", i))
                if past(i, 2):
                    act.wait_ge(q["scores"], q.nth("scores", i, 2))
                act.activation(qT[:, u, :], qT_ps, ACT.Identity, bias=bqs[:, :], scale=scale) \
                    .then_inc(q["q"], 1)

            def copy_OT(i, u):
                act.wait_ge(q["OTps"], q.nth("OTps", i))
                if past(i, 2):
                    act.wait_ge(q["out"], q.nth("out", i, 2))
                act.activation(OT[:, u, :], OT_ps, ACT.Copy).then_inc(q["OT"], 1)

            def step(s, u, h):
                a = (u + 1) % 2
                if real(s - 2):
                    copy_pv(s - 2, u)
                for g in range(4):
                    if real(s - 1) and g < groups:
                        probabilities(s - 1, a, g)
                    if real(s + 1) and g == 1:
                        copy_yT(s + 1, a)
                if real(s + 1):
                    copy_q(s + 1, a)
                if real(s - 2):
                    copy_OT(s - 2, u)
            run_slots(act, step, 1, 2)

        @block.gpsimd
        def _(pool):
            def add_bias(i, u):
                pool.wait_ge(q["y"], q.nth("y", i))
                xi = m.X[:, bass.ds(i, 1), :].rearrange("p a d -> p (a d)")
                if inner is None:
                    pool.tensor_tensor(xi, xi, bo[:, :], ALU.add).then_inc(q["bias"], 1)
                else:
                    pool.tensor_tensor(y0[:, u, :], y0[:, u, :], bo[:, :], ALU.add).then_inc(q["y0"], 1)
                    pool.wait_ge(q["y0"], q.nth("y0", i))
                    pool.tensor_tensor(xi, xi, y0[:, u, :], ALU.add).then_inc(q["bias"], 1)

            def step(s, u, h):
                a = (u + 1) % 2
                if inner is not None and real(s + 1):
                    pool.wait_ge(q["yT"], q.nth("yT", s + 1))
                    if past(s + 1, 2):
                        pool.wait_ge(q["proj"], q.nth("proj", s + 1, 2))
                    pool.tensor_tensor(yT[:, a, :], xw[:, a, :], m.WIDTH_FEATURES[:, :], ALU.mult) \
                        .then_inc(q["xT"], 1)
                if real(s):
                    add_bias(s, u)
                if inner is not None and real(s + 2):
                    pool.wait_ge(q["ivar"], q.nth("ivar", s + 2))
                    pool.tensor_tensor(in_rstd[:, u, :], in_var[:, u, :], m.MINUS_HALF[:, 0:1], ALU.pow) \
                        .then_inc(q["irstd"], 1)
            run_slots(pool, step, 2, 0)

        @block.vector
        def _(dve):
            def pass_wait():
                dve.sem_inc(q["passed"], 1)

            def normalise(i, u):
                xi = m.X[:, bass.ds(i, 1), :].rearrange("p a d -> p (a d)")
                mean, rstd = m.MEAN[:, bass.ds(i, 1)], m.RSTD[:, bass.ds(i, 1)]
                if inner is None:
                    if past(i, 2):
                        dve.wait_ge(q["yTps"], q.nth("yTps", i, 2))
                    dve.tensor_scalar(y[:, u, :], xi, mean, rstd, ALU.subtract, ALU.mult).then_inc(q["y"], 1)
                    return
                if past(i, 2):
                    dve.wait_ge(q["bias"], q.nth("bias", i, 2))
                dve.tensor_scalar(y0[:, u, :], xi, mean, rstd, ALU.subtract, ALU.mult).then_inc(q["yraw"], 1)
                dve.wait_ge(q["yraw"], q.nth("yraw", i))
                dve.bn_stats(in_stats[:, u, :], y0[:, u, :]).then_inc(q["istat"], 1)
                dve.wait_ge(q["istat"], q.nth("istat", i))
                pass_wait()
                dve.bn_aggr(in_mv[:, u, :], in_stats[:, u, :]).then_inc(q["imv"], 1)
                dve.wait_ge(q["imv"], q.nth("imv", i))
                dve.tensor_scalar(in_var[:, u, :], in_mv[:, u, 1:2], EPS, None, ALU.add).then_inc(q["ivar"], 1)

            def normalise_inner(i, u):
                dve.wait_ge(q["irstd"], q.nth("irstd", i))
                if past(i, 2):
                    dve.wait_ge(q["yTps"], q.nth("yTps", i, 2))
                dve.tensor_scalar(y[:, u, :], y0[:, u, :], in_mv[:, u, 0:1], in_rstd[:, u, :],
                                  ALU.subtract, ALU.mult).then_inc(q["y"], 1)

            def norm_heads(i, u):
                pv = PS[:, 6, 0:groups * S].rearrange("p (h e) -> p h e", e=32)
                dve.wait_ge(q["back"], q.nth("back", i))
                dve.reciprocal(rec[:, u, :], pv[:, :, dh:dh + 1].rearrange("p h e -> p (h e)")) \
                    .then_inc(q["rec"], 1)
                dve.wait_ge(q["rec"], q.nth("rec", i))
                if past(i, 2):
                    dve.wait_ge(q["OTps"], q.nth("OTps", i, 2))
                last = dve.tensor_tensor(O[:, u, :].rearrange("p (h e) -> p h e", e=dh), pv[:, :, 0:dh],
                                         bcast(rec[:, u, :], 2, dh), ALU.mult)
                if inner is not None:
                    last.then_inc(q["Oall"], 1)
                    dve.wait_ge(q["Oall"], q.nth("Oall", i))
                    last = dve.tensor_tensor(O[:, u, :], O[:, u, :], m.WIDTH_TOKENS[:, :], ALU.mult)
                last.then_inc(q["O"], 1)

            def subtract_max(i, u, h):
                raw = PS[:, 0:4, 0:hpg * keys].rearrange("p g (a c) -> p g a c", c=keys)
                t4 = T[:, u, :].rearrange("p (g a c) -> p g a c", a=hpg, c=keys)
                t3 = T[:, u, :].rearrange("p (h c) -> p h c", c=keys)
                m4 = mx[:, u, :].rearrange("p (g a) -> p g a", a=hpg)
                dve.wait_ge(q["scores"], q.nth("scores", i))
                for g in range(groups):
                    if past(i, 2):
                        dve.wait_ge(q[f"PT{g}"], q.nth(f"PT{g}", i, 2))
                if mask is not None:
                    dve.wait_ge(q[f"mask{u}"], h * 16 + (16 + mask_base))
                    for g in range(4):
                        last = dve.scalar_tensor_tensor(
                            out=t4[:, g, :, :], in0=bcast(mk[:, u, :], 1, hpg), scalar=-1.0e9,
                            in1=raw[:, g, :, :], op0=ALU.mult, op1=ALU.add)
                    last.then_inc(q["sfree"], 1)
                    dve.wait_ge(q["sfree"], q.nth("sfree", i))
                    dve.tensor_reduce(mx[:, u, :], t3, AX, ALU.max).then_inc(q["mx"], 1)
                    dve.wait_ge(q["mx"], q.nth("mx", i))
                    dve.tensor_tensor(t3, t3, bcast(mx[:, u, :], 2, keys), ALU.subtract).then_inc(q["T"], 1)
                    return
                dve.tensor_reduce(m4, raw, AX, ALU.max).then_inc(q["mx"], 1)
                dve.wait_ge(q["mx"], q.nth("mx", i))
                if not topk:
                    dve.tensor_tensor(t4, raw, bcast(m4, 3, keys), ALU.subtract) \
                        .then_inc(q["sfree"], 1)
                    return
                dve.tensor_tensor(t4, bcast(m4, 3, keys), raw, ALU.subtract).then_inc(q["sfree"], 1)
                rest = keys - topk - 8
                dve.wait_ge(q["sfree"], q.nth("sfree", i))
                pass_wait()
                for h in range(heads):
                    last = dve.max(r1[:, u, 8 * h:8 * h + 8], t3[:, h, :])
                last.then_inc(q["r1"], 1)
                dve.wait_ge(q["r1"], q.nth("r1", i))
                pass_wait()
                for h in range(heads):
                    last = dve.match_replace(t3[:, h, :], r1[:, u, 8 * h:8 * h + 8], t3[:, h, :], FAR)
                last.then_inc(q["t1"], 1)
                dve.wait_ge(q["t1"], q.nth("t1", i))
                pass_wait()
                for h in range(heads):
                    last = dve.max(r2[:, u, 8 * h:8 * h + 8], t3[:, h, :])
                last.then_inc(q["r2"], 1)
                dve.wait_ge(q["r2"], q.nth("r2", i))
                dve.memset(r2[:, u, :].rearrange("p (h e) -> p h e", e=8)[:, :, rest:8], FAR) \
                    .then_inc(q["r2cut"], 1)
                dve.wait_ge(q["r2cut"], q.nth("r2cut", i))
                pass_wait()
                for h in range(heads):
                    last = dve.match_replace(t3[:, h, :], r2[:, u, 8 * h:8 * h + 8], t3[:, h, :], FAR)
                last.then_inc(q["T"], 1)

            def spread_k(i, u):
                dve.wait_ge(q["proj"], q.nth("proj", i))
                if past(i, 2):
                    dve.wait_ge(q["scores"], q.nth("scores", i, 2))
                dve.scalar_tensor_tensor(
                    out=kblk[:, u, :].rearrange("p (a c) -> p a c", c=keys),
                    in0=bcast(kT_ps, 1, hpg), scalar=bk[:, :],
                    in1=bcast(m.HEAD[dh][:, :], 2, keys), op0=ALU.add, op1=ALU.mult).then_inc(q["k"], 1)

            def place_v(i, u):
                if past(i, 2):
                    dve.wait_ge(q["pv"], q.nth("pv", i, 2))
                dve.tensor_tensor(vaug[:, u, :].rearrange("p (h e) -> p h e", e=32)[:, :, 0:dh],
                                  v_ps.rearrange("p (h e) -> p h e", e=dh),
                                  bv[0:keys, :].rearrange("p (h e) -> p h e", e=dh), ALU.add) \
                    .then_inc(q["v"], 1)

            def residual(i, u):
                xi = m.X[:, bass.ds(i, 1), :].rearrange("p a d -> p (a d)")
                dve.wait_ge(q["out"], q.nth("out", i))
                dve.wait_ge(q["bias"], q.nth("bias", i))
                if inner is None:
                    dve.tensor_tensor(xi, out_ps, xi, ALU.add).then_inc(q["x"], 1)
                else:
                    dve.tensor_tensor(tmp[:, u, :], out_ps, m.WIDTH_TOKENS[:, :], ALU.mult) \
                        .then_inc(q["tmp"], 1)
                    dve.wait_ge(q["tmp"], q.nth("tmp", i))
                    dve.tensor_tensor(xi, tmp[:, u, :], xi, ALU.add).then_inc(q["x"], 1)
                dve.wait_ge(q["x"], q.nth("x", i))
                dve.bn_stats(m.STATS[:, bass.ds(i, 1), :].rearrange("p a d -> p (a d)"), xi)

            def step(s, u, h):
                a = (u + 1) % 2
                if real(s - 2):
                    norm_heads(s - 2, u)
                if inner is not None and real(s + 1):
                    normalise_inner(s + 1, a)
                if real(s):
                    subtract_max(s, u, h)
                if real(s + 1):
                    spread_k(s + 1, a)
                    place_v(s + 1, a)
                if real(s - 2):
                    residual(s - 2, u)
                if real(s + 2):
                    normalise(s + 2, u)
            run_slots(dve, step, 2, 2)

        used = ["y", "yTps", "yT", "proj", "q", "k", "v", "scores", "sfree", "mx", "pv", "oT", "back",
                "rec", "O", "OTps", "OT", "out", "bias", "x"]
        used += [f"{n}{g}" for n in ("PT", "P") for g in range(groups)]
        used += ["T"] if less_max == "T" else []
        used += ["xT"] if inner is not None else []
        for n in used:
            q.done[n] += B
        if context is not None:
            m.ctx_loads += 16 * (B // 2)
        if mask is not None:
            m.mask_loads += 16 * (B // 2)


def seq(tensor, i):
    return tensor[:, bass.ds(i, 1), :].rearrange("p a d -> p (a d)")


def layer0_cross(nc, m, t):
    n = "L0_xattn_"
    CH = 4
    NCH = -(-C // CH)
    CP = NCH * CH
    PARTS = [(0, 20), (20, 40), (60, C), (40, 60)]
    POOL_PART = 3
    with ExitStack() as ctx:
        def sb(name, shape, dt=F32):
            return ctx.enter_context(nc.sbuf_tensor(f"l0_{name}", shape, dt))

        Ws, W = sb("Ws", [D, D]), sb("W", [D, D])
        bvec, wvec = sb("b", [D, 1]), sb("w", [D, 1])
        wc = sb("wc", [D, 2])
        wc_wide = sb("wc_wide", [D, 2, S])
        wide = sb("wide", [D, 64])
        bc = sb("bc", [S, 2])
        ctxT = sb("ctxT", [D, B, C])
        y = sb("y", [S, 2, D])
        yT = sb("yT", [D, 2, S])
        feat = sb("feat", [D, 2, S])
        text = sb("text", [D, 2, C])
        H = sb("H", [D, 2, C * S])
        qm = sb("qm", [S, 2, C], I32)
        neg = sb("neg", [S, 2, CP])
        rhoT = sb("rhoT", [S, 2, BANK])
        rho = sb("rho", [S, 2, CP])
        nmx = sb("nmx", [S, 2, 1])
        e = sb("e", [S, 2, CP])
        esum = sb("esum", [S, 2, 1])
        rec = sb("rec", [S, 2, 1])
        junk = sb("junk", [S, 2, 2 * C])
        acc = sb("acc", [S, 2, 2])
        z = sb("z", [S, 2, 2])
        gate = sb("gate", [S, 2, 2])
        y2 = sb("y2", [S, 2, D])
        q = Signals(ctx, nc, "l0", [
            "prep", "y", "yTps", "yT", "proj", "projd", "text", "sum0", "sum1", "sum2", "sum3", "tanh0", "tanh1",
            "tanh2", "tanh3", "rho", "rhoT", "turned", "masked", "nmx", "e", "rec", "acc", "z", "gate", "y2",
            "part", "x", "cw", "neg", "qm0", "qm1", "passed"])
        PS = m.PS
        yT_ps, feat_ps, text_ps = PS[:, 0, 0:128], PS[:, 0, 128:256], PS[:, 0, 256:256 + C]
        cw_ps = PS[:, 3, 0:2 * C]

        with nc.Block() as block:
            loads = [(Ws[:, :], t[n + "Ws"]), (W[:, :], t[n + "W"]), (bvec[:, :], t[n + "b"].rearrange("a d -> d a")),
                     (wvec[:, :], t[n + "w"]), (wc[:, 0:1], t[n + "Wcw"].rearrange("a d -> d a")),
                     (wc[:, 1:2], t[n + "Wcb"].rearrange("a d -> d a")),
                     (bc[:, 0:1], t[n + "bcw"].partition_broadcast(S)),
                     (bc[:, 1:2], t[n + "bcb"].partition_broadcast(S)), (ctxT[:, :, :], t["ctxT"])]

            @block.sync
            def _(sp):
                for dst, src in loads:
                    sp.dma_start(dst, src).then_inc(m.s_weights, 16)
            m.weight_loads += 16 * len(loads)

            @block.vector
            def _(dve):
                dve.memset(wide[:, :], 0.0)
                dve.memset(neg[:, :, C:CP], FAR)
                dve.memset(e[:, :, :], 0.0).then_inc(q["prep"], 1)
                dve.wait_ge(m.s_weights, m.weight_loads)
                dve.wait_ge(q["prep"], 1)
                dve.tensor_copy(wide[:, 32:33], wvec[:, :])
                dve.tensor_copy(wc_wide[:, :, :], bcast(wc[:, :], 2, S))

        norm_stats(nc, m)
        block = ctx.enter_context(nc.Block())

        @block.sync
        def _(sp):
            def step(i, u, h):
                if past(i, 2):
                    sp.wait_ge(q["neg"], q.nth("neg", i, 2))
                sp.dma_start(qm[:, u, :], t["q_masks"][bass.ds(i, 1), :].rearrange("a c -> (a c)")
                             .partition_broadcast(S)).then_inc(q[f"qm{u}"], 16)
            run_slots(sp, step, 0, 0)

        @block.tensor
        def _(pe):
            def turn_y(i, u):
                pe.wait_ge(q["y"], q.nth("y", i))
                if past(i, 1):
                    pe.wait_ge(q["text"], q.nth("text", i, 1))
                pe.transpose(yT_ps, y[:, u, :], m.IDENT[:, :]).then_inc(q["yTps"], 1)

            def project(i, u):
                pe.wait_ge(q["yT"], q.nth("yT", i))
                pe.matmul(feat_ps, W[:, :], yT[:, u, :], start=True, stop=True)
                pe.matmul(text_ps, Ws[:, :], seq(ctxT, i), start=True, stop=True).then_inc(q["proj"], 1)
                if past(i, 2):
                    pe.wait_ge(q["sum2"], q.nth("sum2", i, 2))
                pe.matmul(PS[:, 1 + u, 0:S], W[:, :], yT[:, u, :], start=True, stop=True).then_inc(q["projd"], 1)

            def sum_rho(i, u, part):
                lo, hi = PARTS[part]
                pe.wait_ge(q[f"tanh{part}"], q.nth(f"tanh{part}", i))
                if part == 0:
                    if past(i, 2):
                        pe.wait_ge(q["rhoT"], q.nth("rhoT", i, 2))
                for c in range(lo // CH, -(-hi // CH)):
                    j, r = c % 4, c // 4
                    cols = (min(C, CH * (c + 1)) - CH * c) * S
                    last = pe.matmul(PS[32 * j:32 * j + 32, 4 + u, 0:cols], wide[:, 32 - r:64 - r],
                                     H[:, u, CH * c * S:CH * c * S + cols], start=(r == 0),
                                     stop=(part == POOL_PART and c >= hi // CH - 4), tile_position=(0, 32 * j),
                                     skip_group_check=True)
                if part == POOL_PART:
                    last.then_inc(q["rho"], 1)

            def turn_rho(i, u):
                pe.wait_ge(q["rhoT"], q.nth("rhoT", i))
                if past(i, 1):
                    pe.wait_ge(q["masked"], q.nth("masked", i, 1))
                for k in range(CH):
                    last = pe.transpose(PS[:, 6, k * S:(k + 1) * S], rhoT[:, u, k * S:(k + 1) * S], m.IDENT[:, :])
                last.then_inc(q["turned"], 1)
                if past(i, 1):
                    pe.wait_ge(q["z"], q.nth("z", i, 1))
                for k in range(2):
                    last = pe.matmul(cw_ps[:, k * C:(k + 1) * C], wc_wide[:, k, :], seq(ctxT, i),
                                     start=True, stop=True)
                last.then_inc(q["cw"], 1)

            def step(s, u, h):
                a = (u + 1) % 2
                if real(s - 1):
                    turn_rho(s - 1, a)
                if real(s):
                    sum_rho(s, u, 0)
                if real(s + 2):
                    turn_y(s + 2, u)
                if real(s):
                    sum_rho(s, u, 1)
                if real(s + 2):
                    project(s + 2, u)
                if real(s):
                    sum_rho(s, u, 2)
                    sum_rho(s, u, 3)
            run_slots(pe, step, 2, 1)

        @block.scalar
        def _(act):
            act.activation(m.scratch[:, 0:1], m.scratch[:, 1:2], ACT.Exp)

            def tanh(i, u, part):
                lo, hi = PARTS[part]
                act.wait_ge(q[f"sum{part}"], q.nth(f"sum{part}", i))
                cells = H[:, u, lo * S:hi * S]
                act.activation(cells, cells, ACT.Tanh).then_inc(q[f"tanh{part}"], 1)

            def step(s, u, h):
                a = (u + 1) % 2
                if real(s - 1):
                    act.wait_ge(q["rho"], q.nth("rho", s - 1))
                    if past(s - 1, 2):
                        act.wait_ge(q["turned"], q.nth("turned", s - 1, 2))
                    act.activation(rhoT[:, a, :], PS[:, 4 + a, :], ACT.Copy).then_inc(q["rhoT"], 1)
                if real(s):
                    tanh(s, u, 0)
                if real(s + 2):
                    act.wait_ge(q["yTps"], q.nth("yTps", s + 2))
                    if past(s + 2, 2):
                        act.wait_ge(q["projd"], q.nth("projd", s + 2, 2))
                    act.activation(yT[:, u, :], yT_ps, ACT.Copy).then_inc(q["yT"], 1)
                if real(s - 1):
                    act.wait_ge(q["nmx"], q.nth("nmx", s - 1))
                    if past(s - 1, 2):
                        act.wait_ge(q["acc"], q.nth("acc", s - 1, 2))
                    act.activation(e[:, a, :], rho[:, a, :], ACT.Exp, bias=nmx[:, a, :],
                                   accum_out=esum[:, a, :]).then_inc(q["e"], 1)
                if real(s):
                    tanh(s, u, 1)
                if real(s + 2):
                    act.wait_ge(q["proj"], q.nth("proj", s + 2))
                    if past(s + 2, 2):
                        act.wait_ge(q[f"sum{POOL_PART}"], q.nth(f"sum{POOL_PART}", s + 2, 2))
                    if past(s + 2, 2):
                        act.wait_ge(q["sum2"], q.nth("sum2", s + 2, 2))
                    act.activation(feat[:, u, :], feat_ps, ACT.Copy)
                    act.activation(text[:, u, :], text_ps, ACT.Identity, bias=bvec[:, :]).then_inc(q["text"], 1)
                if real(s):
                    tanh(s, u, 2)
                if real(s - 1):
                    act.wait_ge(q["z"], q.nth("z", s - 1))
                    if past(s - 1, 2):
                        act.wait_ge(q["x"], q.nth("x", s - 1, 2))
                    act.activation(gate[:, a, :], z[:, a, :], ACT.Tanh).then_inc(q["gate"], 1)
                if real(s):
                    tanh(s, u, 3)
            run_slots(act, step, 2, 1)

        @block.gpsimd
        def _(pool):
            def step(s, u, h):
                a = (u + 1) % 2
                if real(s + 1):
                    lo, hi = PARTS[POOL_PART]
                    pool.wait_ge(q["text"], q.nth("text", s + 1))
                    if past(s + 1, 2):
                        pool.wait_ge(q["rho"], q.nth("rho", s + 1, 2))
                    pool.tensor_tensor(H[:, a, lo * S:hi * S].rearrange("p (t f) -> p t f", f=S),
                                       bcast(feat[:, a, :], 1, hi - lo), bcast(text[:, a, lo:hi], 2, S), ALU.add) \
                        .then_inc(q[f"sum{POOL_PART}"], 1)
                if real(s):
                    pool.wait_ge(q[f"qm{u}"], h * 16 + 16)
                    if past(s, 2):
                        pool.wait_ge(q["masked"], q.nth("masked", s, 2))
                    pool.sem_inc(q["passed"], 1)
                    pool.tensor_scalar(neg[:, u, 0:C], qm[:, u, :], -1.0, 1.0e30, ALU.add, ALU.mult) \
                        .then_inc(q["neg"], 1)
            run_slots(pool, step, 1, 0)

        @block.vector
        def _(dve):
            def add_part(i, u, part):
                lo, hi = PARTS[part]
                if part == 0:
                    dve.wait_ge(q["text"], q.nth("text", i))
                    dve.wait_ge(q["projd"], q.nth("projd", i))
                    if past(i, 2):
                        dve.wait_ge(q["rho"], q.nth("rho", i, 2))
                dve.tensor_tensor(H[:, u, lo * S:hi * S].rearrange("p (t f) -> p t f", f=S),
                                  bcast(PS[:, 1 + u, 0:S], 1, hi - lo), bcast(text[:, u, lo:hi], 2, S), ALU.add) \
                    .then_inc(q[f"sum{part}"], 1)

            def mask_rho(i, u):
                dve.wait_ge(q["turned"], q.nth("turned", i))
                dve.wait_ge(q["neg"], q.nth("neg", i))
                if past(i, 2):
                    dve.wait_ge(q["e"], q.nth("e", i, 2))
                turned = PS[:, 6, :].rearrange("p (k j r) -> p r j k", k=4, j=4)[:, 0:NCH // 4, :, :]
                dve.tensor_tensor(rho[:, u, :].rearrange("p (r j k) -> p r j k", j=4, k=4), turned,
                                  neg[:, u, :].rearrange("p (r j k) -> p r j k", j=4, k=4), ALU.add) \
                    .then_inc(q["masked"], 1)
                dve.wait_ge(q["masked"], q.nth("masked", i))
                dve.tensor_reduce(nmx[:, u, :], rho[:, u, :], AX, ALU.max, negate=True).then_inc(q["nmx"], 1)

            def attend(i, u):
                dve.wait_ge(q["e"], q.nth("e", i))
                dve.wait_ge(q["cw"], q.nth("cw", i))
                dve.reciprocal(rec[:, u, :], esum[:, u, :]).then_inc(q["rec"], 1)
                for k in range(2):
                    last = dve.scalar_tensor_tensor(
                        out=junk[:, u, k * C:(k + 1) * C], in0=e[:, u, 0:C], scalar=1.0,
                        in1=cw_ps[:, k * C:(k + 1) * C], op0=ALU.mult, op1=ALU.mult,
                        accum_out=acc[:, u, k:k + 1])
                last.then_inc(q["acc"], 1)
                dve.wait_ge(q["acc"], q.nth("acc", i))
                dve.wait_ge(q["rec"], q.nth("rec", i))
                if past(i, 2):
                    dve.wait_ge(q["gate"], q.nth("gate", i, 2))
                dve.scalar_tensor_tensor(out=z[:, u, :], in0=acc[:, u, :], scalar=rec[:, u, :], in1=bc[:, :],
                                         op0=ALU.mult, op1=ALU.add).then_inc(q["z"], 1)

            def update(i, u):
                dve.tensor_scalar(y2[:, u, :], seq(m.X, i), m.MEAN[:, bass.ds(i, 1)], m.RSTD[:, bass.ds(i, 1)],
                                  ALU.subtract, ALU.mult).then_inc(q["y2"], 1)
                dve.wait_ge(q["y2"], q.nth("y2", i))
                dve.wait_ge(q["gate"], q.nth("gate", i))
                dve.scalar_tensor_tensor(out=y2[:, u, :], in0=y2[:, u, :], scalar=gate[:, u, 0:1], in1=seq(m.X, i),
                                         op0=ALU.mult, op1=ALU.add).then_inc(q["part"], 1)
                dve.wait_ge(q["part"], q.nth("part", i))
                dve.tensor_scalar(seq(m.X, i), y2[:, u, :], gate[:, u, 1:2], None, ALU.add).then_inc(q["x"], 1)
                dve.wait_ge(q["x"], q.nth("x", i))
                dve.bn_stats(seq(m.STATS, i), seq(m.X, i))

            def step(s, u, h):
                a = (u + 1) % 2
                if real(s + 1):
                    add_part(s + 1, a, 0)
                if real(s - 1):
                    mask_rho(s - 1, a)
                if real(s + 1):
                    add_part(s + 1, a, 1)
                if real(s - 1):
                    attend(s - 1, a)
                if real(s + 1):
                    add_part(s + 1, a, 2)
                if real(s - 1):
                    update(s - 1, a)
                if real(s + 3):
                    if past(s + 3, 2):
                        dve.wait_ge(q["yTps"], q.nth("yTps", s + 3, 2))
                    dve.tensor_scalar(y[:, a, :], seq(m.X, s + 3), m.MEAN[:, bass.ds(s + 3, 1)],
                                      m.RSTD[:, bass.ds(s + 3, 1)], ALU.subtract, ALU.mult).then_inc(q["y"], 1)
            run_slots(dve, step, 3, 1)


G = 4
NG = B // G
N = G * S
ROWS = 72
PAD = 8


def group(tensor, i):
    return tensor[:, bass.ds(i * G, G), :]


def normalise_group(dve, m, q, y, i, u):
    if past(i, 2):
        dve.wait_ge(q["yTps"], q.nth("yTps", i, 2))
    x = group(m.X, i)
    mean = bcast(m.MEAN[:, bass.ds(i * G, G)], 2, D)
    rstd = bcast(m.RSTD[:, bass.ds(i * G, G)], 2, D)
    y3 = y[:, u, :].rearrange("p (g d) -> p g d", d=D)
    dve.tensor_tensor(y3, x, mean, ALU.subtract).then_inc(q["centred"], 1)
    dve.wait_ge(q["centred"], q.nth("centred", i))
    dve.tensor_tensor(y3, y3, rstd, ALU.mult).then_inc(q["y"], 1)


def group_statistics(dve, m, i):
    for g in range(G):
        dve.bn_stats(seq(m.STATS, i * G + g), seq(m.X, i * G + g))


def route_logits(dve, q, r, logits, E, i, u):
    dve.wait_ge(q["logits"], q.nth("logits", i))
    dve.tensor_reduce(r.mx[:, u, :], logits, AX, ALU.max).then_inc(q["lmax"], 1)
    dve.wait_ge(q["lmax"], q.nth("lmax", i))
    if past(i, 2):
        dve.wait_ge(q["exp"], q.nth("exp", i, 2))
    dve.tensor_tensor(r.lt[:, u, :].rearrange("p (g e) -> p g e", e=E), logits, bcast(r.mx[:, u, :], 2, E),
                      ALU.subtract).then_inc(q["lt"], 1)


def route_select(dve, q, r, E, K, normalise, with_mask, i, u):
    ex = r.ex[:, u, :].rearrange("p (g e) -> p g e", e=E + PAD)
    out = r.out[:, u, :].rearrange("p (g e) -> p g e", e=E + PAD)
    parts = r.parts[:, u, :].rearrange("p (g r) -> p g r", r=ROWS)
    sc = r.sc[:, u, :].rearrange("p (g e) -> p g e", e=E)
    rest = r.rest[:, u, :].rearrange("p (g e) -> p g e", e=E)
    dve.wait_ge(q["exp"], q.nth("exp", i))
    if not normalise:
        dve.tensor_reduce(r.sum[:, u, :], ex[:, :, 0:E], AX, ALU.add).then_inc(q["lsum"], 1)
        dve.wait_ge(q["lsum"], q.nth("lsum", i))
        dve.reciprocal(r.rec[:, u, :], r.sum[:, u, :]).then_inc(q["lrec"], 1)
        dve.wait_ge(q["lrec"], q.nth("lrec", i))
        dve.tensor_tensor(ex[:, :, 0:E], ex[:, :, 0:E], bcast(r.rec[:, u, :], 2, E), ALU.mult) \
            .then_inc(q["prob"], 1)
        dve.wait_ge(q["prob"], q.nth("prob", i))
    dve.sem_inc(q["passed"], 1)
    for g in range(G):
        last = dve.max(r.top[:, u, 8 * g:8 * g + 8], ex[:, g, 0:E])
    last.then_inc(q["top"], 1)
    dve.wait_ge(q["top"], q.nth("top", i))
    dve.memset(r.top[:, u, :].rearrange("p (g e) -> p g e", e=8)[:, :, K:8], -1.0).then_inc(q["topk"], 1)
    dve.wait_ge(q["topk"], q.nth("topk", i))
    dve.sem_inc(q["passed"], 1)
    for g in range(G):
        last = dve.match_replace(out[:, g, :], r.top[:, u, 8 * g:8 * g + 8], ex[:, g, :], -2.0)
    last.then_inc(q["marked"], 1)
    dve.wait_ge(q["marked"], q.nth("marked", i))
    if past(i, 2):
        dve.wait_ge(q["partsT"], q.nth("partsT", i, 2))
    if with_mask:
        for k in range(3):
            dve.tensor_scalar(parts[:, :, 3 * E + k * E:3 * E + k * E + E], out[:, :, 0:E], -1.5, None, ALU.is_lt)
    dve.scalar_tensor_tensor(out=sc, in0=out[:, :, 0:E], scalar=-1.5, in1=ex[:, :, 0:E], op0=ALU.is_lt,
                             op1=ALU.mult).then_inc(q["chosen"], 1)
    dve.wait_ge(q["chosen"], q.nth("chosen", i))
    if normalise:
        dve.tensor_reduce(r.sum[:, u, :], sc, AX, ALU.add).then_inc(q["lsum"], 1)
        dve.wait_ge(q["lsum"], q.nth("lsum", i))
        dve.reciprocal(r.rec[:, u, :], r.sum[:, u, :]).then_inc(q["lrec"], 1)
        dve.wait_ge(q["lrec"], q.nth("lrec", i))
        dve.tensor_tensor(sc, sc, bcast(r.rec[:, u, :], 2, E), ALU.mult).then_inc(q["prob"], 1)
        dve.wait_ge(q["prob"], q.nth("prob", i))
    dve.tensor_copy(parts[:, :, 0:E], sc).then_inc(q["hi"], 1)
    dve.wait_ge(q["hi"], q.nth("hi", i))
    dve.tensor_tensor(rest, sc, parts[:, :, 0:E], ALU.subtract).then_inc(q["rest1"], 1)
    dve.wait_ge(q["rest1"], q.nth("rest1", i))
    dve.tensor_copy(parts[:, :, E:2 * E], rest).then_inc(q["mid"], 1)
    dve.wait_ge(q["mid"], q.nth("mid", i))
    dve.tensor_tensor(rest, rest, parts[:, :, E:2 * E], ALU.subtract).then_inc(q["rest2"], 1)
    dve.wait_ge(q["rest2"], q.nth("rest2", i))
    dve.tensor_copy(parts[:, :, 2 * E:3 * E], rest).then_inc(q["parts"], 1)


ROUTE_SIGNALS = ["centred", "y", "yTps", "yT", "logits", "lmax", "lt", "exp", "lsum", "lrec", "prob", "top", "topk",
                 "marked", "chosen", "hi", "rest1", "mid", "rest2", "parts", "partsT", "partsTs", "passed",
                 "total", "totalT", "x"]


def route_buffers(sb, E):
    r = Named()
    r.mx, r.sum, r.rec = (sb(f"r_{name}", [S, 2, G]) for name in ("mx", "sum", "rec"))
    r.lt, r.sc, r.rest = (sb(f"r_{name}", [S, 2, G * E]) for name in ("lt", "sc", "rest"))
    r.ex, r.out = (sb(f"r_{name}", [S, 2, G * (E + PAD)]) for name in ("ex", "out"))
    r.top = sb("r_top", [S, 2, G * 8])
    r.parts = sb("r_parts", [S, 2, G * ROWS], BF16)
    r.partsT = sb("r_partsT", [ROWS, 2, N], BF16)
    return r


def front_tensor(pe, m, q, y, yT, gate, r, E):
    PS = m.PS

    def turn_y(i, u):
        pe.wait_ge(q["y"], q.nth("y", i))
        if past(i, 1):
            pe.wait_ge(q["partsTs"], q.nth("partsTs", i, 1))
        for g in range(G):
            last = pe.transpose(PS[:, 6, g * S:(g + 1) * S], y[:, u, g * D:(g + 1) * D], m.IDENT[:, :])
        last.then_inc(q["yTps"], 1)

    def logits(i, u):
        pe.wait_ge(q["yT"], q.nth("yT", i))
        if past(i, 2):
            pe.wait_ge(q["x"], q.nth("x", i, 2))
        for g in range(G):
            last = pe.matmul(PS[:, 7, g * E:(g + 1) * E], yT[:, u, g * S:(g + 1) * S], gate[:, :],
                             start=True, stop=True)
        last.then_inc(q["logits"], 1)

    def turn_parts(i, u):
        pe.wait_ge(q["parts"], q.nth("parts", i))
        for g in range(G):
            last = pe.transpose(PS[0:ROWS, 6, 0:N // 2].bitcast(BF16)[:, g * S:(g + 1) * S],
                                r.parts[:, u, g * ROWS:(g + 1) * ROWS], m.IDENT_BF[:, :])
        last.then_inc(q["partsT"], 1)

    return turn_y, logits, turn_parts


def front_scalar(act, m, q, yT, r, E, reader):
    PS = m.PS

    def copy_y(i, u):
        act.wait_ge(q["yTps"], q.nth("yTps", i))
        if past_part(i, reader[1] - 1, reader[1], 2 * reader[1]):
            act.wait_ge(q[reader[0]], nth_part(i, reader[1] - 1, reader[1], 2 * reader[1]))
        act.activation(yT[:, u, :], PS[:, 6, :], ACT.Copy).then_inc(q["yT"], 1)

    def exponential(i, u):
        act.wait_ge(q["lt"], q.nth("lt", i))
        if past(i, 2):
            act.wait_ge(q["chosen"], q.nth("chosen", i, 2))
        act.activation(r.ex[:, u, :].rearrange("p (g e) -> p g e", e=E + PAD)[:, :, 0:E],
                       r.lt[:, u, :].rearrange("p (g e) -> p g e", e=E), ACT.Exp).then_inc(q["exp"], 1)

    def copy_parts(i, u):
        act.wait_ge(q["partsT"], q.nth("partsT", i))
        act.activation(r.partsT[:, u, :], PS[0:ROWS, 6, 0:N // 2].bitcast(BF16), ACT.Copy).then_inc(q["partsTs"], 1)

    return copy_y, exponential, copy_parts


def layer0_experts(nc, m, t):
    n = "L0_ffn_"
    E, K, NP = 16, 4, 8
    with ExitStack() as ctx:
        def sb(name, shape, dt=F32):
            return ctx.enter_context(nc.sbuf_tensor(f"e0_{name}", shape, dt))

        w1, w3, w2 = sb("w1", [D, NP * 128]), sb("w3", [D, NP * 128]), sb("w2", [128, NP, D])
        gate = sb("gate", [D, E])
        pick_f, pick = sb("pick_f", [ROWS, NP * 128]), sb("pick", [ROWS, NP * 128], BF16)
        y, yT = sb("y", [S, 2, N]), sb("yT", [D, 2, N])
        r = route_buffers(sb, E)
        act_g = sb("act_g", [128, 2, N])
        gu = sb("gu", [128, 2, N])
        hid = sb("hid", [128, 2, N])
        total = sb("total", [D, 2, N])
        q = Signals(ctx, nc, "e0", ROUTE_SIGNALS + ["prep", "up", "silu", "gu", "hid", "down"])
        PS = m.PS

        with nc.Block() as block:
            loads = [(w1[:, :], t[n + "w1"]), (w3[:, :], t[n + "w3"]), (w2[:, :, :], t[n + "w2"]),
                     (gate[:, :], t[n + "gate_w"]),
                     (pick_f[:, :], t["c_pick_pairs"].rearrange("r p c -> r (p c)"))]

            @block.sync
            def _(sp):
                for dst, src in loads:
                    sp.dma_start(dst, src).then_inc(m.s_weights, 16)
            m.weight_loads += 16 * len(loads)

            @block.vector
            def _(dve):
                dve.memset(r.ex[:, :, :], -1.0)
                dve.memset(r.parts[:, :, :], 0.0)
                dve.wait_ge(m.s_weights, m.weight_loads)
                dve.tensor_copy(pick[:, :], pick_f[:, :])

        norm_stats(nc, m)
        block = ctx.enter_context(nc.Block())


        @block.tensor
        def _(pe):
            turn_y, logits, turn_parts = front_tensor(pe, m, q, y, yT, gate, r, E)

            def up(i, u, p):
                v = p % 2
                if p == 0:
                    pe.wait_ge(q["yT"], q.nth("yT", i))
                if past_part(i, p, NP, 2):
                    pe.wait_ge(q["silu"], nth_part(i, p, NP, 2))
                pe.matmul(PS[:, v, :], w1[:, p * 128:(p + 1) * 128], yT[:, u, :], start=True, stop=True)
                if past_part(i, p, NP, 2):
                    pe.wait_ge(q["gu"], nth_part(i, p, NP, 2))
                pe.matmul(PS[:, 2 + v, :], w3[:, p * 128:(p + 1) * 128], yT[:, u, :], start=True, stop=True)
                if p == 0:
                    pe.wait_ge(q["partsTs"], q.nth("partsTs", i))
                if past_part(i, p, NP, 1):
                    pe.wait_ge(q["hid"], nth_part(i, p, NP, 1))
                pe.matmul(PS[:, 4, :], pick[:, p * 128:(p + 1) * 128], r.partsT[:, u, :],
                          start=True, stop=True).then_inc(q["up"], 1)

            def down(i, p):
                pe.wait_ge(q["hid"], nth_part(i, p, NP))
                if p == 0:
                    if past(i, 1):
                        pe.wait_ge(q["total"], q.nth("total", i, 1))
                last = pe.matmul(PS[:, 5, :], w2[:, p, :], hid[:, p % 2, :], start=(p == 0), stop=(p == NP - 1))
                last.then_inc(q["down"], 1)

            def turn_total(i, u):
                pe.wait_ge(q["total"], q.nth("total", i))
                pe.wait_ge(q["lt"], q.nth("lt", i, -1, NG))
                for g in range(G):
                    last = pe.transpose(PS[:, 7, g * D:(g + 1) * D], total[:, u, g * S:(g + 1) * S], m.IDENT[:, :])
                last.then_inc(q["totalT"], 1)

            def step(s, u, h):
                a = (u + 1) % 2
                for p in range(NP):
                    if real(s, NG):
                        up(s, u, p)
                    if p == 0 and real(s - 1, NG):
                        down(s - 1, NP - 1)
                    if p > 0 and real(s, NG):
                        down(s, p - 1)
                    if p == 1 and real(s + 1, NG):
                        turn_y(s + 1, a)
                    if p == 2 and real(s - 1, NG):
                        turn_total(s - 1, a)
                    if p == 4 and real(s + 1, NG):
                        logits(s + 1, a)
                    if p == 7 and real(s + 1, NG):
                        turn_parts(s + 1, a)
            run_slots(pe, step, 1, 1, NG)

        @block.scalar
        def _(act):
            copy_y, exponential, copy_parts = front_scalar(act, m, q, yT, r, E, ("up", NP))

            def step(s, u, h):
                a = (u + 1) % 2
                for p in range(NP):
                    if real(s, NG):
                        act.wait_ge(q["up"], nth_part(s, p, NP))
                        if past_part(s, p, NP, 2):
                            act.wait_ge(q["gu"], nth_part(s, p, NP, 2))
                        act.activation(act_g[:, p % 2, :], PS[:, p % 2, :], ACT.Silu).then_inc(q["silu"], 1)
                    if p == 0 and real(s - 1, NG):
                        act.wait_ge(q["down"], nth_part(s - 1, NP - 1, NP))
                        if past(s - 1, 2):
                            act.wait_ge(q["totalT"], q.nth("totalT", s - 1, 2))
                        act.activation(total[:, a, :], PS[:, 5, :], ACT.Copy).then_inc(q["total"], 1)
                    if p == 1 and real(s + 1, NG):
                        copy_y(s + 1, a)
                    if p == 5 and real(s + 1, NG):
                        exponential(s + 1, a)
                if real(s + 1, NG):
                    copy_parts(s + 1, a)
            run_slots(act, step, 1, 1, NG)

        @block.vector
        def _(dve):
            def step(s, u, h):
                a = (u + 1) % 2
                for p in range(NP):
                    v = p % 2
                    if real(s, NG):
                        dve.wait_ge(q["silu"], nth_part(s, p, NP))
                        dve.tensor_tensor(gu[:, v, :], act_g[:, v, :], PS[:, 2 + v, :], ALU.mult).then_inc(q["gu"], 1)
                        dve.wait_ge(q["gu"], nth_part(s, p, NP))
                        if past_part(s, p, NP, 2):
                            dve.wait_ge(q["down"], nth_part(s, p, NP, 2))
                        dve.tensor_tensor(hid[:, v, :], gu[:, v, :], PS[:, 4, :], ALU.mult).then_inc(q["hid"], 1)
                    if p == 3 and real(s - 1, NG):
                        dve.wait_ge(q["totalT"], q.nth("totalT", s - 1))
                        dve.tensor_tensor(group(m.X, s - 1), group(m.X, s - 1),
                                          PS[:, 7, :].rearrange("p (g d) -> p g d", d=D), ALU.add).then_inc(q["x"], 1)
                        dve.wait_ge(q["x"], q.nth("x", s - 1))
                        group_statistics(dve, m, s - 1)
                    if p == 4 and real(s + 1, NG):
                        route_logits(dve, q, r, PS[:, 7, 0:G * E].rearrange("p (g e) -> p g e", e=E), E, s + 1, a)
                    if p == 5 and real(s + 1, NG):
                        route_select(dve, q, r, E, K, True, False, s + 1, a)
                if real(s + 2, NG):
                    normalise_group(dve, m, q, y, s + 2, u)
            run_slots(dve, step, 2, 1, NG)


def layer1_experts(nc, m, t):
    n = "L1_ffn_"
    E, K = 8, 2
    NE = E + 2
    with ExitStack() as ctx:
        def sb(name, shape, dt=F32):
            return ctx.enter_context(nc.sbuf_tensor(f"e1_{name}", shape, dt))

        w1, w2, w3 = (sb(c, [D, E, 128]) for c in ("w1", "w2", "w3"))
        sw1, sw2, sw3 = sb("sw1", [D, 256]), sb("sw2", [D, 256]), sb("sw3", [128, 2, D])
        b1, b2 = sb("b1", [128, E]), sb("b2", [D, E])
        gate = sb("gate", [D, E])
        pick_f, pick = sb("pick_f", [ROWS, E * 128]), sb("pick", [ROWS, E * 128], BF16)
        bias_rows = sb("bias_rows", [ROWS, D])
        bias_rest = sb("bias_rest", [ROWS, D])
        bias_parts = sb("bias_parts", [ROWS, 3, D], BF16)
        pick_b = sb("pick_b", [ROWS, 3, E])
        b3 = sb("b3", [ROWS, E * 128], BF16)
        y, yT = sb("y", [S, 2, N]), sb("yT", [D, 2, N])
        r = route_buffers(sb, E)
        xs = sb("xs", [D, 2, N])
        hid = sb("hid", [128, 2, N])
        up = sb("up", [128, 2, N])
        prod = sb("prod", [128, 2, N])
        acc = sb("acc", [D, 2, N])
        total = sb("total", [D, 2, N])
        q = Signals(ctx, nc, "e1", ROUTE_SIGNALS + [
            "bzero", "bhi", "brest", "bmid", "brest2", "blo", "bsum", "wide", "xs", "gate", "hid", "value", "up",
            "upc", "down", "prod", "acc", "held"])
        PS = m.PS

        with nc.Block() as block:
            loads = [(w1[:, :, :], t[n + "w1"]), (w2[:, :, :], t[n + "w2"]), (w3[:, :, :], t[n + "w3"]),
                     (sw1[:, :], t[n + "sw1"]), (sw2[:, :], t[n + "sw2"]), (sw3[:, :, :], t[n + "sw3"]),
                     (b1[:, :], t[n + "b1"]), (b2[:, :], t[n + "b2"]), (gate[:, :], t[n + "gate_w"]),
                     (pick_f[:, :], t["c_pick_weight"].rearrange("r p c -> r (p c)")),
                     (pick_b[:, :, :], t["c_pick_bias"])]
            loads += [(bias_rows[8 * k:8 * k + 8, :], t[n + "b3"]) for k in range(6)]

            @block.sync
            def _(sp):
                sp.wait_ge(q["bzero"], 1)
                for dst, src in loads:
                    sp.dma_start(dst, src).then_inc(m.s_weights, 16)
            m.weight_loads += 16 * len(loads)

            @block.vector
            def _(dve):
                dve.memset(r.ex[:, :, :], -1.0)
                dve.memset(r.parts[:, :, :], 0.0)
                dve.memset(bias_rows[:, :], 0.0).then_inc(q["bzero"], 1)
                dve.wait_ge(m.s_weights, m.weight_loads)
                dve.tensor_copy(pick[:, :], pick_f[:, :])
                dve.tensor_copy(bias_parts[:, 0, :], bias_rows[:, :]).then_inc(q["bhi"], 1)
                dve.wait_ge(q["bhi"], 1)
                dve.tensor_tensor(bias_rest[:, :], bias_rows[:, :], bias_parts[:, 0, :], ALU.subtract) \
                    .then_inc(q["brest"], 1)
                dve.wait_ge(q["brest"], 1)
                dve.tensor_copy(bias_parts[:, 1, :], bias_rest[:, :]).then_inc(q["bmid"], 1)
                dve.wait_ge(q["bmid"], 1)
                dve.tensor_tensor(bias_rows[:, :], bias_rest[:, :], bias_parts[:, 1, :], ALU.subtract) \
                    .then_inc(q["brest2"], 1)
                dve.wait_ge(q["brest2"], 1)
                dve.tensor_copy(bias_parts[:, 2, :], bias_rows[:, :]).then_inc(q["blo"], 1)
                dve.wait_ge(q["blo"], 1)
                for k in range(3):
                    if k:
                        dve.wait_ge(q["bsum"], E * k)
                    for e in range(E):
                        row_part = b3[:, e * 128:(e + 1) * 128]
                        if k == 0:
                            last = dve.tensor_scalar(row_part, bias_parts[:, k, :], pick_b[:, k, e:e + 1], None,
                                                     ALU.mult)
                        else:
                            last = dve.scalar_tensor_tensor(out=row_part, in0=bias_parts[:, k, :],
                                                            scalar=pick_b[:, k, e:e + 1], in1=row_part,
                                                            op0=ALU.mult, op1=ALU.add)
                        last.then_inc(q["bsum"], 1)

        norm_stats(nc, m)
        block = ctx.enter_context(nc.Block())


        @block.tensor
        def _(pe):
            turn_y, logits, turn_parts = front_tensor(pe, m, q, y, yT, gate, r, E)

            def widen(i, u, e):
                if e == 0:
                    pe.wait_ge(q["partsTs"], q.nth("partsTs", i))
                if past_part(i, e, E, 1):
                    pe.wait_ge(q["xs"], nth_part(i, e, E, 1))
                pe.matmul(PS[:, 2, :], pick[:, e * 128:(e + 1) * 128], r.partsT[:, u, :],
                          start=True, stop=True).then_inc(q["wide"], 1)

            def gate_up(i, u, e):
                if past_part(i, e, NE, 1):
                    pe.wait_ge(q["hid"], nth_part(i, e, NE, 1))
                if e < E:
                    pe.wait_ge(q["xs"], nth_part(i, e, E))
                    pe.matmul(PS[:, 0, :], w1[:, e, :], xs[:, e % 2, :], start=True, stop=True).then_inc(q["gate"], 1)
                    if past_part(i, e, E, 1):
                        pe.wait_ge(q["upc"], nth_part(i, e, E, 1))
                    pe.matmul(PS[:, 1, :], b3[:, e * 128:(e + 1) * 128], r.partsT[:, u, :], start=True, stop=False)
                    pe.matmul(PS[:, 1, :], w3[:, e, :], xs[:, e % 2, :], start=False, stop=True).then_inc(q["up"], 1)
                else:
                    c = slice((e - E) * 128, (e - E + 1) * 128)
                    pe.matmul(PS[:, 0, :], sw1[:, c], yT[:, u, :], start=True, stop=True).then_inc(q["gate"], 1)
                    if past_part(i, e, NE, E + 1 if e == E else 1):
                        pe.wait_ge(q["prod"], nth_part(i, e, NE, E + 1 if e == E else 1))
                    pe.matmul(PS[:, 4, :], sw2[:, c], yT[:, u, :], start=True, stop=True).then_inc(q["value"], 1)

            def down(i, u, e):
                pe.wait_ge(q["hid"], nth_part(i, e, NE))
                if e < E:
                    if past_part(i, e, NE, 1):
                        pe.wait_ge(q["prod"], nth_part(i, e, NE, 1))
                    pe.matmul(PS[:, 3, :], w2[:, e, :], hid[:, e % 2, :], start=True, stop=True) \
                        .then_inc(q["down"], 1)
                else:
                    pe.wait_ge(q["prod"], nth_part(i, e, NE))
                    if e == E:
                        if past(i, 1):
                            pe.wait_ge(q["total"], q.nth("total", i, 1))
                    last = pe.matmul(PS[:, 5, :], sw3[:, e - E, :], prod[:, e % 2, :], start=(e == E),
                                     stop=(e == NE - 1))
                    last.then_inc(q["down"], 1)

            def turn_total(i, u):
                pe.wait_ge(q["total"], q.nth("total", i))
                pe.wait_ge(q["lt"], q.nth("lt", i, -1, NG))
                for g in range(G):
                    last = pe.transpose(PS[:, 7, g * D:(g + 1) * D], total[:, u, g * S:(g + 1) * S], m.IDENT[:, :])
                last.then_inc(q["totalT"], 1)

            def step(s, u, h):
                a = (u + 1) % 2
                if real(s, NG):
                    widen(s, u, 0)
                for e in range(NE):
                    if real(s, NG):
                        if e + 1 < E:
                            widen(s, u, e + 1)
                        gate_up(s, u, e)
                    if e == 0 and real(s - 1, NG):
                        down(s - 1, a, NE - 1)
                    if e > 0 and real(s, NG):
                        down(s, u, e - 1)
                    if e == 1 and real(s + 1, NG):
                        turn_y(s + 1, a)
                    if e == 2 and real(s - 1, NG):
                        turn_total(s - 1, a)
                    if e == 4 and real(s + 1, NG):
                        logits(s + 1, a)
                    if e == 8 and real(s + 1, NG):
                        turn_parts(s + 1, a)
            run_slots(pe, step, 1, 1, NG)

        @block.scalar
        def _(act):
            copy_y, exponential, copy_parts = front_scalar(act, m, q, yT, r, E, ("value", 2))

            def step(s, u, h):
                a = (u + 1) % 2
                for e in range(NE):
                    if real(s, NG):
                        act.wait_ge(q["gate"], nth_part(s, e, NE))
                        if past_part(s, e, NE, 2):
                            act.wait_ge(q["down"], nth_part(s, e, NE, 2))
                        if past_part(s, e, NE, 2):
                            act.wait_ge(q["prod"], nth_part(s, e, NE, 2))
                        bias = {"bias": b1[:, e:e + 1]} if e < E else {}
                        act.activation(hid[:, e % 2, :], PS[:, 0, :], ACT.Silu, **bias).then_inc(q["hid"], 1)
                        if e < E:
                            act.wait_ge(q["up"], nth_part(s, e, E))
                            act.activation(up[:, e % 2, :], PS[:, 1, :], ACT.Copy).then_inc(q["upc"], 1)
                    if e == 1 and real(s + 1, NG):
                        copy_y(s + 1, a)
                    if e == 5 and real(s + 1, NG):
                        exponential(s + 1, a)
                if real(s + 1, NG):
                    copy_parts(s + 1, a)
            run_slots(act, step, 1, 1, NG)

        @block.gpsimd
        def _(pool):
            def step(s, u, h):
                for e in range(E):
                    if real(s, NG):
                        pool.wait_ge(q["prod"], nth_part(s, e, NE))
                        if e == 0:
                            if past(s, 2):
                                pool.wait_ge(q["total"], q.nth("total", s, 2))
                            pool.sem_inc(q["held"], 1)
                            pool.tensor_copy(acc[:, u, :], prod[:, e % 2, :]).then_inc(q["acc"], 1)
                        else:
                            if past_part(s, e, E, 1):
                                pool.wait_ge(q["acc"], nth_part(s, e, E, 1))
                            pool.tensor_tensor(acc[:, u, :], acc[:, u, :], prod[:, e % 2, :], ALU.add) \
                                .then_inc(q["acc"], 1)
            run_slots(pool, step, 0, 0, NG)

        @block.vector
        def _(dve):
            def scale_x(i, u, e):
                dve.wait_ge(q["wide"], nth_part(i, e, E))
                if past_part(i, e, E, 2):
                    dve.wait_ge(q["up"], nth_part(i, e, E, 2))
                dve.tensor_tensor(xs[:, e % 2, :], yT[:, u, :], PS[:, 2, :], ALU.mult).then_inc(q["xs"], 1)

            def multiply(i, u, e):
                if e < E:
                    dve.wait_ge(q["down"], nth_part(i, e, NE))
                    dve.wait_ge(q["upc"], nth_part(i, e, E))
                    if past_part(i, e, E, 2):
                        dve.wait_ge(q["acc"], nth_part(i, e, E, 2))
                    dve.scalar_tensor_tensor(out=prod[:, e % 2, :], in0=PS[:, 3, :], scalar=b2[:, e:e + 1],
                                             in1=up[:, e % 2, :], op0=ALU.add, op1=ALU.mult).then_inc(q["prod"], 1)
                else:
                    dve.wait_ge(q["value"], nth_part(i, e - E, 2))
                    dve.wait_ge(q["hid"], nth_part(i, e, NE))
                    dve.wait_ge(q["acc"], nth_part(i, e - 2, E))
                    dve.tensor_tensor(prod[:, e % 2, :], hid[:, e % 2, :], PS[:, 4, :], ALU.mult) \
                        .then_inc(q["prod"], 1)

            def finish(i, u):
                dve.wait_ge(q["down"], nth_part(i, NE - 1, NE))
                dve.wait_ge(q["acc"], nth_part(i, E - 1, E))
                if past(i, 2):
                    dve.wait_ge(q["totalT"], q.nth("totalT", i, 2))
                dve.tensor_tensor(total[:, u, :], acc[:, u, :], PS[:, 5, :], ALU.add).then_inc(q["total"], 1)

            def step(s, u, h):
                a = (u + 1) % 2
                if real(s, NG):
                    scale_x(s, u, 0)
                for e in range(NE):
                    if real(s, NG) and e + 1 < E:
                        scale_x(s, u, e + 1)
                    if e == 0 and real(s - 1, NG):
                        finish(s - 1, a)
                    if e > 0 and real(s, NG):
                        multiply(s, u, e - 1)
                    if e == 3 and real(s - 1, NG):
                        dve.wait_ge(q["totalT"], q.nth("totalT", s - 1))
                        dve.tensor_tensor(group(m.X, s - 1), group(m.X, s - 1),
                                          PS[:, 7, :].rearrange("p (g d) -> p g d", d=D), ALU.add).then_inc(q["x"], 1)
                        dve.wait_ge(q["x"], q.nth("x", s - 1))
                        group_statistics(dve, m, s - 1)
                    if e == 4 and real(s + 1, NG):
                        route_logits(dve, q, r, PS[:, 7, 0:G * E].rearrange("p (g e) -> p g e", e=E), E, s + 1, a)
                    if e == 6 and real(s + 1, NG):
                        route_select(dve, q, r, E, K, False, True, s + 1, a)
                if real(s, NG):
                    multiply(s, u, NE - 1)
                if real(s + 2, NG):
                    normalise_group(dve, m, q, y, s + 2, u)
            run_slots(dve, step, 2, 1, NG)


def layer3_experts(nc, m, t):
    n = "L3_ffn_"
    E, K, CAP, I = 64, 4, 128, 64
    SLOTS = E * CAP
    NP = E // 2
    with ExitStack() as ctx:
        def sb(name, shape, dt=F32):
            return ctx.enter_context(nc.sbuf_tensor(f"e3_{name}", shape, dt))

        rows = nc.dram_tensor("expert_rows", (SLOTS, D), F32, kind="Internal").ap()
        results = nc.dram_tensor("expert_results", (SLOTS, D), F32, kind="Internal").ap()
        w1, w2 = sb("w1", [D, E, 2 * I]), sb("w2", [2 * I, NP, D])
        results_at = sb("results_at", [S, B, K], U32)
        weight = sb("weight", [S, B, K])
        q = Signals(ctx, nc, "e3", [
            "zeroed", "centred", "y", "yTps", "yT", "logits", "lmax", "lt", "exp", "lsum",
            "lrec", "prob", "top", "topk", "marked", "mask", "red", "ahead", "pos", "near", "far", "key", "skey1", "skey2",
            "keytop", "skeytop", "at", "pick", "passed", "scat0", "scat1", "in0", "in1", "xT", "xTs", "up", "gate",
            "hid", "hidT", "hidTs", "down", "ress", "store0", "store1", "atc", "gath0", "gath1",
            "sum0", "sum1", "sum2", "sum", "held", "out0", "out1", "loaded"])
        PS = m.PS

        with ExitStack() as inner:
            def sc(name, shape, dt=F32):
                return inner.enter_context(nc.sbuf_tensor(f"e3r_{name}", shape, dt))

            zero = sc("zero", [128, 2048])
            gate = sc("gate", [D, E])
            before_f, before = sc("before_f", [S, S]), sc("before", [S, S], BF16)
            ones = sc("ones", [S, S], BF16)
            slot0 = sc("slot0", [S, E])
            y, yT = sc("y", [S, 2, N]), sc("yT", [D, 2, N])
            lt, mx = sc("lt", [S, 2, G * E]), sc("mx", [S, 2, G])
            ex = sc("ex", [S, 2, G * (E + PAD)])
            mark = sc("mark", [S, 2, G * (E + PAD)])
            top = sc("top", [S, 2, G * 8])
            lsum, rec = sc("lsum", [S, 2, G]), sc("rec", [S, 2, G])
            mask = sc("mask", [S, 2, G * E], BF16)
            red = sc("red", [S, 2, E])
            ahead = sc("ahead", [S, 2, E], BF16)
            near, far = sc("near", [S, 2, G * E]), sc("far", [S, 2, G * E])
            key, skey = sc("key", [S, 2, G * E]), sc("skey", [S, 2, G * E])
            keytop, skeytop = sc("keytop", [S, 2, G * 8]), sc("skeytop", [S, 2, G * 8])
            rows_at = sc("rows_at", [S, 2, G * K], U32)
            junk = sc("junk", [S, 2, G * K * E])
            picked = sc("picked", [S, 2, G * K])

            with nc.Block() as block:
                loads = [(gate[:, :], t[n + "router_w"]), (before_f[:, :], t["c_before"]),
                         (slot0[:, :], t["c_slot0"])]

                @block.sync
                def _(sp):
                    for dst, src in loads:
                        sp.dma_start(dst, src).then_inc(m.s_weights, 16)
                m.weight_loads += 16 * len(loads)

                @block.vector
                def _(dve):
                    dve.memset(zero[:, :], 0.0)
                    dve.memset(ex[:, :, :], -1.0)
                    dve.memset(ones[:, :], 1.0)
                    dve.memset(ahead[:, :, :], 0.0)
                    dve.wait_ge(m.s_weights, m.weight_loads)
                    dve.tensor_copy(before[:, :], before_f[:, :])

            norm_stats(nc, m)

            with nc.Block() as block:
                @block.sync
                def _(sp):
                    for k in range(4):
                        sp.dma_start(rows[k * (SLOTS // 4):(k + 1) * (SLOTS // 4), :]
                                     .rearrange("(p a) d -> p (a d)", p=128), zero[:, :]).then_inc(q["zeroed"], 16)
                    sp.dma_start(w1[:, :, :], t[n + "w1"]).then_inc(q["loaded"], 16)
                    sp.dma_start(w2[:, :, :], t[n + "w2"]).then_inc(q["loaded"], 16)
                    sp.wait_ge(q["loaded"], 32)

                @block.tensor
                def _(pe):
                    def front(i, u):
                        pe.wait_ge(q["y"], q.nth("y", i))
                        if past(i, 1):
                            pe.wait_ge(q["yT"], q.nth("yT", i, 1))
                        for g in range(G):
                            last = pe.transpose(PS[:, 6, g * S:(g + 1) * S], y[:, u, g * D:(g + 1) * D], m.IDENT[:, :])
                        last.then_inc(q["yTps"], 1)

                    def logits(i, u):
                        pe.wait_ge(q["yT"], q.nth("yT", i))
                        if past(i, 1):
                            pe.wait_ge(q["lt"], q.nth("lt", i, 1))
                        for g in range(G):
                            last = pe.matmul(PS[:, 7, g * E:(g + 1) * E], yT[:, u, g * S:(g + 1) * S], gate[:, :],
                                             start=True, stop=True)
                        last.then_inc(q["logits"], 1)

                    def positions(i, u):
                        pe.wait_ge(q["mask"], q.nth("mask", i))
                        if past(i, 1):
                            pe.wait_ge(q["ahead"], q.nth("ahead", i, 1))
                        if past(i, 1):
                            pe.wait_ge(q["far"], q.nth("far", i, 1))
                        for g in range(G):
                            out = PS[:, 5, g * E:(g + 1) * E]
                            pe.matmul(out, before[:, :], mask[:, u, g * E:(g + 1) * E], start=(g == 0), stop=False,
                                      skip_group_check=True)
                            for c in range(g):
                                pe.matmul(out, ones[:, :], mask[:, u, c * E:(c + 1) * E], start=False, stop=False,
                                          skip_group_check=True)
                            last = pe.matmul(out, ones[:, :], ahead[:, u, :], start=False, stop=(g == G - 1),
                                             skip_group_check=True)
                        last.then_inc(q["pos"], 1)

                    def step(s, u, h):
                        a = (u + 1) % 2
                        if real(s + 1, NG):
                            front(s + 1, a)
                            logits(s + 1, a)
                        if real(s, NG):
                            positions(s, u)
                    run_slots(pe, step, 1, 0, NG)

                @block.scalar
                def _(act):
                    act.activation(m.scratch[:, 0:1], m.scratch[:, 1:2], ACT.Exp)

                    def step(s, u, h):
                        a = (u + 1) % 2
                        if real(s + 1, NG):
                            act.wait_ge(q["yTps"], q.nth("yTps", s + 1))
                            if past(s + 1, 2):
                                act.wait_ge(q["logits"], q.nth("logits", s + 1, 2))
                            act.activation(yT[:, a, :], PS[:, 6, :], ACT.Copy).then_inc(q["yT"], 1)
                        if real(s, NG):
                            act.wait_ge(q["lt"], q.nth("lt", s))
                            if past(s, 2):
                                act.wait_ge(q["pick"], q.nth("pick", s, 2))
                            act.activation(ex[:, u, :].rearrange("p (g e) -> p g e", e=E + PAD)[:, :, 0:E],
                                           lt[:, u, :].rearrange("p (g e) -> p g e", e=E), ACT.Exp).then_inc(q["exp"], 1)
                    run_slots(act, step, 1, 0, NG)

                @block.gpsimd
                def _(pool):
                    pool.wait_ge(q["zeroed"], 64)

                    def step(s, u, h):
                        pool.wait_ge(q["at"], q.nth("at", s))
                        pool.sem_inc(q["held"], 1)
                        for g in range(G):
                            for k in range(K):
                                pool.indirect_dma_start(
                                    out=rows[:, :],
                                    out_offset=bass.IndirectOffsetOnAxis(ap=rows_at[:, u, g * K + k:g * K + k + 1], axis=0),
                                    in_=y[:, u, g * D:(g + 1) * D], in_offset=None,
                                    bounds_check=SLOTS - 1, oob_is_err=False).then_inc(q[f"scat{u}"], 16)
                    run_slots(pool, step, 0, 0, NG)
                    for u in range(2):
                        pool.wait_ge(q[f"scat{u}"], NG // 2 * G * K * 16)

                @block.vector
                def _(dve):
                    def normalise(i, u, h):
                        if not isinstance(i, int) or i >= 2:
                            dve.wait_ge(q[f"scat{u}"], h * (G * K * 16))
                        y3 = y[:, u, :].rearrange("p (g d) -> p g d", d=D)
                        dve.tensor_tensor(y3, group(m.X, i), bcast(m.MEAN[:, bass.ds(i * G, G)], 2, D),
                                          ALU.subtract).then_inc(q["centred"], 1)
                        dve.wait_ge(q["centred"], q.nth("centred", i))
                        dve.tensor_tensor(y3, y3, bcast(m.RSTD[:, bass.ds(i * G, G)], 2, D), ALU.mult) \
                            .then_inc(q["y"], 1)

                    def less_max(i, u):
                        lg = PS[:, 7, 0:G * E].rearrange("p (g e) -> p g e", e=E)
                        dve.wait_ge(q["logits"], q.nth("logits", i))
                        dve.tensor_reduce(mx[:, u, :], lg, AX, ALU.max).then_inc(q["lmax"], 1)
                        dve.wait_ge(q["lmax"], q.nth("lmax", i))
                        if past(i, 2):
                            dve.wait_ge(q["exp"], q.nth("exp", i, 2))
                        dve.tensor_tensor(lt[:, u, :].rearrange("p (g e) -> p g e", e=E), lg, bcast(mx[:, u, :], 2, E),
                                          ALU.subtract).then_inc(q["lt"], 1)

                    def select(i, u):
                        ex3 = ex[:, u, :].rearrange("p (g e) -> p g e", e=E + PAD)
                        mark3 = mark[:, u, :].rearrange("p (g e) -> p g e", e=E + PAD)
                        dve.wait_ge(q["exp"], q.nth("exp", i))
                        dve.tensor_reduce(lsum[:, u, :], ex3[:, :, 0:E], AX, ALU.add).then_inc(q["lsum"], 1)
                        dve.wait_ge(q["lsum"], q.nth("lsum", i))
                        dve.reciprocal(rec[:, u, :], lsum[:, u, :]).then_inc(q["lrec"], 1)
                        dve.wait_ge(q["lrec"], q.nth("lrec", i))
                        dve.tensor_tensor(ex3[:, :, 0:E], ex3[:, :, 0:E], bcast(rec[:, u, :], 2, E), ALU.mult) \
                            .then_inc(q["prob"], 1)
                        dve.wait_ge(q["prob"], q.nth("prob", i))
                        dve.sem_inc(q["passed"], 1)
                        for g in range(G):
                            last = dve.max(top[:, u, 8 * g:8 * g + 8], ex3[:, g, 0:E])
                        last.then_inc(q["top"], 1)
                        dve.wait_ge(q["top"], q.nth("top", i))
                        dve.memset(top[:, u, :].rearrange("p (g e) -> p g e", e=8)[:, :, K:8], -1.0) \
                            .then_inc(q["topk"], 1)
                        dve.wait_ge(q["topk"], q.nth("topk", i))
                        dve.sem_inc(q["passed"], 1)
                        for g in range(G):
                            last = dve.match_replace(mark3[:, g, :], top[:, u, 8 * g:8 * g + 8], ex3[:, g, :], -2.0)
                        last.then_inc(q["marked"], 1)
                        dve.wait_ge(q["marked"], q.nth("marked", i))
                        if past(i, 2):
                            dve.wait_ge(q["pos"], q.nth("pos", i, 2))
                        dve.tensor_scalar(mask[:, u, :].rearrange("p (g e) -> p g e", e=E), mark3[:, :, 0:E], -1.5,
                                          None, ALU.is_lt).then_inc(q["mask"], 1)
                        dve.wait_ge(q["mask"], q.nth("mask", i))
                        dve.tensor_reduce(red[:, u, :], mask[:, u, :].rearrange("p (g e) -> p e g", e=E), AX,
                                          ALU.add).then_inc(q["red"], 1)
                        dve.wait_ge(q["red"], q.nth("red", i))
                        if past(i, 1):
                            dve.wait_ge(q["pos"], q.nth("pos", i, 1))
                        dve.tensor_tensor(ahead[:, (u + 1) % 2, :], ahead[:, u, :], red[:, u, :], ALU.add) \
                            .then_inc(q["ahead"], 1)

                    def place(i, u):
                        pos = PS[:, 5, 0:G * E].rearrange("p (g e) -> p g e", e=E)
                        mask_row = mask[:, u, :]
                        dve.wait_ge(q["pos"], q.nth("pos", i))
                        dve.scalar_tensor_tensor(out=near[:, u, :].rearrange("p (g e) -> p g e", e=E), in0=pos,
                                                 scalar=CAP - 1.0, in1=bcast(slot0[:, :], 1, G), op0=ALU.min,
                                                 op1=ALU.add).then_inc(q["near"], 1)
                        dve.tensor_scalar(far[:, u, :], PS[:, 5, 0:G * E], float(CAP), float(SLOTS), ALU.is_ge,
                                          ALU.mult).then_inc(q["far"], 1)
                        dve.wait_ge(q["near"], q.nth("near", i))
                        dve.tensor_tensor(key[:, u, :], near[:, u, :], mask_row, ALU.mult).then_inc(q["key"], 1)
                        dve.wait_ge(q["far"], q.nth("far", i))
                        dve.tensor_tensor(skey[:, u, :], near[:, u, :], far[:, u, :], ALU.add).then_inc(q["skey1"], 1)
                        dve.wait_ge(q["skey1"], q.nth("skey1", i))
                        dve.tensor_tensor(skey[:, u, :], skey[:, u, :], mask_row, ALU.mult).then_inc(q["skey2"], 1)
                        dve.wait_ge(q["key"], q.nth("key", i))
                        dve.wait_ge(q["skey2"], q.nth("skey2", i))
                        dve.sem_inc(q["passed"], 1)
                        for g in range(G):
                            dve.max(keytop[:, u, 8 * g:8 * g + 8], key[:, u, g * E:(g + 1) * E])
                            last = dve.max(skeytop[:, u, 8 * g:8 * g + 8], skey[:, u, g * E:(g + 1) * E])
                        last.then_inc(q["keytop"], 1)
                        dve.wait_ge(q["keytop"], q.nth("keytop", i))
                        k3 = keytop[:, u, :].rearrange("p (g e) -> p g e", e=8)
                        s3 = skeytop[:, u, :].rearrange("p (g e) -> p g e", e=8)
                        dve.tensor_scalar(group(results_at, i), k3[:, :, 0:K], -1.0, None, ALU.add)
                        dve.tensor_scalar(rows_at[:, u, :].rearrange("p (g k) -> p g k", k=K), s3[:, :, 0:K], -1.0,
                                          None, ALU.add).then_inc(q["at"], 1)
                        for g in range(G):
                            for k in range(K):
                                c = g * K + k
                                last = dve.scalar_tensor_tensor(
                                    out=junk[:, u, c * E:(c + 1) * E], in0=key[:, u, g * E:(g + 1) * E],
                                    scalar=keytop[:, u, 8 * g + k:8 * g + k + 1],
                                    in1=ex[:, u, g * (E + PAD):g * (E + PAD) + E], op0=ALU.is_equal, op1=ALU.mult,
                                    accum_out=picked[:, u, c:c + 1])
                        last.then_inc(q["pick"], 1)
                        dve.wait_ge(q["pick"], q.nth("pick", i))
                        dve.tensor_copy(group(weight, i), picked[:, u, :].rearrange("p (g k) -> p g k", k=K))

                    def step(s, u, h):
                        a = (u + 1) % 2
                        if real(s, NG):
                            less_max(s, u)
                        if real(s + 1, NG):
                            normalise(s + 1, a, h + u)
                        if real(s, NG):
                            select(s, u)
                            place(s, u)
                    run_slots(dve, step, 1, 0, NG)

        with ExitStack() as inner:
            def sc(name, shape, dt=F32):
                return inner.enter_context(nc.sbuf_tensor(f"e3x_{name}", shape, dt))

            xin = sc("xin", [CAP, 2, 2 * D])
            xT = sc("xT", [D, 2, 2 * CAP])
            gated = sc("gated", [CAP, 2, 2 * I])
            hid = sc("hid", [CAP, 2, 4 * I])
            hidT = sc("hidT", [2 * I, 2, 2 * CAP])
            res = sc("res", [CAP, 2, 2 * D])

            with nc.Block() as block:
                @block.vector
                def _(dve):
                    dve.memset(hid[:, :, :], 0.0)

            block = inner.enter_context(nc.Block())

            def slots(table, i):
                return table[bass.ds(i * 2 * CAP, 2 * CAP), :].rearrange("(e p) d -> p e d", p=CAP)

            @block.sync
            def _(sp):
                def step(s, u, h):
                    if real(s + 2, NP):
                        if past(s + 2, 2):
                            sp.wait_ge(q["xT"], q.nth("xT", s + 2, 2))
                        sp.dma_start(xin[:, u, :].rearrange("p (e d) -> p e d", d=D), slots(rows, s + 2)) \
                            .then_inc(q[f"in{u}"], 16)
                    if real(s, NP):
                        sp.wait_ge(q["ress"], q.nth("ress", s))
                        sp.dma_start(slots(results, s), res[:, u, :].rearrange("p (e d) -> p e d", d=D)) \
                            .then_inc(q[f"store{u}"], 16)
                run_slots(sp, step, 2, 0, NP)
                for u in range(2):
                    sp.wait_ge(q[f"store{u}"], NP // 2 * 16)

            @block.tensor
            def _(pe):
                def turn_rows(i, u, h):
                    pe.wait_ge(q[f"in{u}"], h * 16 + 16)
                    if past(i, 1):
                        pe.wait_ge(q["xTs"], q.nth("xTs", i, 1))
                    for e in range(2):
                        last = pe.transpose(PS[:, 0, e * CAP:(e + 1) * CAP], xin[:, u, e * D:(e + 1) * D],
                                            m.IDENT[:, :])
                    last.then_inc(q["xT"], 1)

                def up(i, u):
                    pe.wait_ge(q["xTs"], q.nth("xTs", i))
                    if past(i, 2):
                        pe.wait_ge(q["hid"], q.nth("hid", i, 2))
                    for e in range(2):
                        last = pe.matmul(PS[:, 1 + u, e * 2 * I:(e + 1) * 2 * I], xT[:, u, e * CAP:(e + 1) * CAP],
                                         seq(w1, 2 * i + e), start=True, stop=True)
                    last.then_inc(q["up"], 1)

                def turn_hidden(i, u):
                    pe.wait_ge(q["hid"], q.nth("hid", i))
                    if past(i, 1):
                        pe.wait_ge(q["hidTs"], q.nth("hidTs", i, 1))
                    for e in range(2):
                        last = pe.transpose(PS[:, 3, e * CAP:(e + 1) * CAP], hid[:, u, e * 2 * I:(e + 1) * 2 * I],
                                            m.IDENT[:, :])
                    last.then_inc(q["hidT"], 1)

                def down(i, u):
                    pe.wait_ge(q["hidTs"], q.nth("hidTs", i))
                    if past(i, 2):
                        pe.wait_ge(q["ress"], q.nth("ress", i, 2))
                    for e in range(2):
                        last = pe.matmul(PS[:, 4 + u, e * D:(e + 1) * D], hidT[:, u, e * CAP:(e + 1) * CAP],
                                         seq(w2, i), start=True, stop=True)
                    last.then_inc(q["down"], 1)

                def step(s, u, h):
                    a = (u + 1) % 2
                    if real(s + 1, NP):
                        turn_rows(s + 1, a, h + u)
                    if real(s, NP):
                        turn_hidden(s, u)
                    if real(s + 1, NP):
                        up(s + 1, a)
                    if real(s, NP):
                        down(s, u)
                run_slots(pe, step, 1, 0, NP)

            @block.scalar
            def _(act):
                act.activation(m.scratch[:, 0:1], m.scratch[:, 1:2], ACT.Silu)

                def step(s, u, h):
                    a = (u + 1) % 2
                    if real(s + 1, NP):
                        act.wait_ge(q["xT"], q.nth("xT", s + 1))
                        if past(s + 1, 2):
                            act.wait_ge(q["up"], q.nth("up", s + 1, 2))
                        act.activation(xT[:, a, :], PS[:, 0, 0:2 * CAP], ACT.Copy).then_inc(q["xTs"], 1)
                    if real(s, NP):
                        act.wait_ge(q["hidT"], q.nth("hidT", s))
                        if past(s, 2):
                            act.wait_ge(q["down"], q.nth("down", s, 2))
                        act.activation(hidT[:, u, :], PS[:, 3, 0:2 * CAP], ACT.Copy).then_inc(q["hidTs"], 1)
                    if real(s + 1, NP):
                        act.wait_ge(q["up"], q.nth("up", s + 1))
                        if past(s + 1, 2):
                            act.wait_ge(q["hid"], q.nth("hid", s + 1, 2))
                        act.activation(gated[:, a, :].rearrange("p (e c) -> p e c", e=2),
                                       PS[:, 1 + a, 0:4 * I].rearrange("p (e c) -> p e c", e=2)[:, :, 0:I],
                                       ACT.Silu).then_inc(q["gate"], 1)
                run_slots(act, step, 1, 0, NP)

            @block.vector
            def _(dve):
                def step(s, u, h):
                    a = (u + 1) % 2
                    if real(s + 1, NP):
                        dve.wait_ge(q["gate"], q.nth("gate", s + 1))
                        if past(s + 1, 2):
                            dve.wait_ge(q["hidT"], q.nth("hidT", s + 1, 2))
                        dve.tensor_tensor(hid[:, a, :].rearrange("p (k c) -> p k c", c=I)[:, 0:4:3, :],
                                          gated[:, a, :].rearrange("p (e c) -> p e c", e=2),
                                          PS[:, 1 + a, 0:4 * I].rearrange("p (e c) -> p e c", e=2)[:, :, I:2 * I],
                                          ALU.mult).then_inc(q["hid"], 1)
                    if real(s, NP):
                        dve.wait_ge(q["down"], q.nth("down", s))
                        if not isinstance(s, int) or s >= 2:
                            dve.wait_ge(q[f"store{u}"], h * 16)
                        dve.tensor_copy(res[:, u, :], PS[:, 4 + u, 0:2 * D]).then_inc(q["ress"], 1)
                run_slots(dve, step, 1, 0, NP)

        with ExitStack() as inner:
            yk = inner.enter_context(nc.sbuf_tensor("e3c_yk", [S, 2, K * D], F32))
            part = inner.enter_context(nc.sbuf_tensor("e3c_part", [S, 2, K * D], F32))
            at = inner.enter_context(nc.sbuf_tensor("e3c_at", [S, 2, K], U32))
            block = inner.enter_context(nc.Block())

            @block.gpsimd
            def _(pool):
                def step(s, u, h):
                    pool.wait_ge(q["atc"], q.nth("atc", s))
                    if past(s, 2):
                        pool.wait_ge(q["sum"], q.nth("sum", s, 2))
                    pool.sem_inc(q["held"], 1)
                    for k in range(K):
                        pool.indirect_dma_start(
                            out=yk[:, u, k * D:(k + 1) * D], out_offset=None, in_=results[:, :],
                            in_offset=bass.IndirectOffsetOnAxis(ap=at[:, u, k:k + 1], axis=0)) \
                            .then_inc(q[f"gath{u}"], 16)
                run_slots(pool, step, 0, 0)

            @block.vector
            def _(dve):
                def step(s, u, h):
                    a = (u + 1) % 2
                    if real(s + 1):
                        if not isinstance(s, int) or s + 1 >= 2:
                            dve.wait_ge(q[f"gath{a}"], (h + u) * (16 * K))
                        dve.tensor_copy(at[:, a, :], seq(results_at, s + 1)).then_inc(q["atc"], 1)
                    if not real(s):
                        return
                    dve.wait_ge(q[f"gath{u}"], h * (16 * K) + 16 * K)
                    if not isinstance(s, int) or s >= 2:
                        dve.wait_ge(q[f"out{u}"], h * 16)
                    for k in range(K):
                        src = seq(m.X, s) if k == 0 else part[:, u, (k - 1) * D:k * D]
                        dve.scalar_tensor_tensor(out=part[:, u, k * D:(k + 1) * D], in0=yk[:, u, k * D:(k + 1) * D],
                                                 scalar=seq(weight, s)[:, k:k + 1], in1=src, op0=ALU.mult, op1=ALU.add) \
                            .then_inc(q["sum" if k == K - 1 else f"sum{k}"], 1)
                        if k < K - 1:
                            dve.wait_ge(q[f"sum{k}"], q.nth(f"sum{k}", s))
                run_slots(dve, step, 1, 0)

            @block.sync
            def _(sp):
                def step(s, u, h):
                    sp.wait_ge(q["sum"], q.nth("sum", s))
                    sp.dma_start(t["out"][bass.ds(s, 1), :, :].rearrange("b s d -> (b s) d"),
                                 part[:, u, (K - 1) * D:K * D]).then_inc(q[f"out{u}"], 16)
                run_slots(sp, step, 0, 0)
                for u in range(2):
                    sp.wait_ge(q[f"out{u}"], B // 2 * 16)


def program(nc, t):
    with ExitStack() as ctx:
        def sb(name, shape, dt=F32):
            return ctx.enter_context(nc.sbuf_tensor(name, shape, dt))

        def sem(name):
            return ctx.enter_context(nc.semaphore(name))

        m = Named()
        m.X = sb("X", [S, B, D])
        m.STATS = sb("STATS", [S, B, 6])
        m.MEAN = sb("MEAN", [S, B])
        m.RSTD = sb("RSTD", [S, B])
        m.MINUS_HALF = sb("MINUS_HALF", [S, B])
        m.IDENT = sb("IDENT", [S, S])
        m.IDENT_BF = sb("IDENT_BF", [S, S], BF16)
        m.WIDTH_TOKENS = sb("WIDTH_TOKENS", [S, D])
        m.WIDTH_FEATURES = sb("WIDTH_FEATURES", [D, S])
        m.HEAD = {8: sb("HEAD8", [D, 4]), 16: sb("HEAD16", [D, 2])}
        m.scratch = sb("scratch", [S, 2])
        m.PS = ctx.enter_context(nc.psum_tensor("PS", [128, 8, BANK], F32))
        m.s_weights = sem("weights")
        m.s_norm_a = sem("norm_parts")
        m.s_norm_b = sem("norm_rstd")
        m.norms = m.weight_loads = m.ctx_loads = m.mask_loads = m.preps = 0
        m.at = Signals(ctx, nc, "at", [
            "prep", "fold", "ctx0", "ctx1", "mask0", "mask1",
            "y", "yTps", "yT", "proj", "q", "k", "v", "scores", "sfree", "mx", "pv", "oT", "back",
            "rec", "O", "OTps", "OT", "out", "bias", "x", "T", "xT", "PT0", "PT1", "PT2", "PT3",
            "P0", "P1", "P2", "P3", "passed", "r1", "t1", "r2", "r2cut", "abs0", "abs1", "abs2", "abs3",
            "y0", "yraw", "istat", "imv", "ivar", "irstd", "Oall", "tmp"])
        load_x(nc, m, t)
        layers = [layer0_cross, layer0_experts, layer1_cross, layer1_experts, layer2_cross,
                  layer2_self, layer3_cross, layer3_experts]
        for p in PHASES:
            layers[p](nc, m, t)
        if 7 not in PHASES:
            with nc.Block() as block:
                @block.sync
                def _(sp):
                    sp.dma_start(t["out"].rearrange("b s d -> s b d"), m.X[:, :, :]).then_inc(m.s_weights, 16)
                    sp.wait_ge(m.s_weights, m.weight_loads + 16)


def load_x(nc, m, t):
    with ExitStack() as ctx:
        parts = 8
        s_x = [ctx.enter_context(nc.semaphore(f"x_in{n}")) for n in range(parts)]
        s_const = ctx.enter_context(nc.semaphore("const_in"))
        block = ctx.enter_context(nc.Block())
        consts = [(m.IDENT, "c_ident"), (m.WIDTH_TOKENS, "c_width_tokens"), (m.WIDTH_FEATURES, "c_width_features"),
                  (m.HEAD[8], "c_head8"), (m.HEAD[16], "c_head16")]

        @block.sync
        def _(sp):
            x = t["x"].rearrange("b s d -> s b d")
            for n in range(parts):
                c = slice(n * B // parts, (n + 1) * B // parts)
                sp.dma_start(m.X[:, c, :], x[:, c, :]).then_inc(s_x[n], 16)
            for dst, name in consts:
                sp.dma_start(dst[:, :], t[name]).then_inc(s_const, 16)
            sp.wait_ge(s_const, 16 * len(consts))

        @block.gpsimd
        def _(pool):
            pool.memset(m.MINUS_HALF[:, :], -0.5)
            pool.memset(m.scratch[:, :], 0.0)

        @block.vector
        def _(dve):
            dve.wait_ge(s_const, 16 * len(consts))
            dve.tensor_copy(m.IDENT_BF[:, :], m.IDENT[:, :])
            for b in range(B):
                if b % (B // parts) == 0:
                    dve.wait_ge(s_x[b // (B // parts)], 16)
                dve.bn_stats(m.STATS[:, b, :], m.X[:, b, :])


def layer1_cross(nc, m, t):
    n = "L1_xattn_"
    w = Named()
    w.Wq, w.Wk, w.Wv, w.Wo = t[n + "Wq"], t[n + "Wkv"][:, 0:D], t[n + "Wkv"][:, D:2 * D], t[n + "Wo"]
    w.bq, w.bk, w.bv, w.bo = t[n + "bq"], t[n + "bkv"][0:D], t[n + "bkv"][D:2 * D], t[n + "bo"]
    attention_layer(nc, m, 0, w, heads=16, keys=C, scale=8 ** -0.5, context=t["ctxT"])


def layer2_cross(nc, m, t):
    n = "L2_xattn_"
    w = Named()
    w.Wq, w.Wk, w.Wv, w.Wo = (t[n + f"W{c}T"] for c in "qkvo")
    w.bq, w.bk, w.bv, w.bo = (t[n + f"b{c}"] for c in "qkvo")
    attention_layer(nc, m, 1, w, heads=16, keys=C, scale=8 ** -0.5, context=t["ctxT"], mask=t["mask"])


def layer2_self(nc, m, t):
    n = "L2_ffn_"
    w = Named()
    w.Wq, w.Wk, w.Wv, w.Wo = (t[n + f"{c}_wT"] for c in "qkvo")
    w.bq, w.bk, w.bv, w.bo = (t[n + f"{c}_b"] for c in "qkvo")
    w.nw, w.nb = t[n + "norm_w"], t[n + "norm_b"]
    attention_layer(nc, m, 2, w, heads=8, keys=S, scale=D ** -0.5, inner=True)


def layer3_cross(nc, m, t):
    n = "L3_xattn_"
    w = Named()
    w.U, w.V = [t[n + f"U{c}T"] for c in "qkvo"], [t[n + f"V{c}T"] for c in "qkvo"]
    w.bq, w.bk, w.bv, w.bo = (t[n + f"b{c}"] for c in "qkvo")
    attention_layer(nc, m, 3, w, heads=16, keys=C, scale=8 ** -0.5, context=t["ctxT_reversed"], topk=64,
                    lowrank=True)



def laid_out(inputs):
    import numpy as np
    a = {n: np.asarray(v) for n, v in inputs.items()}
    ctx = a["ctx_1024"]
    out = {"x": a["x"], "ctxT": ctx.transpose(2, 0, 1), "ctxT_reversed": ctx[:, ::-1].transpose(2, 0, 1),
           "mask": a["mask_Bx1xSxS2_fk0"][:, 0].transpose(1, 0, 2), "q_masks": a["mask_BxS2_ik0"]}
    for n, v in a.items():
        if n[0:2] in ("L0", "L1", "L2", "L3"):
            out[n] = v
    out["L0_ffn_gate_w"] = a["L0_ffn_gate_w"].T
    for n in ("L0_ffn_w1", "L0_ffn_w3"):
        out[n] = a[n].transpose(1, 0, 2).reshape(D, -1)
    out["L0_ffn_w2"] = a["L0_ffn_w2"].reshape(8, 128, D).transpose(1, 0, 2)
    out["L1_ffn_gate_w"] = a["L1_ffn_gate_w"].T
    for n in ("L1_ffn_w1", "L1_ffn_w2", "L1_ffn_w3"):
        out[n] = a[n].transpose(2, 0, 1)
    for n in ("L1_ffn_b1", "L1_ffn_b2", "L1_ffn_sw1", "L1_ffn_sw2"):
        out[n] = a[n].T
    out["L1_ffn_sw3"] = a["L1_ffn_sw3"].reshape(D, 2, 128).transpose(2, 1, 0)
    out["L3_ffn_w1"] = a["L3_ffn_w1"].transpose(1, 0, 2)
    out["L3_ffn_w2"] = a["L3_ffn_w2"].reshape(32, 128, D).transpose(1, 0, 2)
    out["c_before"] = (np.arange(S)[:, None] < np.arange(S)[None, :]).astype(np.float32)
    out["c_slot0"] = (np.zeros((S, 1)) + np.arange(64)[None, :] * 128 + 1).astype(np.float32)
    for n in ("L2_xattn_Wq", "L2_xattn_Wk", "L2_xattn_Wv", "L2_xattn_Wo", "L2_ffn_q_w", "L2_ffn_k_w",
              "L2_ffn_v_w", "L2_ffn_o_w", "L3_xattn_Uq", "L3_xattn_Uk", "L3_xattn_Uv", "L3_xattn_Uo",
              "L3_xattn_Vq", "L3_xattn_Vk", "L3_xattn_Vv", "L3_xattn_Vo"):
        out[n + "T"] = out.pop(n).T
    f, tok = np.arange(D), np.arange(S)
    width = (f[None, :] < (D >> (tok[:, None] // 32))).astype(np.float32)
    out["c_ident"] = np.eye(S, dtype=np.float32)
    out["c_width_tokens"] = width
    out["c_width_features"] = width.T
    row, pair, expert = np.arange(72), np.arange(8), np.arange(8)
    half = 2 * pair[None, :, None] + (f // 64)[None, None, :]
    out["c_pick_pairs"] = ((row[:, None, None] % 16 == half) & (row[:, None, None] < 48)).astype(np.float32)
    mine = row[:, None] % 8 == expert[None, :]
    out["c_pick_weight"] = np.repeat((mine & (row[:, None] < 24))[:, :, None], D, 2).astype(np.float32)
    part = 24 + 8 * np.arange(3)
    out["c_pick_bias"] = (mine[:, None, :] & (row[:, None, None] // 8 * 8 == part[None, :, None])).astype(np.float32)
    for dh in (8, 16):
        out[f"c_head{dh}"] = ((f[:, None] % 32) // dh == np.arange(32 // dh)[None, :]).astype(np.float32)
    return out


def kernel(**inputs):
    import numpy as _np
    import concourse.bacc as _bacc
    from concourse import mybir as _mybir
    from concourse.bass_utils import run_bass_kernel_spmd as _run

    nc = _bacc.Bacc("TRN2", target_bir_lowering=False, num_devices=1)
    arrays, t = {}, {}
    for name, a in laid_out(inputs).items():
        a = _np.ascontiguousarray(a)
        arrays[f"in_{name}"] = a
        t[name] = nc.dram_tensor(f"in_{name}", a.shape, _mybir.dt.from_np(a.dtype), kind="ExternalInput").ap()
    t["out"] = nc.dram_tensor("out", (B, S, D), _mybir.dt.float32, kind="ExternalOutput").ap()
    program(nc, t)
    r = _run(nc, [arrays], core_ids=[0])
    return r.results[0]["out"]
```

```python
from contextlib import ExitStack

import concourse.bass as bass
from concourse import mybir

F32 = mybir.dt.float32
BF16 = mybir.dt.bfloat16
I32 = mybir.dt.int32
U32 = mybir.dt.uint32
ALU = mybir.AluOpType
ACT = mybir.ActivationFunctionType
AX = mybir.AxisListType.X

B = 64
S = 128
D = 128
C = 77
EPS = 1e-5
FIRST = 24
BANK = 512
FAR = -3.0e38



class Named:
    pass


def real(i, n=B):
    return not isinstance(i, int) or 0 <= i < n


def past(i, back):
    return not isinstance(i, int) or i >= back


def nth_part(i, p, per, back=0):
    return i * per + (p + 1 - back)


def past_part(i, p, per, back):
    return not isinstance(i, int) or nth_part(i, p, per, back) > 0


def run_slots(eng, step, lead, tail, n=B, slots=2):
    first = 4
    last = first + (n - max(lead, 2) - first) // slots * slots
    for s in range(-lead, first):
        step(s, s % slots, s // 2)
    with eng.Fori(0, (last - first) // slots) as j:
        h = eng.snap(j * (slots // 2) + first // 2)
        s0 = eng.snap(2 * h)
        for v in range(slots):
            step(s0 + v, v, h + v // 2 if v > 1 else h)
    for s in range(last, n + tail):
        step(s, s % slots, s // 2)


class Signals(dict):

    def __init__(self, ctx, nc, prefix, names):
        super().__init__((n, nc.alloc_semaphore(f"{prefix}_{n}")) for n in names)
        self.done = {n: 0 for n in names}
        ctx.callback(self.give_back, nc)

    def nth(self, name, i, back=0, n=B):
        if isinstance(i, int):
            i = min(i - back, n - 1) + back
        return i + (self.done[name] + 1 - back)

    def give_back(self, nc):
        nc.clear_and_free_semaphores(list(self.values()))
        nc.all_engine_barrier()


def bcast(ap, axis, n):
    a = ap.unsqueeze(axis)
    shape = list(a.shape)
    shape[axis] = n
    return a.broadcast_to(shape)



def norm_vector(dve, m):
    t, k = m.norm_tmp, m.norms
    mean_even, var_even = m.STATS[:, :, 1], m.STATS[:, :, 2]
    mean_odd, var_odd = m.STATS[:, :, 4], m.STATS[:, :, 5]
    dve.tensor_tensor(t[:, 0, :], mean_even, mean_odd, ALU.add)
    dve.tensor_tensor(t[:, 1, :], mean_even, mean_odd, ALU.subtract)
    dve.tensor_tensor(t[:, 2, :], var_even, var_odd, ALU.add).then_inc(m.s_norm_a, 1)
    dve.wait_ge(m.s_norm_a, 4 * k + 1)
    dve.tensor_scalar(m.MEAN[:, :], t[:, 0, :], 0.5, None, ALU.mult)
    dve.tensor_tensor(t[:, 3, :], t[:, 1, :], t[:, 1, :], ALU.mult).then_inc(m.s_norm_a, 1)
    dve.wait_ge(m.s_norm_a, 4 * k + 2)
    dve.tensor_scalar(t[:, 1, :], t[:, 3, :], 0.25, EPS, ALU.mult, ALU.add).then_inc(m.s_norm_a, 1)
    dve.wait_ge(m.s_norm_a, 4 * k + 3)
    dve.scalar_tensor_tensor(out=t[:, 0, :], in0=t[:, 2, :], scalar=1.0 / D, in1=t[:, 1, :],
                             op0=ALU.mult, op1=ALU.add).then_inc(m.s_norm_a, 1)


def norm_gpsimd(pool, m):
    pool.wait_ge(m.s_norm_a, 4 * m.norms + 4)
    pool.tensor_tensor(m.RSTD[:, 0:FIRST], m.norm_tmp[:, 0, 0:FIRST], m.MINUS_HALF[:, 0:FIRST], ALU.pow) \
        .then_inc(m.s_norm_b, 1)


def norm_gpsimd_rest(pool, m):
    pool.tensor_tensor(m.RSTD[:, FIRST:B], m.norm_tmp[:, 0, FIRST:B], m.MINUS_HALF[:, FIRST:B], ALU.pow) \
        .then_inc(m.s_norm_b, 1)



def attention_layer(nc, m, k, w, heads, keys, scale, context=None, mask=None, topk=0, lowrank=False,
                    inner=None):
    dh = D // heads
    hpg = 32 // dh
    groups = heads // 4
    lag = 2 if topk else 1
    slots = 4
    k_ready = "k_by_scalar" if topk else "k"
    sfree = "copied" if topk else "sfree"
    less_max = "T" if mask is not None or topk else "sfree"
    kv_base = m.ctx_loads
    mask_base = m.mask_loads
    q = m.at
    with ExitStack() as ctx:
        def sb(name, shape, dt=F32):
            return ctx.enter_context(nc.sbuf_tensor(f"a{k}_{name}", shape, dt))

        Wq, Wk, Wv, Wo = (sb(n, [D, D]) for n in ("Wq", "Wk", "Wv", "Wo"))
        bq = sb("bq", [D, 1])
        bqs = sb("bqs", [D, 1])
        bk = sb("bk", [D, 1])
        bk_heads = sb("bk_heads", [D, hpg])
        bv = sb("bv", [D, D])
        bo = sb("bo", [D, D])
        y = sb("y", [S, 2, D])
        yT = sb("yT", [D, 2, S])
        cT = sb("cT", [D, 2, C])
        qT = sb("qT", [D, 2, S])
        kblk = sb("kblk", [D, 2, hpg * keys])
        vaug = sb("vaug", [keys, slots, heads * 32])
        mx = sb("mx", [S, 2, heads])
        T = sb("T", [S, 2, heads * keys])
        Pr = sb("Pr", [keys, 2, heads * S])
        oT = sb("oT", [D, 2, groups * S])
        rec = sb("rec", [S, 2, heads])
        O = sb("O", [S, 2, D])
        OT = sb("OT", [D, 2, S])
        if mask is not None:
            mk = sb("mk", [S, 2, C])
        if topk:
            r1 = sb("r1", [S, 2, heads * 8])
            r2 = sb("r2", [S, 2, heads * 8])
        if lowrank:
            U = sb("U", [D, 4, D])
            V = sb("V", [D, 4, D])
        if inner is not None:
            nw = sb("nw", [D, 1])
            nb = sb("nb", [D, 1])
            y0 = sb("y0", [S, 2, D])
            in_stats = sb("in_stats", [S, 2, 6])
            in_mv = sb("in_mv", [S, 2, 2])
            in_var = sb("in_var", [S, 2, 1])
            in_rstd = sb("in_rstd", [S, 2, 1])
            xw = sb("xw", [D, 2, S])
            tmp = sb("tmp", [S, 2, D])

        PS = m.PS
        yT_ps = PS[:, 5, 0:128]
        qT_ps = PS[:, 5, 128:256]
        OT_ps = PS[:, 5, 256:384]
        kT_ps = PS[:, 7, 0:keys] if k_ready == "k" else PS[:, 5, 384:384 + keys]
        v_ps = PS[0:keys, 7, 128:256]
        out_ps = PS[:, 7, 256:384]

        with nc.Block() as block:
            nload = [0]

            @block.sync
            def _(sp):
                def load(dst, src):
                    sp.dma_start(dst, src).then_inc(m.s_weights, 16)
                    nload[0] += 1
                if lowrank:
                    for n in range(4):
                        load(U[:, n, :], w.U[n])
                        load(V[:, n, :], w.V[n])
                else:
                    load(Wq[:, :], w.Wq)
                    load(Wk[:, :], w.Wk)
                    load(Wv[:, :], w.Wv)
                    load(Wo[:, :], w.Wo)
                load(bq[:, :], w.bq.unsqueeze(1))
                load(bk[:, :], w.bk.unsqueeze(1))
                load(bv[:, :], w.bv.partition_broadcast(D))
                load(bo[:, :], w.bo.partition_broadcast(D))
                if inner is not None:
                    load(nw[:, :], w.nw.unsqueeze(1))
                    load(nb[:, :], w.nb.unsqueeze(1))
            loaded = m.weight_loads + 16 * nload[0]

            @block.gpsimd
            def _(pool):
                norm_gpsimd(pool, m)

            @block.vector
            def _(dve):
                dve.memset(vaug[:, :, :], 0.0).then_inc(q["prep"], 1)
                norm_vector(dve, m)
                dve.wait_ge(m.s_weights, loaded)
                dve.wait_ge(q["prep"], m.preps + 1)
                dve.memset(vaug[:, :, :].rearrange("p u (h e) -> p (u h) e", e=32)[:, :, dh:dh + 1], 1.0)
                if inner is not None:
                    dve.tensor_tensor(bo[:, :], bo[:, :], m.WIDTH_TOKENS[:, :], ALU.mult)
                dve.tensor_scalar(bk_heads[:, :], m.HEAD[dh][:, :], bk[:, :], None, ALU.mult)
                dve.tensor_scalar(bqs[:, :], bq[:, :], scale, None, ALU.mult).then_inc(q["prep"], 1)
                if lowrank:
                    dve.wait_ge(q["fold"], 1)
                    for n, W in enumerate((Wq, Wk, Wv, Wo)):
                        last = dve.tensor_copy(W[:, :], PS[:, 0, n * D:(n + 1) * D])
                    last.then_inc(q["prep"], 1)

            @block.tensor
            def _(pe):
                if lowrank:
                    pe.wait_ge(m.s_weights, loaded)
                    for n in range(4):
                        last = pe.matmul(PS[:, 0, n * D:(n + 1) * D], U[:, n, :], V[:, n, :],
                                         start=True, stop=True)
                    last.then_inc(q["fold"], 1)
            m.weight_loads = loaded
            m.preps += 3 if lowrank else 2

        block = ctx.enter_context(nc.Block())

        @block.sync
        def _(sp):
            def step(i, v, h):
                u = v % 2
                if context is not None:
                    if past(i, 2):
                        sp.wait_ge(q["proj"], q.nth("proj", i, 2))
                    sp.dma_start(cT[:, u, :], context[:, bass.ds(i, 1), :].rearrange("p a c -> p (a c)")) \
                        .then_inc(q[f"ctx{u}"], 16)
                if mask is not None:
                    if past(i, 2):
                        sp.wait_ge(q["sfree1"], q.nth("sfree1", i, 2))
                    sp.dma_start(mk[:, u, :], mask[:, bass.ds(i, 1), :].rearrange("p a c -> p (a c)")) \
                        .then_inc(q[f"mask{u}"], 16)
            if context is not None:
                run_slots(sp, step, 0, 0, slots=slots)

        @block.tensor
        def _(pe):
            def scores(i, u, g):
                if g == 0:
                    pe.wait_ge(q["q"], q.nth("q", i))
                    pe.wait_ge(q[k_ready], q.nth(k_ready, i))
                if g % 2 == 0 and past(i, 1):
                    pe.wait_ge(q[f"{sfree}{g // 2}"], q.nth(f"{sfree}{g // 2}", i, 1))
                last = pe.matmul(PS[:, g, 0:hpg * keys], qT[32 * g:32 * g + 32, u, :],
                                 kblk[32 * g:32 * g + 32, u, :], start=True, stop=True,
                                 tile_position=(32 * g, 0))
                if g % 2 == 1:
                    last.then_inc(q[f"scores{g // 2}"], 1)

            def turn_y(i, u):
                pe.wait_ge(q["y"], q.nth("y", i))
                if past(i, lag + 3):
                    pe.wait_ge(q["OT"], q.nth("OT", i, lag + 3))
                pe.transpose(yT_ps, y[:, u, :], m.IDENT[:, :]).then_inc(q["yTps"], 1)

            def project(i, u, h):
                pe.wait_ge(q["yT"], q.nth("yT", i))
                if inner is not None:
                    pe.wait_ge(q["xT"], q.nth("xT", i))
                kv = yT
                if context is not None:
                    pe.wait_ge(q[f"ctx{u}"], h * 16 + (16 + kv_base))
                    kv = cT
                pe.matmul(qT_ps, Wq[:, :], yT[:, u, :], start=True, stop=True)
                if past(i, lag + 3):
                    pe.wait_ge(q["x"], q.nth("x", i, lag + 3))
                pe.matmul(kT_ps, Wk[:, :], kv[:, u, :], start=True, stop=True)
                pe.matmul(v_ps, kv[:, u, :], Wv[:, :], start=True, stop=True).then_inc(q["proj"], 1)

            def turn_scores(i, u, g):
                half = g // (groups // 2)
                if g in (0, groups // 2):
                    pe.wait_ge(q[f"{less_max}{half}"], q.nth(f"{less_max}{half}", i))
                if g == 0:
                    if past(i, 1):
                        pe.wait_ge(q[f"P{groups - 1}"], q.nth(f"P{groups - 1}", i, 1))
                else:
                    pe.wait_ge(q[f"P{g - 1}"], q.nth(f"P{g - 1}", i))
                for j in range(4):
                    c = (4 * g + j) * keys
                    last = pe.transpose(PS[0:keys, 4, j * S:(j + 1) * S], T[:, u, c:c + keys],
                                        m.IDENT[:, :])
                last.then_inc(q[f"PT{g}"], 1)

            def weigh_values(i, u, v):
                pe.wait_ge(q["v"], q.nth("v", i))
                if past(i, 1):
                    pe.wait_ge(q["O"], q.nth("O", i, 1))
                for g in range(groups):
                    pe.wait_ge(q[f"P{g}"], q.nth(f"P{g}", i))
                    for j in range(4):
                        c = 4 * g + j
                        last = pe.matmul(PS[32 * j:32 * j + 32, 6, g * S:(g + 1) * S],
                                         vaug[:, v, c * 32:c * 32 + 32],
                                         Pr[:, u, c * S:(c + 1) * S], start=True, stop=True,
                                         tile_position=(0, 32 * j))
                last.then_inc(q["pv"], 1)

            def turn_back(i, u):
                pe.wait_ge(q["oT"], q.nth("oT", i))
                for g in range(groups):
                    last = pe.transpose(PS[:, 6, g * S:(g + 1) * S], oT[:, u, g * S:(g + 1) * S],
                                        m.IDENT[:, :])
                last.then_inc(q["back"], 1)

            def turn_out(i, u):
                pe.wait_ge(q["O"], q.nth("O", i))
                if k_ready != "k":
                    pe.wait_ge(q[k_ready], q.nth(k_ready, i, -(lag + 2)))
                pe.wait_ge(q["q"], q.nth("q", i, -(lag + 2)))
                pe.transpose(OT_ps, O[:, u, :], m.IDENT[:, :]).then_inc(q["OTps"], 1)

            def project_out(i, u):
                pe.wait_ge(q["OT"], q.nth("OT", i))
                pe.wait_ge(q[k_ready], q.nth(k_ready, i, -(lag + 2)))
                pe.wait_ge(q["v"], q.nth("v", i, -(lag + 2)))
                pe.matmul(out_ps, OT[:, u, :], Wo[:, :], start=True, stop=True).then_inc(q["out"], 1)

            def step(s, v, h):
                u, a = v % 2, (v + 1) % 2
                use, end = s - lag, s - lag - 1
                for g in range(4):
                    if real(s):
                        scores(s, u, g)
                    if real(end) and g == 2:
                        turn_out(end, (v - lag - 1) % 2)
                    if real(end) and g == 3:
                        project_out(end, (v - lag - 1) % 2)
                    if real(use) and g < groups:
                        turn_scores(use, (v - lag) % 2, g)
                    if real(s + 1) and g == 0:
                        turn_y(s + 1, a)
                    if real(end) and g == 0:
                        turn_back(end, (v - lag - 1) % 2)
                    if real(s + 1) and g == 1:
                        project(s + 1, a, h + (v + 1) // 2 - v // 2)
                if real(use):
                    weigh_values(use, (v - lag) % 2, (v - lag) % slots)
            run_slots(pe, step, 1, lag + 1, slots=slots)

        @block.scalar
        def _(act):
            act.activation(m.scratch[:, 0:1], m.scratch[:, 1:2], ACT.Exp)

            def copy_pv(i, u):
                act.wait_ge(q["pv"], q.nth("pv", i))
                if past(i, 2):
                    act.wait_ge(q["back"], q.nth("back", i, 2))
                act.activation(oT[:, u, :], PS[:, 6, 0:groups * S], ACT.Copy).then_inc(q["oT"], 1)

            def copy_yT(i, u):
                act.wait_ge(q["yTps"], q.nth("yTps", i))
                if inner is not None:
                    if past(i, 2):
                        act.wait_ge(q["xT"], q.nth("xT", i, 2))
                    act.activation(xw[:, u, :], yT_ps, ACT.Identity, bias=nb[:, :], scale=nw[:, :]) \
                        .then_inc(q["yT"], 1)
                else:
                    if past(i, 2):
                        act.wait_ge(q["proj"], q.nth("proj", i, 2))
                    act.activation(yT[:, u, :], yT_ps, ACT.Copy).then_inc(q["yT"], 1)

            def probabilities(i, u, g):
                act.wait_ge(q[f"PT{g}"], q.nth(f"PT{g}", i))
                if past(i, 2):
                    act.wait_ge(q["pv"], q.nth("pv", i, 2))
                part = Pr[:, u, g * BANK:(g + 1) * BANK]
                if topk:
                    act.activation(part, PS[0:keys, 4, :], ACT.Abs).then_inc(q[f"abs{g}"], 1)
                    act.wait_ge(q[f"abs{g}"], q.nth(f"abs{g}", i))
                    act.activation(part, part, ACT.Exp, scale=-1.0).then_inc(q[f"P{g}"], 1)
                else:
                    act.activation(part, PS[0:keys, 4, :], ACT.Exp).then_inc(q[f"P{g}"], 1)

            def copy_q(i, u):
                act.wait_ge(q["proj"], q.nth("proj", i))
                if past(i, 2):
                    act.wait_ge(q["scores1"], q.nth("scores1", i, 2))
                act.activation(qT[:, u, :], qT_ps, ACT.Identity, bias=bqs[:, :], scale=scale) \
                    .then_inc(q["q"], 1)

            def spread_k(i, u):
                for j in range(hpg):
                    last = act.activation(kblk[:, u, j * keys:(j + 1) * keys], kT_ps, ACT.Identity,
                                          bias=bk_heads[:, j:j + 1], scale=m.HEAD[dh][:, j:j + 1])
                last.then_inc(q["k_by_scalar"], 1)

            def copy_scores(i, u, half):
                banks = slice(2 * half, 2 * half + 2)
                t4 = T[:, u, :].rearrange("p (g c) -> p g c", g=4)[:, banks, :]
                act.wait_ge(q[f"scores{half}"], q.nth(f"scores{half}", i))
                if past(i, 2):
                    turned = f"PT{groups // 2 * (half + 1) - 1}"
                    act.wait_ge(q[turned], q.nth(turned, i, 2))
                act.activation(t4, PS[:, banks, 0:hpg * keys], ACT.Copy).then_inc(q[f"copied{half}"], 1)

            def copy_OT(i, u):
                act.wait_ge(q["OTps"], q.nth("OTps", i))
                if past(i, 2):
                    act.wait_ge(q["out"], q.nth("out", i, 2))
                act.activation(OT[:, u, :], OT_ps, ACT.Copy).then_inc(q["OT"], 1)

            def step(s, v, h):
                a = (v + 1) % 2
                use, end = s - lag, s - lag - 1
                if real(end):
                    copy_pv(end, (v - lag - 1) % 2)
                for g in range(4):
                    if real(use) and g < groups:
                        probabilities(use, (v - lag) % 2, g)
                    if real(s + 1) and g == 0:
                        copy_yT(s + 1, a)
                    if real(s + 1) and g == 1:
                        copy_q(s + 1, a)
                        if k_ready == "k_by_scalar":
                            spread_k(s + 1, a)
                    if real(end) and g == 1:
                        copy_OT(end, (v - lag - 1) % 2)
                    if topk and real(s) and g % 2 == 1:
                        copy_scores(s, v % 2, g // 2)
            run_slots(act, step, 1, lag + 1, slots=slots)

        @block.gpsimd
        def _(pool):
            norm_gpsimd_rest(pool, m)

            def add_bias(i, u):
                pool.wait_ge(q["y"], q.nth("y", i))
                xi = m.X[:, bass.ds(i, 1), :].rearrange("p a d -> p (a d)")
                if inner is None:
                    pool.tensor_tensor(xi, xi, bo[:, :], ALU.add).then_inc(q["bias"], 1)
                else:
                    pool.tensor_tensor(y0[:, u, :], y0[:, u, :], bo[:, :], ALU.add).then_inc(q["y0"], 1)
                    pool.wait_ge(q["y0"], q.nth("y0", i))
                    pool.tensor_tensor(xi, xi, y0[:, u, :], ALU.add).then_inc(q["bias"], 1)

            def distances(i, u, half):
                t3 = T[:, u, :].rearrange("p (k h c) -> p k h c", k=2, c=keys)[:, half, :, :]
                m3 = mx[:, u, :].rearrange("p (k h) -> p k h", k=2)[:, half, :]
                pool.wait_ge(q[f"mx{half}"], q.nth(f"mx{half}", i))
                pool.tensor_tensor(t3, bcast(m3, 2, keys), t3, ALU.subtract).then_inc(q[f"distance{half}"], 1)

            def step(s, v, h):
                u, a = v % 2, (v + 1) % 2
                if inner is not None and real(s + 1):
                    pool.wait_ge(q["yT"], q.nth("yT", s + 1))
                    if past(s + 1, 2):
                        pool.wait_ge(q["proj"], q.nth("proj", s + 1, 2))
                    pool.tensor_tensor(yT[:, a, :], xw[:, a, :], m.WIDTH_FEATURES[:, :], ALU.mult) \
                        .then_inc(q["xT"], 1)
                if real(s):
                    if topk:
                        for half in range(2):
                            distances(s, u, half)
                    add_bias(s, u)
                if inner is not None and real(s + 2):
                    pool.wait_ge(q["ivar"], q.nth("ivar", s + 2))
                    pool.tensor_tensor(in_rstd[:, u, :], in_var[:, u, :], m.MINUS_HALF[:, 0:1], ALU.pow) \
                        .then_inc(q["irstd"], 1)
            run_slots(pool, step, 2, 0, slots=slots)

        @block.vector
        def _(dve):
            def pass_wait():
                dve.sem_inc(q["passed"], 1)

            def normalise(i, u):
                xi = m.X[:, bass.ds(i, 1), :].rearrange("p a d -> p (a d)")
                mean, rstd = m.MEAN[:, bass.ds(i, 1)], m.RSTD[:, bass.ds(i, 1)]
                if not isinstance(i, int):
                    dve.wait_ge(m.s_norm_b, 2 * m.norms + 2)
                if inner is None:
                    if past(i, 2):
                        dve.wait_ge(q["yTps"], q.nth("yTps", i, 2))
                    dve.tensor_scalar(y[:, u, :], xi, mean, rstd, ALU.subtract, ALU.mult).then_inc(q["y"], 1)
                    return
                if past(i, 2):
                    dve.wait_ge(q["bias"], q.nth("bias", i, 2))
                dve.tensor_scalar(y0[:, u, :], xi, mean, rstd, ALU.subtract, ALU.mult).then_inc(q["yraw"], 1)
                dve.wait_ge(q["yraw"], q.nth("yraw", i))
                dve.bn_stats(in_stats[:, u, :], y0[:, u, :]).then_inc(q["istat"], 1)
                dve.wait_ge(q["istat"], q.nth("istat", i))
                pass_wait()
                dve.bn_aggr(in_mv[:, u, :], in_stats[:, u, :]).then_inc(q["imv"], 1)
                dve.wait_ge(q["imv"], q.nth("imv", i))
                dve.tensor_scalar(in_var[:, u, :], in_mv[:, u, 1:2], EPS, None, ALU.add).then_inc(q["ivar"], 1)

            def normalise_inner(i, u):
                dve.wait_ge(q["irstd"], q.nth("irstd", i))
                if past(i, 2):
                    dve.wait_ge(q["yTps"], q.nth("yTps", i, 2))
                dve.tensor_scalar(y[:, u, :], y0[:, u, :], in_mv[:, u, 0:1], in_rstd[:, u, :],
                                  ALU.subtract, ALU.mult).then_inc(q["y"], 1)

            def norm_heads(i, u):
                pv = PS[:, 6, 0:groups * S].rearrange("p (h e) -> p h e", e=32)
                dve.wait_ge(q["back"], q.nth("back", i))
                dve.reciprocal(rec[:, u, :], pv[:, :, dh:dh + 1].rearrange("p h e -> p (h e)")) \
                    .then_inc(q["rec"], 1)
                dve.wait_ge(q["rec"], q.nth("rec", i))
                if past(i, 2):
                    dve.wait_ge(q["OTps"], q.nth("OTps", i, 2))
                last = dve.tensor_tensor(O[:, u, :].rearrange("p (h e) -> p h e", e=dh), pv[:, :, 0:dh],
                                         bcast(rec[:, u, :], 2, dh), ALU.mult)
                if inner is not None:
                    last.then_inc(q["Oall"], 1)
                    dve.wait_ge(q["Oall"], q.nth("Oall", i))
                    last = dve.tensor_tensor(O[:, u, :], O[:, u, :], m.WIDTH_TOKENS[:, :], ALU.mult)
                last.then_inc(q["O"], 1)

            def subtract_max(i, u, h, half):
                banks = slice(2 * half, 2 * half + 2)
                raw = PS[:, banks, 0:hpg * keys].rearrange("p g (a c) -> p g a c", c=keys)
                t4 = T[:, u, :].rearrange("p (g a c) -> p g a c", a=hpg, c=keys)[:, banks, :, :]
                t3 = T[:, u, :].rearrange("p (k h c) -> p k h c", k=2, c=keys)[:, half, :, :]
                m4 = mx[:, u, :].rearrange("p (g a) -> p g a", a=hpg)[:, banks, :]
                m3 = mx[:, u, :].rearrange("p (k h) -> p k h", k=2)[:, half, :]
                if topk:
                    dve.wait_ge(q[f"copied{half}"], q.nth(f"copied{half}", i))
                    if past(i, 2):
                        dve.wait_ge(q[f"distance{half}"], q.nth(f"distance{half}", i, 2))
                    dve.tensor_reduce(m3, t3, AX, ALU.max).then_inc(q[f"mx{half}"], 1)
                    return
                dve.wait_ge(q[f"scores{half}"], q.nth(f"scores{half}", i))
                if past(i, 2):
                    turned = f"PT{groups // 2 * (half + 1) - 1}"
                    dve.wait_ge(q[turned], q.nth(turned, i, 2))
                if mask is not None:
                    dve.wait_ge(q[f"mask{u}"], h * 16 + (16 + mask_base))
                    for g in range(2):
                        last = dve.scalar_tensor_tensor(
                            out=t4[:, g, :, :], in0=bcast(mk[:, u, :], 1, hpg), scalar=-1.0e9,
                            in1=raw[:, g, :, :], op0=ALU.mult, op1=ALU.add)
                    last.then_inc(q[f"sfree{half}"], 1)
                    dve.wait_ge(q[f"sfree{half}"], q.nth(f"sfree{half}", i))
                    dve.tensor_reduce(m3, t3, AX, ALU.max).then_inc(q[f"mx{half}"], 1)
                    dve.wait_ge(q[f"mx{half}"], q.nth(f"mx{half}", i))
                    dve.tensor_tensor(t3, t3, bcast(m3, 2, keys), ALU.subtract).then_inc(q[f"T{half}"], 1)
                    return
                dve.tensor_reduce(m4, raw, AX, ALU.max).then_inc(q[f"mx{half}"], 1)
                dve.wait_ge(q[f"mx{half}"], q.nth(f"mx{half}", i))
                dve.tensor_tensor(t4, raw, bcast(m4, 3, keys), ALU.subtract).then_inc(q[f"sfree{half}"], 1)

            def drop_eight(i, u):
                t3 = T[:, u, :].rearrange("p (h c) -> p h c", c=keys)
                for h in range(heads):
                    if h % (heads // 2) == 0:
                        half = h // (heads // 2)
                        dve.wait_ge(q[f"distance{half}"], q.nth(f"distance{half}", i))
                        pass_wait()
                    last = dve.max(r1[:, u, 8 * h:8 * h + 8], t3[:, h, :])
                last.then_inc(q["r1"], 1)
                dve.wait_ge(q["r1"], q.nth("r1", i))
                pass_wait()
                for h in range(heads):
                    last = dve.match_replace(t3[:, h, :], r1[:, u, 8 * h:8 * h + 8], t3[:, h, :], FAR)
                last.then_inc(q["t1"], 1)

            def drop_rest(i, u):
                t3 = T[:, u, :].rearrange("p (h c) -> p h c", c=keys)
                rest = keys - topk - 8
                dve.wait_ge(q["t1"], q.nth("t1", i))
                pass_wait()
                for h in range(heads):
                    last = dve.max(r2[:, u, 8 * h:8 * h + 8], t3[:, h, :])
                last.then_inc(q["r2"], 1)
                dve.wait_ge(q["r2"], q.nth("r2", i))
                dve.memset(r2[:, u, :].rearrange("p (h e) -> p h e", e=8)[:, :, rest:8], FAR) \
                    .then_inc(q["r2cut"], 1)
                dve.wait_ge(q["r2cut"], q.nth("r2cut", i))
                pass_wait()
                for h in range(heads):
                    last = dve.match_replace(t3[:, h, :], r2[:, u, 8 * h:8 * h + 8], t3[:, h, :], FAR)
                    if h == heads // 2 - 1:
                        last.then_inc(q["T0"], 1)
                last.then_inc(q["T1"], 1)

            def spread_k(i, u):
                dve.wait_ge(q["proj"], q.nth("proj", i))
                if past(i, 2):
                    dve.wait_ge(q["scores1"], q.nth("scores1", i, 2))
                dve.scalar_tensor_tensor(
                    out=kblk[:, u, :].rearrange("p (a c) -> p a c", c=keys),
                    in0=bcast(kT_ps, 1, hpg), scalar=bk[:, :],
                    in1=bcast(m.HEAD[dh][:, :], 2, keys), op0=ALU.add, op1=ALU.mult).then_inc(q["k"], 1)

            def place_v(i, v):
                if past(i, slots):
                    dve.wait_ge(q["pv"], q.nth("pv", i, slots))
                if k_ready != "k":
                    dve.wait_ge(q["proj"], q.nth("proj", i))
                dve.tensor_tensor(vaug[:, v, :].rearrange("p (h e) -> p h e", e=32)[:, :, 0:dh],
                                  v_ps.rearrange("p (h e) -> p h e", e=dh),
                                  bv[0:keys, :].rearrange("p (h e) -> p h e", e=dh), ALU.add) \
                    .then_inc(q["v"], 1)

            def residual(i, u):
                xi = m.X[:, bass.ds(i, 1), :].rearrange("p a d -> p (a d)")
                dve.wait_ge(q["out"], q.nth("out", i))
                dve.wait_ge(q["bias"], q.nth("bias", i))
                if inner is None:
                    dve.tensor_tensor(xi, out_ps, xi, ALU.add).then_inc(q["x"], 1)
                else:
                    dve.tensor_tensor(tmp[:, u, :], out_ps, m.WIDTH_TOKENS[:, :], ALU.mult) \
                        .then_inc(q["tmp"], 1)
                    dve.wait_ge(q["tmp"], q.nth("tmp", i))
                    dve.tensor_tensor(xi, tmp[:, u, :], xi, ALU.add).then_inc(q["x"], 1)
                dve.wait_ge(q["x"], q.nth("x", i))
                dve.bn_stats(m.STATS[:, bass.ds(i, 1), :].rearrange("p a d -> p (a d)"), xi)

            def step(s, v, h):
                u, a = v % 2, (v + 1) % 2
                end = s - lag - 1
                if topk and real(s - 1):
                    drop_eight(s - 1, a)
                if real(end):
                    norm_heads(end, (v - lag - 1) % 2)
                if not topk and real(s):
                    subtract_max(s, u, h, 0)
                if real(s + 1):
                    if k_ready == "k":
                        spread_k(s + 1, a)
                    place_v(s + 1, (v + 1) % slots)
                if inner is not None and real(s + 2):
                    normalise(s + 2, u)
                if topk and real(s - 1):
                    drop_rest(s - 1, a)
                if topk and real(s):
                    subtract_max(s, u, h, 0)
                if real(s):
                    subtract_max(s, u, h, 1)
                if real(end):
                    residual(end, (v - lag - 1) % 2)
                if inner is None and real(s + 2):
                    normalise(s + 2, u)
                if inner is not None and real(s + 2):
                    normalise_inner(s + 2, u)
            run_slots(dve, step, 2, lag + 1, slots=slots)

        used = ["y", "yTps", "yT", "proj", "q", k_ready, "v", "scores0", "scores1", f"{sfree}0", f"{sfree}1", "mx0", "mx1", "pv", "oT", "back",
                "rec", "O", "OTps", "OT", "out", "bias", "x"]
        used += [f"{n}{g}" for n in ("PT", "P") for g in range(groups)]
        used += ["distance0", "distance1"] if topk else []
        used += ["T0", "T1"] if less_max == "T" else []
        used += ["xT"] if inner is not None else []
        for n in used:
            q.done[n] += B
        if context is not None:
            m.ctx_loads += 16 * (B // 2)
        if mask is not None:
            m.mask_loads += 16 * (B // 2)


def seq(tensor, i):
    return tensor[:, bass.ds(i, 1), :].rearrange("p a d -> p (a d)")


def layer0_cross(nc, m, t):
    n = "L0_xattn_"
    CH = 4
    NCH = -(-C // CH)
    CP = NCH * CH
    PARTS = [(0, 16), (16, 32), (60, C), (32, 60)]
    POOL_PART = 3
    with ExitStack() as ctx:
        def sb(name, shape, dt=F32):
            return ctx.enter_context(nc.sbuf_tensor(f"l0_{name}", shape, dt))

        Ws, W = sb("Ws", [D, D]), sb("W", [D, D])
        bvec, wvec = sb("b", [D, 1]), sb("w", [D, 1])
        wc = sb("wc", [D, 2])
        wc_wide = sb("wc_wide", [D, 2, S])
        wide = sb("wide", [D, 64])
        bc = sb("bc", [S, 2])
        ctxT = sb("ctxT", [D, B, C])
        y = sb("y", [S, 2, D])
        yT = sb("yT", [D, 2, S])
        feat = sb("feat", [D, 2, S])
        text = sb("text", [D, 2, C])
        H = sb("H", [D, 2, C * S])
        qm = sb("qm", [S, 2, C], I32)
        neg = sb("neg", [S, 2, CP])
        rhoT = sb("rhoT", [S, 2, BANK])
        rho = sb("rho", [S, 2, CP])
        nmx = sb("nmx", [S, 2, 1])
        e = sb("e", [S, 2, CP])
        esum = sb("esum", [S, 2, 1])
        rec = sb("rec", [S, 2, 1])
        junk = sb("junk", [S, 2, 2 * C])
        acc = sb("acc", [S, 2, 2])
        z = sb("z", [S, 2, 2])
        gate = sb("gate", [S, 2, 2])
        y2 = sb("y2", [S, 2, D])
        q = Signals(ctx, nc, "l0", [
            "prep", "y", "yTps", "yT", "proj", "projd", "text", "sum0", "sum1", "sum2", "sum3", "tanh0", "tanh1",
            "tanh2", "tanh3", "used0", "used1", "used2", "used3", "rhoT", "turned", "masked", "nmx", "e", "rec", "acc", "z", "gate", "y2",
            "part", "x", "cw", "neg", "qm0", "qm1", "passed"])
        PS = m.PS
        yT_ps, feat_ps, text_ps = PS[:, 0, 0:128], PS[:, 0, 128:256], PS[:, 0, 256:256 + C]
        cw_ps = PS[:, 3, 0:2 * C]

        with nc.Block() as block:
            loads = [(Ws[:, :], t[n + "Ws"]), (W[:, :], t[n + "W"]), (bvec[:, :], t[n + "b"].rearrange("a d -> d a")),
                     (wvec[:, :], t[n + "w"]), (wc[:, 0:1], t[n + "Wcw"].rearrange("a d -> d a")),
                     (wc[:, 1:2], t[n + "Wcb"].rearrange("a d -> d a")),
                     (bc[:, 0:1], t[n + "bcw"].partition_broadcast(S)),
                     (bc[:, 1:2], t[n + "bcb"].partition_broadcast(S)), (ctxT[:, :, :], t["ctxT"])]

            @block.sync
            def _(sp):
                for dst, src in loads:
                    sp.dma_start(dst, src).then_inc(m.s_weights, 16)
            m.weight_loads += 16 * len(loads)

            @block.gpsimd
            def _(pool):
                norm_gpsimd(pool, m)

            @block.vector
            def _(dve):
                dve.memset(wide[:, :], 0.0)
                dve.memset(neg[:, :, C:CP], FAR)
                dve.memset(e[:, :, :], 0.0).then_inc(q["prep"], 1)
                norm_vector(dve, m)
                dve.wait_ge(m.s_weights, m.weight_loads)
                dve.wait_ge(q["prep"], 1)
                dve.tensor_copy(wide[:, 32:33], wvec[:, :])
                dve.tensor_copy(wc_wide[:, :, :], bcast(wc[:, :], 2, S))

        block = ctx.enter_context(nc.Block())

        @block.sync
        def _(sp):
            def step(i, u, h):
                if past(i, 2):
                    sp.wait_ge(q["neg"], q.nth("neg", i, 2))
                sp.dma_start(qm[:, u, :], t["q_masks"][bass.ds(i, 1), :].rearrange("a c -> (a c)")
                             .partition_broadcast(S)).then_inc(q[f"qm{u}"], 16)
            run_slots(sp, step, 0, 0)

        @block.tensor
        def _(pe):
            def turn_y(i, u):
                pe.wait_ge(q["y"], q.nth("y", i))
                if past(i, 1):
                    pe.wait_ge(q["text"], q.nth("text", i, 1))
                pe.transpose(yT_ps, y[:, u, :], m.IDENT[:, :]).then_inc(q["yTps"], 1)

            def project(i, u):
                pe.wait_ge(q["yT"], q.nth("yT", i))
                pe.matmul(feat_ps, W[:, :], yT[:, u, :], start=True, stop=True)
                pe.matmul(text_ps, Ws[:, :], seq(ctxT, i), start=True, stop=True).then_inc(q["proj"], 1)
                if past(i, 2):
                    pe.wait_ge(q["sum2"], q.nth("sum2", i, 2))
                pe.matmul(PS[:, 1 + u, 0:S], W[:, :], yT[:, u, :], start=True, stop=True).then_inc(q["projd"], 1)

            def sum_rho(i, u, part):
                lo, hi = PARTS[part]
                pe.wait_ge(q[f"tanh{part}"], q.nth(f"tanh{part}", i))
                if part == 0:
                    if past(i, 2):
                        pe.wait_ge(q["rhoT"], q.nth("rhoT", i, 2))
                for c in range(lo // CH, -(-hi // CH)):
                    j, r = c % 4, c // 4
                    cols = (min(C, CH * (c + 1)) - CH * c) * S
                    last = pe.matmul(PS[32 * j:32 * j + 32, 4 + u, 0:cols], wide[:, 32 - r:64 - r],
                                     H[:, u, CH * c * S:CH * c * S + cols], start=(r == 0),
                                     stop=(part == POOL_PART and c >= hi // CH - 4), tile_position=(0, 32 * j),
                                     skip_group_check=True)
                last.then_inc(q[f"used{part}"], 1)

            def turn_rho(i, u):
                pe.wait_ge(q["rhoT"], q.nth("rhoT", i))
                if past(i, 1):
                    pe.wait_ge(q["masked"], q.nth("masked", i, 1))
                for k in range(CH):
                    last = pe.transpose(PS[:, 6, k * S:(k + 1) * S], rhoT[:, u, k * S:(k + 1) * S], m.IDENT[:, :])
                last.then_inc(q["turned"], 1)
                if past(i, 1):
                    pe.wait_ge(q["z"], q.nth("z", i, 1))
                for k in range(2):
                    last = pe.matmul(cw_ps[:, k * C:(k + 1) * C], wc_wide[:, k, :], seq(ctxT, i),
                                     start=True, stop=True)
                last.then_inc(q["cw"], 1)

            def step(s, u, h):
                a = (u + 1) % 2
                if real(s + 2):
                    turn_y(s + 2, u)
                if real(s):
                    sum_rho(s, u, 0)
                    sum_rho(s, u, 1)
                if real(s - 1):
                    turn_rho(s - 1, a)
                if real(s + 2):
                    project(s + 2, u)
                if real(s):
                    sum_rho(s, u, 2)
                    sum_rho(s, u, 3)
            run_slots(pe, step, 2, 1)

        @block.scalar
        def _(act):
            act.activation(m.scratch[:, 0:1], m.scratch[:, 1:2], ACT.Exp)

            def tanh(i, u, part):
                lo, hi = PARTS[part]
                act.wait_ge(q[f"sum{part}"], q.nth(f"sum{part}", i))
                cells = H[:, u, lo * S:hi * S]
                act.activation(cells, cells, ACT.Tanh).then_inc(q[f"tanh{part}"], 1)

            def step(s, u, h):
                a = (u + 1) % 2
                if real(s):
                    tanh(s, u, 0)
                    tanh(s, u, 1)
                if real(s - 1):
                    act.wait_ge(q["used3"], q.nth("used3", s - 1))
                    if past(s - 1, 2):
                        act.wait_ge(q["turned"], q.nth("turned", s - 1, 2))
                    act.activation(rhoT[:, a, :], PS[:, 4 + a, :], ACT.Copy).then_inc(q["rhoT"], 1)
                if real(s + 2):
                    act.wait_ge(q["yTps"], q.nth("yTps", s + 2))
                    if past(s + 2, 2):
                        act.wait_ge(q["projd"], q.nth("projd", s + 2, 2))
                    act.activation(yT[:, u, :], yT_ps, ACT.Copy).then_inc(q["yT"], 1)
                if real(s):
                    tanh(s, u, 2)
                if real(s - 2):
                    act.wait_ge(q["z"], q.nth("z", s - 2))
                    if past(s - 2, 2):
                        act.wait_ge(q["x"], q.nth("x", s - 2, 2))
                    act.activation(gate[:, u, :], z[:, u, :], ACT.Tanh).then_inc(q["gate"], 1)
                if real(s):
                    tanh(s, u, 3)
                if real(s + 2):
                    act.wait_ge(q["proj"], q.nth("proj", s + 2))
                    if past(s + 2, 2):
                        act.wait_ge(q[f"sum{POOL_PART}"], q.nth(f"sum{POOL_PART}", s + 2, 2))
                        act.wait_ge(q["sum2"], q.nth("sum2", s + 2, 2))
                    act.activation(feat[:, u, :], feat_ps, ACT.Copy)
                    act.activation(text[:, u, :], text_ps, ACT.Identity, bias=bvec[:, :]).then_inc(q["text"], 1)
                if real(s - 1):
                    act.wait_ge(q["nmx"], q.nth("nmx", s - 1))
                    if past(s - 1, 2):
                        act.wait_ge(q["acc"], q.nth("acc", s - 1, 2))
                    act.activation(e[:, a, :], rho[:, a, :], ACT.Exp, bias=nmx[:, a, :],
                                   accum_out=esum[:, a, :]).then_inc(q["e"], 1)
            run_slots(act, step, 2, 2)

        @block.gpsimd
        def _(pool):
            norm_gpsimd_rest(pool, m)

            def step(s, u, h):
                a = (u + 1) % 2
                if real(s + 1):
                    lo, hi = PARTS[POOL_PART]
                    pool.wait_ge(q["text"], q.nth("text", s + 1))
                    if past(s + 1, 2):
                        pool.wait_ge(q["used3"], q.nth("used3", s + 1, 2))
                    pool.tensor_tensor(H[:, a, lo * S:hi * S].rearrange("p (t f) -> p t f", f=S),
                                       bcast(feat[:, a, :], 1, hi - lo), bcast(text[:, a, lo:hi], 2, S), ALU.add) \
                        .then_inc(q[f"sum{POOL_PART}"], 1)
                if real(s):
                    pool.wait_ge(q[f"qm{u}"], h * 16 + 16)
                    if past(s, 2):
                        pool.wait_ge(q["masked"], q.nth("masked", s, 2))
                    pool.sem_inc(q["passed"], 1)
                    pool.tensor_scalar(neg[:, u, 0:C], qm[:, u, :], -1.0, 1.0e30, ALU.add, ALU.mult) \
                        .then_inc(q["neg"], 1)
            run_slots(pool, step, 1, 0)

        @block.vector
        def _(dve):
            def add_part(i, u, part):
                lo, hi = PARTS[part]
                if part == 0:
                    dve.wait_ge(q["text"], q.nth("text", i))
                    dve.wait_ge(q["projd"], q.nth("projd", i))
                if past(i, 2):
                    dve.wait_ge(q[f"used{part}"], q.nth(f"used{part}", i, 2))
                dve.tensor_tensor(H[:, u, lo * S:hi * S].rearrange("p (t f) -> p t f", f=S),
                                  bcast(PS[:, 1 + u, 0:S], 1, hi - lo), bcast(text[:, u, lo:hi], 2, S), ALU.add) \
                    .then_inc(q[f"sum{part}"], 1)

            def mask_rho(i, u):
                dve.wait_ge(q["turned"], q.nth("turned", i))
                dve.wait_ge(q["neg"], q.nth("neg", i))
                if past(i, 2):
                    dve.wait_ge(q["e"], q.nth("e", i, 2))
                turned = PS[:, 6, :].rearrange("p (k j r) -> p r j k", k=4, j=4)[:, 0:NCH // 4, :, :]
                dve.tensor_tensor(rho[:, u, :].rearrange("p (r j k) -> p r j k", j=4, k=4), turned,
                                  neg[:, u, :].rearrange("p (r j k) -> p r j k", j=4, k=4), ALU.add) \
                    .then_inc(q["masked"], 1)
                dve.wait_ge(q["masked"], q.nth("masked", i))
                dve.tensor_reduce(nmx[:, u, :], rho[:, u, :], AX, ALU.max, negate=True).then_inc(q["nmx"], 1)

            def attend(i, u):
                dve.wait_ge(q["e"], q.nth("e", i))
                dve.wait_ge(q["cw"], q.nth("cw", i))
                dve.reciprocal(rec[:, u, :], esum[:, u, :]).then_inc(q["rec"], 1)
                for k in range(2):
                    last = dve.scalar_tensor_tensor(
                        out=junk[:, u, k * C:(k + 1) * C], in0=e[:, u, 0:C], scalar=1.0,
                        in1=cw_ps[:, k * C:(k + 1) * C], op0=ALU.mult, op1=ALU.mult,
                        accum_out=acc[:, u, k:k + 1])
                last.then_inc(q["acc"], 1)
                dve.wait_ge(q["acc"], q.nth("acc", i))
                dve.wait_ge(q["rec"], q.nth("rec", i))
                if past(i, 2):
                    dve.wait_ge(q["gate"], q.nth("gate", i, 2))
                dve.scalar_tensor_tensor(out=z[:, u, :], in0=acc[:, u, :], scalar=rec[:, u, :], in1=bc[:, :],
                                         op0=ALU.mult, op1=ALU.add).then_inc(q["z"], 1)

            def update(i, u):
                dve.tensor_scalar(y2[:, u, :], seq(m.X, i), m.MEAN[:, bass.ds(i, 1)], m.RSTD[:, bass.ds(i, 1)],
                                  ALU.subtract, ALU.mult).then_inc(q["y2"], 1)
                dve.wait_ge(q["y2"], q.nth("y2", i))
                dve.wait_ge(q["gate"], q.nth("gate", i))
                dve.scalar_tensor_tensor(out=y2[:, u, :], in0=y2[:, u, :], scalar=gate[:, u, 0:1], in1=seq(m.X, i),
                                         op0=ALU.mult, op1=ALU.add).then_inc(q["part"], 1)
                dve.wait_ge(q["part"], q.nth("part", i))
                dve.tensor_scalar(seq(m.X, i), y2[:, u, :], gate[:, u, 1:2], None, ALU.add).then_inc(q["x"], 1)
                dve.wait_ge(q["x"], q.nth("x", i))
                dve.bn_stats(seq(m.STATS, i), seq(m.X, i))

            def step(s, u, h):
                a = (u + 1) % 2
                if real(s + 1):
                    add_part(s + 1, a, 0)
                if real(s - 2):
                    attend(s - 2, u)
                if real(s + 1):
                    add_part(s + 1, a, 1)
                if real(s - 1):
                    mask_rho(s - 1, a)
                if real(s + 1):
                    add_part(s + 1, a, 2)
                if real(s - 2):
                    update(s - 2, u)
                if real(s + 3):
                    if past(s + 3, 2):
                        dve.wait_ge(q["yTps"], q.nth("yTps", s + 3, 2))
                    if not isinstance(s, int):
                        dve.wait_ge(m.s_norm_b, 2 * m.norms + 2)
                    dve.tensor_scalar(y[:, a, :], seq(m.X, s + 3), m.MEAN[:, bass.ds(s + 3, 1)],
                                      m.RSTD[:, bass.ds(s + 3, 1)], ALU.subtract, ALU.mult).then_inc(q["y"], 1)
            run_slots(dve, step, 3, 2)


G = 4
NG = B // G
N = G * S
ROWS = 72
PAD = 8


def group(tensor, i):
    return tensor[:, bass.ds(i * G, G), :]


def normalise_group(dve, m, q, y, i, u):
    if past(i, 2):
        dve.wait_ge(q["yTps"], q.nth("yTps", i, 2))
    if not isinstance(i, int) or i * G >= FIRST:
        dve.wait_ge(m.s_norm_b, 2 * m.norms + 2)
    x = group(m.X, i)
    mean = bcast(m.MEAN[:, bass.ds(i * G, G)], 2, D)
    rstd = bcast(m.RSTD[:, bass.ds(i * G, G)], 2, D)
    y3 = y[:, u, :].rearrange("p (g d) -> p g d", d=D)
    dve.tensor_tensor(y3, x, mean, ALU.subtract).then_inc(q["centred"], 1)
    dve.wait_ge(q["centred"], q.nth("centred", i))
    dve.tensor_tensor(y3, y3, rstd, ALU.mult).then_inc(q["y"], 1)


def group_statistics(dve, m, i):
    for g in range(G):
        dve.bn_stats(seq(m.STATS, i * G + g), seq(m.X, i * G + g))


def route_logits(dve, q, r, logits, E, i, u):
    dve.wait_ge(q["logits"], q.nth("logits", i))
    dve.tensor_reduce(r.mx[:, u, :], logits, AX, ALU.max).then_inc(q["lmax"], 1)
    dve.wait_ge(q["lmax"], q.nth("lmax", i))
    if past(i, 2):
        dve.wait_ge(q["exp"], q.nth("exp", i, 2))
    dve.tensor_tensor(r.lt[:, u, :].rearrange("p (g e) -> p g e", e=E), logits, bcast(r.mx[:, u, :], 2, E),
                      ALU.subtract).then_inc(q["lt"], 1)


def route_select(dve, q, r, E, K, normalise, i, u):
    ex = r.ex[:, u, :].rearrange("p (g e) -> p g e", e=E + PAD)
    out = r.out[:, u, :].rearrange("p (g e) -> p g e", e=E + PAD)
    dve.wait_ge(q["exp"], q.nth("exp", i))
    if not normalise:
        dve.tensor_reduce(r.sum[:, u, :], ex[:, :, 0:E], AX, ALU.add).then_inc(q["lsum"], 1)
        dve.wait_ge(q["lsum"], q.nth("lsum", i))
        dve.reciprocal(r.rec[:, u, :], r.sum[:, u, :]).then_inc(q["lrec"], 1)
        dve.wait_ge(q["lrec"], q.nth("lrec", i))
        dve.tensor_tensor(ex[:, :, 0:E], ex[:, :, 0:E], bcast(r.rec[:, u, :], 2, E), ALU.mult) \
            .then_inc(q["prob"], 1)
        dve.wait_ge(q["prob"], q.nth("prob", i))
    dve.sem_inc(q["passed"], 1)
    for g in range(G):
        last = dve.max(r.top[:, u, 8 * g:8 * g + 8], ex[:, g, 0:E])
    last.then_inc(q["top"], 1)
    dve.wait_ge(q["top"], q.nth("top", i))
    dve.memset(r.top[:, u, :].rearrange("p (g e) -> p g e", e=8)[:, :, K:8], -1.0).then_inc(q["topk"], 1)
    dve.wait_ge(q["topk"], q.nth("topk", i))
    dve.sem_inc(q["passed"], 1)
    for g in range(G):
        last = dve.match_replace(out[:, g, :], r.top[:, u, 8 * g:8 * g + 8], ex[:, g, :], -2.0)
    last.then_inc(q["marked"], 1)


def route_weights(dve, q, r, E, normalise, with_mask, i, u):
    ex = r.ex[:, u, :].rearrange("p (g e) -> p g e", e=E + PAD)
    out = r.out[:, u, :].rearrange("p (g e) -> p g e", e=E + PAD)
    parts = r.parts[:, u, :].rearrange("p (g r) -> p g r", r=ROWS)
    sc = r.sc[:, u, :].rearrange("p (g e) -> p g e", e=E)
    rest = r.rest[:, u, :].rearrange("p (g e) -> p g e", e=E)
    dve.wait_ge(q["marked"], q.nth("marked", i))
    if past(i, 2):
        dve.wait_ge(q["partsT"], q.nth("partsT", i, 2))
    if with_mask:
        for k in range(3):
            dve.tensor_scalar(parts[:, :, 3 * E + k * E:3 * E + k * E + E], out[:, :, 0:E], -1.5, None, ALU.is_lt)
    dve.scalar_tensor_tensor(out=sc, in0=out[:, :, 0:E], scalar=-1.5, in1=ex[:, :, 0:E], op0=ALU.is_lt,
                             op1=ALU.mult).then_inc(q["chosen"], 1)
    dve.wait_ge(q["chosen"], q.nth("chosen", i))
    if normalise:
        dve.tensor_reduce(r.sum[:, u, :], sc, AX, ALU.add).then_inc(q["lsum"], 1)
        dve.wait_ge(q["lsum"], q.nth("lsum", i))
        dve.reciprocal(r.rec[:, u, :], r.sum[:, u, :]).then_inc(q["lrec"], 1)
        dve.wait_ge(q["lrec"], q.nth("lrec", i))
        dve.tensor_tensor(sc, sc, bcast(r.rec[:, u, :], 2, E), ALU.mult).then_inc(q["prob"], 1)
        dve.wait_ge(q["prob"], q.nth("prob", i))
    dve.tensor_copy(parts[:, :, 0:E], sc).then_inc(q["hi"], 1)
    dve.wait_ge(q["hi"], q.nth("hi", i))
    dve.tensor_tensor(rest, sc, parts[:, :, 0:E], ALU.subtract).then_inc(q["rest1"], 1)
    dve.wait_ge(q["rest1"], q.nth("rest1", i))
    dve.tensor_copy(parts[:, :, E:2 * E], rest).then_inc(q["mid"], 1)
    dve.wait_ge(q["mid"], q.nth("mid", i))
    dve.tensor_tensor(rest, rest, parts[:, :, E:2 * E], ALU.subtract).then_inc(q["rest2"], 1)
    dve.wait_ge(q["rest2"], q.nth("rest2", i))
    dve.tensor_copy(parts[:, :, 2 * E:3 * E], rest).then_inc(q["parts"], 1)


ROUTE_SIGNALS = ["centred", "y", "yTps", "yT", "logits", "lmax", "lt", "exp", "lsum", "lrec", "prob", "top", "topk",
                 "marked", "chosen", "hi", "rest1", "mid", "rest2", "parts", "partsT", "partsTs", "passed",
                 "total", "totalT", "x"]


def route_buffers(sb, E):
    r = Named()
    r.mx, r.sum, r.rec = (sb(f"r_{name}", [S, 2, G]) for name in ("mx", "sum", "rec"))
    r.lt, r.sc, r.rest = (sb(f"r_{name}", [S, 2, G * E]) for name in ("lt", "sc", "rest"))
    r.ex, r.out = (sb(f"r_{name}", [S, 2, G * (E + PAD)]) for name in ("ex", "out"))
    r.top = sb("r_top", [S, 2, G * 8])
    r.parts = sb("r_parts", [S, 2, G * ROWS], BF16)
    r.partsT = sb("r_partsT", [ROWS, 2, N], BF16)
    return r


def front_tensor(pe, m, q, y, yT, gate, r, E):
    PS = m.PS

    def turn_y(i, u):
        pe.wait_ge(q["y"], q.nth("y", i))
        if past(i, 1):
            pe.wait_ge(q["partsTs"], q.nth("partsTs", i, 1))
        for g in range(G):
            last = pe.transpose(PS[:, 6, g * S:(g + 1) * S], y[:, u, g * D:(g + 1) * D], m.IDENT[:, :])
        last.then_inc(q["yTps"], 1)

    def logits(i, u):
        pe.wait_ge(q["yT"], q.nth("yT", i))
        if past(i, 2):
            pe.wait_ge(q["x"], q.nth("x", i, 2))
        for g in range(G):
            last = pe.matmul(PS[:, 7, g * E:(g + 1) * E], yT[:, u, g * S:(g + 1) * S], gate[:, :],
                             start=True, stop=True)
        last.then_inc(q["logits"], 1)

    def turn_parts(i, u):
        pe.wait_ge(q["parts"], q.nth("parts", i))
        for g in range(G):
            last = pe.transpose(PS[0:ROWS, 6, 0:N // 2].bitcast(BF16)[:, g * S:(g + 1) * S],
                                r.parts[:, u, g * ROWS:(g + 1) * ROWS], m.IDENT_BF[:, :])
        last.then_inc(q["partsT"], 1)

    return turn_y, logits, turn_parts


def front_scalar(act, m, q, yT, r, E, reader):
    PS = m.PS

    def copy_y(i, u):
        act.wait_ge(q["yTps"], q.nth("yTps", i))
        if past_part(i, reader[1] - 1, reader[1], 2 * reader[1]):
            act.wait_ge(q[reader[0]], nth_part(i, reader[1] - 1, reader[1], 2 * reader[1]))
        act.activation(yT[:, u, :], PS[:, 6, :], ACT.Copy).then_inc(q["yT"], 1)

    def exponential(i, u):
        act.wait_ge(q["lt"], q.nth("lt", i))
        if past(i, 2):
            act.wait_ge(q["chosen"], q.nth("chosen", i, 2))
        act.activation(r.ex[:, u, :].rearrange("p (g e) -> p g e", e=E + PAD)[:, :, 0:E],
                       r.lt[:, u, :].rearrange("p (g e) -> p g e", e=E), ACT.Exp).then_inc(q["exp"], 1)

    def copy_parts(i, u):
        act.wait_ge(q["partsT"], q.nth("partsT", i))
        act.activation(r.partsT[:, u, :], PS[0:ROWS, 6, 0:N // 2].bitcast(BF16), ACT.Copy).then_inc(q["partsTs"], 1)

    return copy_y, exponential, copy_parts


def layer0_experts(nc, m, t):
    n = "L0_ffn_"
    E, K, NP = 16, 4, 8
    with ExitStack() as ctx:
        def sb(name, shape, dt=F32):
            return ctx.enter_context(nc.sbuf_tensor(f"e0_{name}", shape, dt))

        w1, w3, w2 = sb("w1", [D, NP * 128]), sb("w3", [D, NP * 128]), sb("w2", [128, NP, D])
        gate = sb("gate", [D, E])
        pick_f, pick = sb("pick_f", [ROWS, NP * 128]), sb("pick", [ROWS, NP * 128], BF16)
        y, yT = sb("y", [S, 2, N]), sb("yT", [D, 2, N])
        r = route_buffers(sb, E)
        act_g = sb("act_g", [128, 2, N])
        gu = sb("gu", [128, 2, N])
        hid = sb("hid", [128, 2, N])
        total = sb("total", [D, 2, N])
        q = Signals(ctx, nc, "e0", ROUTE_SIGNALS + ["prep", "up", "silu", "gu", "hid", "down"])
        PS = m.PS

        with nc.Block() as block:
            loads = [(w1[:, :], t[n + "w1"]), (w3[:, :], t[n + "w3"]), (w2[:, :, :], t[n + "w2"]),
                     (gate[:, :], t[n + "gate_w"]),
                     (pick_f[:, :], t["c_pick_pairs"].rearrange("r p c -> r (p c)"))]

            @block.sync
            def _(sp):
                for dst, src in loads:
                    sp.dma_start(dst, src).then_inc(m.s_weights, 16)
            m.weight_loads += 16 * len(loads)

            @block.gpsimd
            def _(pool):
                norm_gpsimd(pool, m)

            @block.vector
            def _(dve):
                dve.memset(r.ex[:, :, :], -1.0)
                dve.memset(r.parts[:, :, :], 0.0)
                norm_vector(dve, m)
                dve.wait_ge(m.s_weights, m.weight_loads)
                dve.tensor_copy(pick[:, :], pick_f[:, :])

        block = ctx.enter_context(nc.Block())


        @block.tensor
        def _(pe):
            turn_y, logits, turn_parts = front_tensor(pe, m, q, y, yT, gate, r, E)

            def up(i, u, p):
                v = p % 2
                if p == 0:
                    pe.wait_ge(q["yT"], q.nth("yT", i))
                if past_part(i, p, NP, 2):
                    pe.wait_ge(q["silu"], nth_part(i, p, NP, 2))
                pe.matmul(PS[:, v, :], w1[:, p * 128:(p + 1) * 128], yT[:, u, :], start=True, stop=True)
                if past_part(i, p, NP, 2):
                    pe.wait_ge(q["gu"], nth_part(i, p, NP, 2))
                pe.matmul(PS[:, 2 + v, :], w3[:, p * 128:(p + 1) * 128], yT[:, u, :], start=True, stop=True)
                if p == 0:
                    pe.wait_ge(q["partsTs"], q.nth("partsTs", i))
                if past_part(i, p, NP, 1):
                    pe.wait_ge(q["hid"], nth_part(i, p, NP, 1))
                pe.matmul(PS[:, 4, :], pick[:, p * 128:(p + 1) * 128], r.partsT[:, u, :],
                          start=True, stop=True).then_inc(q["up"], 1)

            def down(i, p):
                pe.wait_ge(q["hid"], nth_part(i, p, NP))
                if p == 0:
                    if past(i, 1):
                        pe.wait_ge(q["total"], q.nth("total", i, 1))
                last = pe.matmul(PS[:, 5, :], w2[:, p, :], hid[:, p % 2, :], start=(p == 0), stop=(p == NP - 1))
                last.then_inc(q["down"], 1)

            def turn_total(i, u):
                pe.wait_ge(q["total"], q.nth("total", i))
                pe.wait_ge(q["lt"], q.nth("lt", i, -1, NG))
                for g in range(G):
                    last = pe.transpose(PS[:, 7, g * D:(g + 1) * D], total[:, u, g * S:(g + 1) * S], m.IDENT[:, :])
                last.then_inc(q["totalT"], 1)

            def step(s, u, h):
                a = (u + 1) % 2
                for p in range(NP):
                    if real(s, NG):
                        up(s, u, p)
                    if p == 0 and real(s - 1, NG):
                        down(s - 1, NP - 1)
                    if p > 0 and real(s, NG):
                        down(s, p - 1)
                    if p == 1 and real(s + 1, NG):
                        turn_y(s + 1, a)
                    if p == 2 and real(s - 1, NG):
                        turn_total(s - 1, a)
                    if p == 4 and real(s + 1, NG):
                        logits(s + 1, a)
                    if p == 7 and real(s + 1, NG):
                        turn_parts(s + 1, a)
            run_slots(pe, step, 1, 1, NG)

        @block.scalar
        def _(act):
            copy_y, exponential, copy_parts = front_scalar(act, m, q, yT, r, E, ("up", NP))

            def step(s, u, h):
                a = (u + 1) % 2
                for p in range(NP):
                    if real(s, NG):
                        act.wait_ge(q["up"], nth_part(s, p, NP))
                        if past_part(s, p, NP, 2):
                            act.wait_ge(q["gu"], nth_part(s, p, NP, 2))
                        act.activation(act_g[:, p % 2, :], PS[:, p % 2, :], ACT.Silu).then_inc(q["silu"], 1)
                    if p == 0 and real(s - 1, NG):
                        act.wait_ge(q["down"], nth_part(s - 1, NP - 1, NP))
                        if past(s - 1, 2):
                            act.wait_ge(q["totalT"], q.nth("totalT", s - 1, 2))
                        act.activation(total[:, a, :], PS[:, 5, :], ACT.Copy).then_inc(q["total"], 1)
                    if p == 1 and real(s + 1, NG):
                        copy_y(s + 1, a)
                    if p == 5 and real(s + 1, NG):
                        exponential(s + 1, a)
                if real(s + 1, NG):
                    copy_parts(s + 1, a)
            run_slots(act, step, 1, 1, NG)

        @block.vector
        def _(dve):
            def step(s, u, h):
                a = (u + 1) % 2
                for p in range(NP):
                    v = p % 2
                    if real(s, NG):
                        dve.wait_ge(q["silu"], nth_part(s, p, NP))
                        dve.tensor_tensor(gu[:, v, :], act_g[:, v, :], PS[:, 2 + v, :], ALU.mult).then_inc(q["gu"], 1)
                        dve.wait_ge(q["gu"], nth_part(s, p, NP))
                        if past_part(s, p, NP, 2):
                            dve.wait_ge(q["down"], nth_part(s, p, NP, 2))
                        dve.tensor_tensor(hid[:, v, :], gu[:, v, :], PS[:, 4, :], ALU.mult).then_inc(q["hid"], 1)
                    if p == 3 and real(s - 1, NG):
                        dve.wait_ge(q["totalT"], q.nth("totalT", s - 1))
                        dve.tensor_tensor(group(m.X, s - 1), group(m.X, s - 1),
                                          PS[:, 7, :].rearrange("p (g d) -> p g d", d=D), ALU.add).then_inc(q["x"], 1)
                        dve.wait_ge(q["x"], q.nth("x", s - 1))
                        group_statistics(dve, m, s - 1)
                    if p == 4 and real(s + 1, NG):
                        route_logits(dve, q, r, PS[:, 7, 0:G * E].rearrange("p (g e) -> p g e", e=E), E, s + 1, a)
                    if p == 5 and real(s + 1, NG):
                        route_select(dve, q, r, E, K, True, s + 1, a)
                    if p == 6 and real(s + 1, NG):
                        route_weights(dve, q, r, E, True, False, s + 1, a)
                if real(s + 2, NG):
                    normalise_group(dve, m, q, y, s + 2, u)
            run_slots(dve, step, 2, 1, NG)

        @block.gpsimd
        def _(pool):
            norm_gpsimd_rest(pool, m)


def layer1_experts(nc, m, t):
    n = "L1_ffn_"
    E, K = 8, 2
    NE = E + 2
    with ExitStack() as ctx:
        def sb(name, shape, dt=F32):
            return ctx.enter_context(nc.sbuf_tensor(f"e1_{name}", shape, dt))

        w1, w2, w3 = (sb(c, [D, E, 128]) for c in ("w1", "w2", "w3"))
        sw1, sw2, sw3 = sb("sw1", [D, 256]), sb("sw2", [D, 256]), sb("sw3", [128, 2, D])
        b1, b2 = sb("b1", [128, E]), sb("b2", [D, E])
        gate = sb("gate", [D, E])
        pick_f, pick = sb("pick_f", [ROWS, E * 128]), sb("pick", [ROWS, E * 128], BF16)
        bias_rows = sb("bias_rows", [ROWS, D])
        bias_rest = sb("bias_rest", [ROWS, D])
        bias_parts = sb("bias_parts", [ROWS, 3, D], BF16)
        pick_b = sb("pick_b", [ROWS, 3, E])
        b3 = sb("b3", [ROWS, E * 128], BF16)
        y, yT = sb("y", [S, 2, N]), sb("yT", [D, 2, N])
        r = route_buffers(sb, E)
        xs = sb("xs", [D, 2, N])
        hid = sb("hid", [128, 2, N])
        up = sb("up", [128, 2, N])
        prod = sb("prod", [128, 2, N])
        acc = sb("acc", [D, 2, N])
        total = sb("total", [D, 2, N])
        q = Signals(ctx, nc, "e1", ROUTE_SIGNALS + [
            "bzero", "bhi", "brest", "bmid", "brest2", "blo", "bsum", "wide", "xs", "gate", "hid", "value", "up",
            "upc", "down", "prod", "acc", "held"])
        PS = m.PS

        with nc.Block() as block:
            loads = [(w1[:, :, :], t[n + "w1"]), (w2[:, :, :], t[n + "w2"]), (w3[:, :, :], t[n + "w3"]),
                     (sw1[:, :], t[n + "sw1"]), (sw2[:, :], t[n + "sw2"]), (sw3[:, :, :], t[n + "sw3"]),
                     (b1[:, :], t[n + "b1"]), (b2[:, :], t[n + "b2"]), (gate[:, :], t[n + "gate_w"]),
                     (pick_f[:, :], t["c_pick_weight"].rearrange("r p c -> r (p c)")),
                     (pick_b[:, :, :], t["c_pick_bias"])]
            loads += [(bias_rows[8 * k:8 * k + 8, :], t[n + "b3"]) for k in range(6)]

            @block.sync
            def _(sp):
                sp.wait_ge(q["bzero"], 1)
                for dst, src in loads:
                    sp.dma_start(dst, src).then_inc(m.s_weights, 16)
            m.weight_loads += 16 * len(loads)

            @block.gpsimd
            def _(pool):
                norm_gpsimd(pool, m)

            @block.vector
            def _(dve):
                dve.memset(r.ex[:, :, :], -1.0)
                dve.memset(r.parts[:, :, :], 0.0)
                dve.memset(bias_rows[:, :], 0.0).then_inc(q["bzero"], 1)
                norm_vector(dve, m)
                dve.wait_ge(m.s_weights, m.weight_loads)
                dve.tensor_copy(pick[:, :], pick_f[:, :])
                dve.tensor_copy(bias_parts[:, 0, :], bias_rows[:, :]).then_inc(q["bhi"], 1)
                dve.wait_ge(q["bhi"], 1)
                dve.tensor_tensor(bias_rest[:, :], bias_rows[:, :], bias_parts[:, 0, :], ALU.subtract) \
                    .then_inc(q["brest"], 1)
                dve.wait_ge(q["brest"], 1)
                dve.tensor_copy(bias_parts[:, 1, :], bias_rest[:, :]).then_inc(q["bmid"], 1)
                dve.wait_ge(q["bmid"], 1)
                dve.tensor_tensor(bias_rows[:, :], bias_rest[:, :], bias_parts[:, 1, :], ALU.subtract) \
                    .then_inc(q["brest2"], 1)
                dve.wait_ge(q["brest2"], 1)
                dve.tensor_copy(bias_parts[:, 2, :], bias_rows[:, :]).then_inc(q["blo"], 1)
                dve.wait_ge(q["blo"], 1)
                for k in range(3):
                    if k:
                        dve.wait_ge(q["bsum"], E * k)
                    for e in range(E):
                        row_part = b3[:, e * 128:(e + 1) * 128]
                        if k == 0:
                            last = dve.tensor_scalar(row_part, bias_parts[:, k, :], pick_b[:, k, e:e + 1], None,
                                                     ALU.mult)
                        else:
                            last = dve.scalar_tensor_tensor(out=row_part, in0=bias_parts[:, k, :],
                                                            scalar=pick_b[:, k, e:e + 1], in1=row_part,
                                                            op0=ALU.mult, op1=ALU.add)
                        last.then_inc(q["bsum"], 1)

        block = ctx.enter_context(nc.Block())


        @block.tensor
        def _(pe):
            turn_y, logits, turn_parts = front_tensor(pe, m, q, y, yT, gate, r, E)

            def widen(i, u, e):
                if e == 0:
                    pe.wait_ge(q["partsTs"], q.nth("partsTs", i))
                if past_part(i, e, E, 1):
                    pe.wait_ge(q["xs"], nth_part(i, e, E, 1))
                pe.matmul(PS[:, 2, :], pick[:, e * 128:(e + 1) * 128], r.partsT[:, u, :],
                          start=True, stop=True).then_inc(q["wide"], 1)

            def gate_up(i, u, e):
                if past_part(i, e, NE, 1):
                    pe.wait_ge(q["hid"], nth_part(i, e, NE, 1))
                if e < E:
                    pe.wait_ge(q["xs"], nth_part(i, e, E))
                    pe.matmul(PS[:, 0, :], w1[:, e, :], xs[:, e % 2, :], start=True, stop=True).then_inc(q["gate"], 1)
                    if past_part(i, e, E, 1):
                        pe.wait_ge(q["upc"], nth_part(i, e, E, 1))
                    pe.matmul(PS[:, 1, :], b3[:, e * 128:(e + 1) * 128], r.partsT[:, u, :], start=True, stop=False)
                    pe.matmul(PS[:, 1, :], w3[:, e, :], xs[:, e % 2, :], start=False, stop=True).then_inc(q["up"], 1)
                else:
                    c = slice((e - E) * 128, (e - E + 1) * 128)
                    pe.matmul(PS[:, 0, :], sw1[:, c], yT[:, u, :], start=True, stop=True).then_inc(q["gate"], 1)
                    if past_part(i, e, NE, E + 1 if e == E else 1):
                        pe.wait_ge(q["prod"], nth_part(i, e, NE, E + 1 if e == E else 1))
                    pe.matmul(PS[:, 4, :], sw2[:, c], yT[:, u, :], start=True, stop=True).then_inc(q["value"], 1)

            def down(i, u, e):
                pe.wait_ge(q["hid"], nth_part(i, e, NE))
                if e < E:
                    if past_part(i, e, NE, 1):
                        pe.wait_ge(q["prod"], nth_part(i, e, NE, 1))
                    pe.matmul(PS[:, 3, :], w2[:, e, :], hid[:, e % 2, :], start=True, stop=True) \
                        .then_inc(q["down"], 1)
                else:
                    pe.wait_ge(q["prod"], nth_part(i, e, NE))
                    if e == E:
                        if past(i, 1):
                            pe.wait_ge(q["total"], q.nth("total", i, 1))
                    last = pe.matmul(PS[:, 5, :], sw3[:, e - E, :], prod[:, e % 2, :], start=(e == E),
                                     stop=(e == NE - 1))
                    last.then_inc(q["down"], 1)

            def turn_total(i, u):
                pe.wait_ge(q["total"], q.nth("total", i))
                pe.wait_ge(q["lt"], q.nth("lt", i, -1, NG))
                for g in range(G):
                    last = pe.transpose(PS[:, 7, g * D:(g + 1) * D], total[:, u, g * S:(g + 1) * S], m.IDENT[:, :])
                last.then_inc(q["totalT"], 1)

            def step(s, u, h):
                a = (u + 1) % 2
                for e in range(NE):
                    if real(s, NG):
                        if e + 1 < E:
                            widen(s, u, e + 1)
                        gate_up(s, u, e)
                    if e == 0 and real(s - 1, NG):
                        down(s - 1, a, NE - 1)
                    if e > 0 and real(s, NG):
                        down(s, u, e - 1)
                    if e == 1 and real(s + 1, NG):
                        turn_y(s + 1, a)
                    if e == 2 and real(s - 1, NG):
                        turn_total(s - 1, a)
                    if e == 4 and real(s + 1, NG):
                        logits(s + 1, a)
                    if e == 8 and real(s + 1, NG):
                        turn_parts(s + 1, a)
                    if e == 9 and real(s + 1, NG):
                        widen(s + 1, a, 0)
            run_slots(pe, step, 1, 1, NG)

        @block.scalar
        def _(act):
            copy_y, exponential, copy_parts = front_scalar(act, m, q, yT, r, E, ("value", 2))

            def step(s, u, h):
                a = (u + 1) % 2
                for e in range(NE):
                    if real(s, NG):
                        act.wait_ge(q["gate"], nth_part(s, e, NE))
                        if past_part(s, e, NE, 2):
                            act.wait_ge(q["down"], nth_part(s, e, NE, 2))
                        if past_part(s, e, NE, 2):
                            act.wait_ge(q["prod"], nth_part(s, e, NE, 2))
                        bias = {"bias": b1[:, e:e + 1]} if e < E else {}
                        act.activation(hid[:, e % 2, :], PS[:, 0, :], ACT.Silu, **bias).then_inc(q["hid"], 1)
                        if e < E:
                            act.wait_ge(q["up"], nth_part(s, e, E))
                            act.activation(up[:, e % 2, :], PS[:, 1, :], ACT.Copy).then_inc(q["upc"], 1)
                    if e == 1 and real(s + 1, NG):
                        copy_y(s + 1, a)
                    if e == 5 and real(s + 1, NG):
                        exponential(s + 1, a)
                    if e == 8 and real(s + 1, NG):
                        copy_parts(s + 1, a)
            run_slots(act, step, 1, 1, NG)

        @block.gpsimd
        def _(pool):
            norm_gpsimd_rest(pool, m)

            def step(s, u, h):
                for e in range(E):
                    if real(s, NG):
                        pool.wait_ge(q["prod"], nth_part(s, e, NE))
                        if e == 0:
                            if past(s, 2):
                                pool.wait_ge(q["total"], q.nth("total", s, 2))
                            pool.sem_inc(q["held"], 1)
                            pool.tensor_copy(acc[:, u, :], prod[:, e % 2, :]).then_inc(q["acc"], 1)
                        else:
                            if past_part(s, e, E, 1):
                                pool.wait_ge(q["acc"], nth_part(s, e, E, 1))
                            pool.tensor_tensor(acc[:, u, :], acc[:, u, :], prod[:, e % 2, :], ALU.add) \
                                .then_inc(q["acc"], 1)
            run_slots(pool, step, 0, 0, NG)

        @block.vector
        def _(dve):
            def scale_x(i, u, e):
                dve.wait_ge(q["wide"], nth_part(i, e, E))
                if past_part(i, e, E, 2):
                    dve.wait_ge(q["up"], nth_part(i, e, E, 2))
                dve.tensor_tensor(xs[:, e % 2, :], yT[:, u, :], PS[:, 2, :], ALU.mult).then_inc(q["xs"], 1)

            def multiply(i, u, e):
                if e < E:
                    dve.wait_ge(q["down"], nth_part(i, e, NE))
                    dve.wait_ge(q["upc"], nth_part(i, e, E))
                    if past_part(i, e, E, 2):
                        dve.wait_ge(q["acc"], nth_part(i, e, E, 2))
                    dve.scalar_tensor_tensor(out=prod[:, e % 2, :], in0=PS[:, 3, :], scalar=b2[:, e:e + 1],
                                             in1=up[:, e % 2, :], op0=ALU.add, op1=ALU.mult).then_inc(q["prod"], 1)
                else:
                    dve.wait_ge(q["value"], nth_part(i, e - E, 2))
                    dve.wait_ge(q["hid"], nth_part(i, e, NE))
                    dve.wait_ge(q["acc"], nth_part(i, e - 2, E))
                    dve.tensor_tensor(prod[:, e % 2, :], hid[:, e % 2, :], PS[:, 4, :], ALU.mult) \
                        .then_inc(q["prod"], 1)

            def finish(i, u):
                dve.wait_ge(q["down"], nth_part(i, NE - 1, NE))
                dve.wait_ge(q["acc"], nth_part(i, E - 1, E))
                if past(i, 2):
                    dve.wait_ge(q["totalT"], q.nth("totalT", i, 2))
                dve.tensor_tensor(total[:, u, :], acc[:, u, :], PS[:, 5, :], ALU.add).then_inc(q["total"], 1)

            def step(s, u, h):
                a = (u + 1) % 2
                for e in range(NE):
                    if real(s, NG) and e + 1 < E:
                        scale_x(s, u, e + 1)
                    if e == 0 and real(s - 1, NG):
                        finish(s - 1, a)
                    if e > 0 and real(s, NG):
                        multiply(s, u, e - 1)
                    if e == 3 and real(s - 1, NG):
                        dve.wait_ge(q["totalT"], q.nth("totalT", s - 1))
                        dve.tensor_tensor(group(m.X, s - 1), group(m.X, s - 1),
                                          PS[:, 7, :].rearrange("p (g d) -> p g d", d=D), ALU.add).then_inc(q["x"], 1)
                        dve.wait_ge(q["x"], q.nth("x", s - 1))
                        group_statistics(dve, m, s - 1)
                    if e == 4 and real(s + 1, NG):
                        route_logits(dve, q, r, PS[:, 7, 0:G * E].rearrange("p (g e) -> p g e", e=E), E, s + 1, a)
                    if e == 6 and real(s + 1, NG):
                        route_select(dve, q, r, E, K, False, s + 1, a)
                    if e == 7 and real(s + 1, NG):
                        route_weights(dve, q, r, E, False, True, s + 1, a)
                    if e == 9 and real(s + 1, NG):
                        scale_x(s + 1, a, 0)
                if real(s, NG):
                    multiply(s, u, NE - 1)
                if real(s + 2, NG):
                    normalise_group(dve, m, q, y, s + 2, u)
            run_slots(dve, step, 2, 1, NG)


def layer3_experts(nc, m, t):
    n = "L3_ffn_"
    E, K, CAP, I = 64, 4, 128, 64
    SLOTS = E * CAP
    NP = E // 2
    with ExitStack() as ctx:
        def sb(name, shape, dt=F32):
            return ctx.enter_context(nc.sbuf_tensor(f"e3_{name}", shape, dt))

        rows = nc.dram_tensor("expert_rows", (SLOTS, D), F32, kind="Internal").ap()
        results = nc.dram_tensor("expert_results", (SLOTS, D), F32, kind="Internal").ap()
        w1, w2 = sb("w1", [D, E, 2 * I]), sb("w2", [2 * I, NP, D])
        results_at = sb("results_at", [S, B, K], U32)
        weight = sb("weight", [S, B, K])
        q = Signals(ctx, nc, "e3", [
            "zeroed", "centred", "y", "yTps", "yT", "logits", "lmax", "lt", "exp", "lsum",
            "lrec", "prob", "top", "topk", "marked", "mask", "red", "ahead", "pos", "near", "far", "key", "skey1", "skey2",
            "keytop", "skeytop", "at", "pick", "passed", "scat0", "scat1", "in0", "in1", "xT", "xTs", "up", "gate",
            "hid", "hidT", "hidTs", "down", "ress", "store0", "store1", "atc", "gath0", "gath1",
            "sum0", "sum1", "sum2", "sum", "held", "out0", "out1", "loaded"])
        PS = m.PS

        with ExitStack() as inner:
            def sc(name, shape, dt=F32):
                return inner.enter_context(nc.sbuf_tensor(f"e3r_{name}", shape, dt))

            zero = sc("zero", [128, 2048])
            gate = sc("gate", [D, E])
            before_f, before = sc("before_f", [S, S]), sc("before", [S, S], BF16)
            ones = sc("ones", [S, S], BF16)
            slot0 = sc("slot0", [S, E])
            y, yT = sc("y", [S, 2, N]), sc("yT", [D, 2, N])
            lt, mx = sc("lt", [S, 2, G * E]), sc("mx", [S, 2, G])
            ex = sc("ex", [S, 2, G * (E + PAD)])
            mark = sc("mark", [S, 2, G * (E + PAD)])
            top = sc("top", [S, 2, G * 8])
            lsum, rec = sc("lsum", [S, 2, G]), sc("rec", [S, 2, G])
            mask = sc("mask", [S, 2, G * E], BF16)
            red = sc("red", [S, 2, E])
            ahead = sc("ahead", [S, 2, E], BF16)
            near, far = sc("near", [S, 2, G * E]), sc("far", [S, 2, G * E])
            key, skey = sc("key", [S, 2, G * E]), sc("skey", [S, 2, G * E])
            keytop, skeytop = sc("keytop", [S, 2, G * 8]), sc("skeytop", [S, 2, G * 8])
            rows_at = sc("rows_at", [S, 2, G * K], U32)
            junk = sc("junk", [S, 2, G * K * E])
            picked = sc("picked", [S, 2, G * K])

            with nc.Block() as block:
                loads = [(gate[:, :], t[n + "router_w"]), (before_f[:, :], t["c_before"]),
                         (slot0[:, :], t["c_slot0"])]

                @block.sync
                def _(sp):
                    for dst, src in loads:
                        sp.dma_start(dst, src).then_inc(m.s_weights, 16)
                m.weight_loads += 16 * len(loads)

                @block.gpsimd
                def _(pool):
                    norm_gpsimd(pool, m)

                @block.vector
                def _(dve):
                    dve.memset(zero[:, :], 0.0)
                    dve.memset(ex[:, :, :], -1.0)
                    dve.memset(ones[:, :], 1.0)
                    dve.memset(ahead[:, :, :], 0.0)
                    norm_vector(dve, m)
                    dve.wait_ge(m.s_weights, m.weight_loads)
                    dve.tensor_copy(before[:, :], before_f[:, :])

            with nc.Block() as block:
                @block.sync
                def _(sp):
                    for k in range(4):
                        sp.dma_start(rows[k * (SLOTS // 4):(k + 1) * (SLOTS // 4), :]
                                     .rearrange("(p a) d -> p (a d)", p=128), zero[:, :]).then_inc(q["zeroed"], 16)
                    sp.dma_start(w1[:, :, :], t[n + "w1"]).then_inc(q["loaded"], 16)
                    sp.dma_start(w2[:, :, :], t[n + "w2"]).then_inc(q["loaded"], 16)
                    sp.wait_ge(q["loaded"], 32)

                @block.tensor
                def _(pe):
                    def front(i, u):
                        pe.wait_ge(q["y"], q.nth("y", i))
                        if past(i, 1):
                            pe.wait_ge(q["yT"], q.nth("yT", i, 1))
                        for g in range(G):
                            last = pe.transpose(PS[:, 6, g * S:(g + 1) * S], y[:, u, g * D:(g + 1) * D], m.IDENT[:, :])
                        last.then_inc(q["yTps"], 1)

                    def logits(i, u):
                        pe.wait_ge(q["yT"], q.nth("yT", i))
                        if past(i, 1):
                            pe.wait_ge(q["lt"], q.nth("lt", i, 1))
                        for g in range(G):
                            last = pe.matmul(PS[:, 7, g * E:(g + 1) * E], yT[:, u, g * S:(g + 1) * S], gate[:, :],
                                             start=True, stop=True)
                        last.then_inc(q["logits"], 1)

                    def positions(i, u):
                        pe.wait_ge(q["mask"], q.nth("mask", i))
                        if past(i, 1):
                            pe.wait_ge(q["ahead"], q.nth("ahead", i, 1))
                        if past(i, 1):
                            pe.wait_ge(q["far"], q.nth("far", i, 1))
                        for g in range(G):
                            out = PS[:, 5, g * E:(g + 1) * E]
                            pe.matmul(out, before[:, :], mask[:, u, g * E:(g + 1) * E], start=(g == 0), stop=False,
                                      skip_group_check=True)
                            for c in range(g):
                                pe.matmul(out, ones[:, :], mask[:, u, c * E:(c + 1) * E], start=False, stop=False,
                                          skip_group_check=True)
                            last = pe.matmul(out, ones[:, :], ahead[:, u, :], start=False, stop=(g == G - 1),
                                             skip_group_check=True)
                        last.then_inc(q["pos"], 1)

                    def step(s, u, h):
                        a = (u + 1) % 2
                        if real(s, NG):
                            positions(s, u)
                        if real(s + 1, NG):
                            front(s + 1, a)
                            logits(s + 1, a)
                    run_slots(pe, step, 1, 0, NG)

                @block.scalar
                def _(act):
                    act.activation(m.scratch[:, 0:1], m.scratch[:, 1:2], ACT.Exp)

                    def step(s, u, h):
                        a = (u + 1) % 2
                        if real(s, NG):
                            act.wait_ge(q["lt"], q.nth("lt", s))
                            if past(s, 2):
                                act.wait_ge(q["pick"], q.nth("pick", s, 2))
                            act.activation(ex[:, u, :].rearrange("p (g e) -> p g e", e=E + PAD)[:, :, 0:E],
                                           lt[:, u, :].rearrange("p (g e) -> p g e", e=E), ACT.Exp).then_inc(q["exp"], 1)
                        if real(s + 1, NG):
                            act.wait_ge(q["yTps"], q.nth("yTps", s + 1))
                            if past(s + 1, 2):
                                act.wait_ge(q["logits"], q.nth("logits", s + 1, 2))
                            act.activation(yT[:, a, :], PS[:, 6, :], ACT.Copy).then_inc(q["yT"], 1)
                    run_slots(act, step, 1, 0, NG)

                @block.gpsimd
                def _(pool):
                    norm_gpsimd_rest(pool, m)
                    pool.wait_ge(q["zeroed"], 64)

                    def step(s, u, h):
                        pool.wait_ge(q["at"], q.nth("at", s))
                        pool.sem_inc(q["held"], 1)
                        for g in range(G):
                            for k in range(K):
                                pool.indirect_dma_start(
                                    out=rows[:, :],
                                    out_offset=bass.IndirectOffsetOnAxis(ap=rows_at[:, u, g * K + k:g * K + k + 1], axis=0),
                                    in_=y[:, u, g * D:(g + 1) * D], in_offset=None,
                                    bounds_check=SLOTS - 1, oob_is_err=False).then_inc(q[f"scat{u}"], 16)
                    run_slots(pool, step, 0, 0, NG)
                    for u in range(2):
                        pool.wait_ge(q[f"scat{u}"], NG // 2 * G * K * 16)

                @block.vector
                def _(dve):
                    def normalise(i, u, h):
                        if not isinstance(i, int) or i >= 2:
                            dve.wait_ge(q[f"scat{u}"], h * (G * K * 16))
                        if not isinstance(i, int) or i * G >= FIRST:
                            dve.wait_ge(m.s_norm_b, 2 * m.norms + 2)
                        y3 = y[:, u, :].rearrange("p (g d) -> p g d", d=D)
                        dve.tensor_tensor(y3, group(m.X, i), bcast(m.MEAN[:, bass.ds(i * G, G)], 2, D),
                                          ALU.subtract).then_inc(q["centred"], 1)
                        dve.wait_ge(q["centred"], q.nth("centred", i))
                        dve.tensor_tensor(y3, y3, bcast(m.RSTD[:, bass.ds(i * G, G)], 2, D), ALU.mult) \
                            .then_inc(q["y"], 1)

                    def less_max(i, u):
                        lg = PS[:, 7, 0:G * E].rearrange("p (g e) -> p g e", e=E)
                        dve.wait_ge(q["logits"], q.nth("logits", i))
                        dve.tensor_reduce(mx[:, u, :], lg, AX, ALU.max).then_inc(q["lmax"], 1)
                        dve.wait_ge(q["lmax"], q.nth("lmax", i))
                        if past(i, 2):
                            dve.wait_ge(q["exp"], q.nth("exp", i, 2))
                        dve.tensor_tensor(lt[:, u, :].rearrange("p (g e) -> p g e", e=E), lg, bcast(mx[:, u, :], 2, E),
                                          ALU.subtract).then_inc(q["lt"], 1)

                    def select(i, u):
                        ex3 = ex[:, u, :].rearrange("p (g e) -> p g e", e=E + PAD)
                        mark3 = mark[:, u, :].rearrange("p (g e) -> p g e", e=E + PAD)
                        dve.wait_ge(q["exp"], q.nth("exp", i))
                        dve.tensor_reduce(lsum[:, u, :], ex3[:, :, 0:E], AX, ALU.add).then_inc(q["lsum"], 1)
                        dve.wait_ge(q["lsum"], q.nth("lsum", i))
                        dve.reciprocal(rec[:, u, :], lsum[:, u, :]).then_inc(q["lrec"], 1)
                        dve.wait_ge(q["lrec"], q.nth("lrec", i))
                        dve.tensor_tensor(ex3[:, :, 0:E], ex3[:, :, 0:E], bcast(rec[:, u, :], 2, E), ALU.mult) \
                            .then_inc(q["prob"], 1)
                        dve.wait_ge(q["prob"], q.nth("prob", i))
                        dve.sem_inc(q["passed"], 1)
                        for g in range(G):
                            last = dve.max(top[:, u, 8 * g:8 * g + 8], ex3[:, g, 0:E])
                        last.then_inc(q["top"], 1)
                        dve.wait_ge(q["top"], q.nth("top", i))
                        dve.memset(top[:, u, :].rearrange("p (g e) -> p g e", e=8)[:, :, K:8], -1.0) \
                            .then_inc(q["topk"], 1)
                        dve.wait_ge(q["topk"], q.nth("topk", i))
                        dve.sem_inc(q["passed"], 1)
                        for g in range(G):
                            last = dve.match_replace(mark3[:, g, :], top[:, u, 8 * g:8 * g + 8], ex3[:, g, :], -2.0)
                        last.then_inc(q["marked"], 1)
                        dve.wait_ge(q["marked"], q.nth("marked", i))
                        if past(i, 2):
                            dve.wait_ge(q["pos"], q.nth("pos", i, 2))
                        dve.tensor_scalar(mask[:, u, :].rearrange("p (g e) -> p g e", e=E), mark3[:, :, 0:E], -1.5,
                                          None, ALU.is_lt).then_inc(q["mask"], 1)
                        dve.wait_ge(q["mask"], q.nth("mask", i))
                        dve.tensor_reduce(red[:, u, :], mask[:, u, :].rearrange("p (g e) -> p e g", e=E), AX,
                                          ALU.add).then_inc(q["red"], 1)
                        dve.wait_ge(q["red"], q.nth("red", i))
                        if past(i, 1):
                            dve.wait_ge(q["pos"], q.nth("pos", i, 1))
                        dve.tensor_tensor(ahead[:, (u + 1) % 2, :], ahead[:, u, :], red[:, u, :], ALU.add) \
                            .then_inc(q["ahead"], 1)

                    def place(i, u):
                        pos = PS[:, 5, 0:G * E].rearrange("p (g e) -> p g e", e=E)
                        mask_row = mask[:, u, :]
                        dve.wait_ge(q["pos"], q.nth("pos", i))
                        dve.scalar_tensor_tensor(out=near[:, u, :].rearrange("p (g e) -> p g e", e=E), in0=pos,
                                                 scalar=CAP - 1.0, in1=bcast(slot0[:, :], 1, G), op0=ALU.min,
                                                 op1=ALU.add).then_inc(q["near"], 1)
                        dve.tensor_scalar(far[:, u, :], PS[:, 5, 0:G * E], float(CAP), float(SLOTS), ALU.is_ge,
                                          ALU.mult).then_inc(q["far"], 1)
                        dve.wait_ge(q["near"], q.nth("near", i))
                        dve.tensor_tensor(key[:, u, :], near[:, u, :], mask_row, ALU.mult).then_inc(q["key"], 1)
                        dve.wait_ge(q["far"], q.nth("far", i))
                        dve.tensor_tensor(skey[:, u, :], near[:, u, :], far[:, u, :], ALU.add).then_inc(q["skey1"], 1)
                        dve.wait_ge(q["skey1"], q.nth("skey1", i))
                        dve.tensor_tensor(skey[:, u, :], skey[:, u, :], mask_row, ALU.mult).then_inc(q["skey2"], 1)
                        dve.wait_ge(q["key"], q.nth("key", i))
                        dve.wait_ge(q["skey2"], q.nth("skey2", i))
                        dve.sem_inc(q["passed"], 1)
                        for g in range(G):
                            dve.max(keytop[:, u, 8 * g:8 * g + 8], key[:, u, g * E:(g + 1) * E])
                            last = dve.max(skeytop[:, u, 8 * g:8 * g + 8], skey[:, u, g * E:(g + 1) * E])
                        last.then_inc(q["keytop"], 1)
                        dve.wait_ge(q["keytop"], q.nth("keytop", i))
                        k3 = keytop[:, u, :].rearrange("p (g e) -> p g e", e=8)
                        s3 = skeytop[:, u, :].rearrange("p (g e) -> p g e", e=8)
                        dve.tensor_scalar(group(results_at, i), k3[:, :, 0:K], -1.0, None, ALU.add)
                        dve.tensor_scalar(rows_at[:, u, :].rearrange("p (g k) -> p g k", k=K), s3[:, :, 0:K], -1.0,
                                          None, ALU.add).then_inc(q["at"], 1)
                        for g in range(G):
                            for k in range(K):
                                c = g * K + k
                                last = dve.scalar_tensor_tensor(
                                    out=junk[:, u, c * E:(c + 1) * E], in0=key[:, u, g * E:(g + 1) * E],
                                    scalar=keytop[:, u, 8 * g + k:8 * g + k + 1],
                                    in1=ex[:, u, g * (E + PAD):g * (E + PAD) + E], op0=ALU.is_equal, op1=ALU.mult,
                                    accum_out=picked[:, u, c:c + 1])
                        last.then_inc(q["pick"], 1)
                        dve.wait_ge(q["pick"], q.nth("pick", i))
                        dve.tensor_copy(group(weight, i), picked[:, u, :].rearrange("p (g k) -> p g k", k=K))

                    def step(s, u, h):
                        a = (u + 1) % 2
                        if real(s, NG):
                            less_max(s, u)
                            select(s, u)
                            place(s, u)
                        if real(s + 1, NG):
                            normalise(s + 1, a, h + u)
                    run_slots(dve, step, 1, 0, NG)

        with ExitStack() as inner:
            def sc(name, shape, dt=F32):
                return inner.enter_context(nc.sbuf_tensor(f"e3x_{name}", shape, dt))

            xin = sc("xin", [CAP, 2, 2 * D])
            xT = sc("xT", [D, 2, 2 * CAP])
            gated = sc("gated", [CAP, 2, 2 * I])
            hid = sc("hid", [CAP, 2, 4 * I])
            hidT = sc("hidT", [2 * I, 2, 2 * CAP])
            res = sc("res", [CAP, 2, 2 * D])

            with nc.Block() as block:
                @block.vector
                def _(dve):
                    dve.memset(hid[:, :, :], 0.0)

            block = inner.enter_context(nc.Block())

            def slots(table, i):
                return table[bass.ds(i * 2 * CAP, 2 * CAP), :].rearrange("(e p) d -> p e d", p=CAP)

            @block.sync
            def _(sp):
                def step(s, u, h):
                    if real(s + 2, NP):
                        if past(s + 2, 2):
                            sp.wait_ge(q["xT"], q.nth("xT", s + 2, 2))
                        sp.dma_start(xin[:, u, :].rearrange("p (e d) -> p e d", d=D), slots(rows, s + 2)) \
                            .then_inc(q[f"in{u}"], 16)
                    if real(s, NP):
                        sp.wait_ge(q["ress"], q.nth("ress", s))
                        sp.dma_start(slots(results, s), res[:, u, :].rearrange("p (e d) -> p e d", d=D)) \
                            .then_inc(q[f"store{u}"], 16)
                run_slots(sp, step, 2, 0, NP)
                for u in range(2):
                    sp.wait_ge(q[f"store{u}"], NP // 2 * 16)

            @block.tensor
            def _(pe):
                def turn_rows(i, u, h):
                    pe.wait_ge(q[f"in{u}"], h * 16 + 16)
                    if past(i, 1):
                        pe.wait_ge(q["xTs"], q.nth("xTs", i, 1))
                    for e in range(2):
                        last = pe.transpose(PS[:, 0, e * CAP:(e + 1) * CAP], xin[:, u, e * D:(e + 1) * D],
                                            m.IDENT[:, :])
                    last.then_inc(q["xT"], 1)

                def up(i, u):
                    pe.wait_ge(q["xTs"], q.nth("xTs", i))
                    if past(i, 2):
                        pe.wait_ge(q["hid"], q.nth("hid", i, 2))
                    for e in range(2):
                        last = pe.matmul(PS[:, 1 + u, e * 2 * I:(e + 1) * 2 * I], xT[:, u, e * CAP:(e + 1) * CAP],
                                         seq(w1, 2 * i + e), start=True, stop=True)
                    last.then_inc(q["up"], 1)

                def turn_hidden(i, u):
                    pe.wait_ge(q["hid"], q.nth("hid", i))
                    if past(i, 1):
                        pe.wait_ge(q["hidTs"], q.nth("hidTs", i, 1))
                    for e in range(2):
                        last = pe.transpose(PS[:, 3, e * CAP:(e + 1) * CAP], hid[:, u, e * 2 * I:(e + 1) * 2 * I],
                                            m.IDENT[:, :])
                    last.then_inc(q["hidT"], 1)

                def down(i, u):
                    pe.wait_ge(q["hidTs"], q.nth("hidTs", i))
                    if past(i, 2):
                        pe.wait_ge(q["ress"], q.nth("ress", i, 2))
                    for e in range(2):
                        last = pe.matmul(PS[:, 4 + u, e * D:(e + 1) * D], hidT[:, u, e * CAP:(e + 1) * CAP],
                                         seq(w2, i), start=True, stop=True)
                    last.then_inc(q["down"], 1)

                def step(s, u, h):
                    a = (u + 1) % 2
                    if real(s + 1, NP):
                        turn_rows(s + 1, a, h + u)
                    if real(s, NP):
                        turn_hidden(s, u)
                    if real(s + 1, NP):
                        up(s + 1, a)
                    if real(s, NP):
                        down(s, u)
                run_slots(pe, step, 1, 0, NP)

            @block.scalar
            def _(act):
                act.activation(m.scratch[:, 0:1], m.scratch[:, 1:2], ACT.Silu)

                def step(s, u, h):
                    a = (u + 1) % 2
                    if real(s + 1, NP):
                        act.wait_ge(q["xT"], q.nth("xT", s + 1))
                        if past(s + 1, 2):
                            act.wait_ge(q["up"], q.nth("up", s + 1, 2))
                        act.activation(xT[:, a, :], PS[:, 0, 0:2 * CAP], ACT.Copy).then_inc(q["xTs"], 1)
                    if real(s, NP):
                        act.wait_ge(q["hidT"], q.nth("hidT", s))
                        if past(s, 2):
                            act.wait_ge(q["down"], q.nth("down", s, 2))
                        act.activation(hidT[:, u, :], PS[:, 3, 0:2 * CAP], ACT.Copy).then_inc(q["hidTs"], 1)
                    if real(s + 1, NP):
                        act.wait_ge(q["up"], q.nth("up", s + 1))
                        if past(s + 1, 2):
                            act.wait_ge(q["hid"], q.nth("hid", s + 1, 2))
                        act.activation(gated[:, a, :].rearrange("p (e c) -> p e c", e=2),
                                       PS[:, 1 + a, 0:4 * I].rearrange("p (e c) -> p e c", e=2)[:, :, 0:I],
                                       ACT.Silu).then_inc(q["gate"], 1)
                run_slots(act, step, 1, 0, NP)

            @block.vector
            def _(dve):
                def step(s, u, h):
                    a = (u + 1) % 2
                    if real(s + 1, NP):
                        dve.wait_ge(q["gate"], q.nth("gate", s + 1))
                        if past(s + 1, 2):
                            dve.wait_ge(q["hidT"], q.nth("hidT", s + 1, 2))
                        dve.tensor_tensor(hid[:, a, :].rearrange("p (k c) -> p k c", c=I)[:, 0:4:3, :],
                                          gated[:, a, :].rearrange("p (e c) -> p e c", e=2),
                                          PS[:, 1 + a, 0:4 * I].rearrange("p (e c) -> p e c", e=2)[:, :, I:2 * I],
                                          ALU.mult).then_inc(q["hid"], 1)
                    if real(s, NP):
                        dve.wait_ge(q["down"], q.nth("down", s))
                        if not isinstance(s, int) or s >= 2:
                            dve.wait_ge(q[f"store{u}"], h * 16)
                        dve.tensor_copy(res[:, u, :], PS[:, 4 + u, 0:2 * D]).then_inc(q["ress"], 1)
                run_slots(dve, step, 1, 0, NP)

        with ExitStack() as inner:
            yk = inner.enter_context(nc.sbuf_tensor("e3c_yk", [S, 2, K * D], F32))
            part = inner.enter_context(nc.sbuf_tensor("e3c_part", [S, 2, K * D], F32))
            at = inner.enter_context(nc.sbuf_tensor("e3c_at", [S, 2, K], U32))
            block = inner.enter_context(nc.Block())

            @block.gpsimd
            def _(pool):
                def step(s, u, h):
                    pool.wait_ge(q["atc"], q.nth("atc", s))
                    if past(s, 2):
                        pool.wait_ge(q["sum"], q.nth("sum", s, 2))
                    pool.sem_inc(q["held"], 1)
                    for k in range(K):
                        pool.indirect_dma_start(
                            out=yk[:, u, k * D:(k + 1) * D], out_offset=None, in_=results[:, :],
                            in_offset=bass.IndirectOffsetOnAxis(ap=at[:, u, k:k + 1], axis=0)) \
                            .then_inc(q[f"gath{u}"], 16)
                run_slots(pool, step, 0, 0)

            @block.vector
            def _(dve):
                def step(s, u, h):
                    a = (u + 1) % 2
                    if real(s + 1):
                        if not isinstance(s, int) or s + 1 >= 2:
                            dve.wait_ge(q[f"gath{a}"], (h + u) * (16 * K))
                        dve.tensor_copy(at[:, a, :], seq(results_at, s + 1)).then_inc(q["atc"], 1)
                    if not real(s):
                        return
                    dve.wait_ge(q[f"gath{u}"], h * (16 * K) + 16 * K)
                    if not isinstance(s, int) or s >= 2:
                        dve.wait_ge(q[f"out{u}"], h * 16)
                    for k in range(K):
                        src = seq(m.X, s) if k == 0 else part[:, u, (k - 1) * D:k * D]
                        dve.scalar_tensor_tensor(out=part[:, u, k * D:(k + 1) * D], in0=yk[:, u, k * D:(k + 1) * D],
                                                 scalar=seq(weight, s)[:, k:k + 1], in1=src, op0=ALU.mult, op1=ALU.add) \
                            .then_inc(q["sum" if k == K - 1 else f"sum{k}"], 1)
                        if k < K - 1:
                            dve.wait_ge(q[f"sum{k}"], q.nth(f"sum{k}", s))
                run_slots(dve, step, 1, 0)

            @block.sync
            def _(sp):
                def step(s, u, h):
                    sp.wait_ge(q["sum"], q.nth("sum", s))
                    sp.dma_start(t["out"][bass.ds(s, 1), :, :].rearrange("b s d -> (b s) d"),
                                 part[:, u, (K - 1) * D:K * D]).then_inc(q[f"out{u}"], 16)
                run_slots(sp, step, 0, 0)
                for u in range(2):
                    sp.wait_ge(q[f"out{u}"], B // 2 * 16)


def program(nc, t):
    with ExitStack() as ctx:
        def sb(name, shape, dt=F32):
            return ctx.enter_context(nc.sbuf_tensor(name, shape, dt))

        def sem(name):
            return ctx.enter_context(nc.semaphore(name))

        m = Named()
        m.X = sb("X", [S, B, D])
        m.STATS = sb("STATS", [S, B, 6])
        m.MEAN = sb("MEAN", [S, B])
        m.RSTD = sb("RSTD", [S, B])
        m.norm_tmp = sb("norm_tmp", [S, 4, B])
        m.MINUS_HALF = sb("MINUS_HALF", [S, B])
        m.IDENT = sb("IDENT", [S, S])
        m.IDENT_BF = sb("IDENT_BF", [S, S], BF16)
        m.WIDTH_TOKENS = sb("WIDTH_TOKENS", [S, D])
        m.WIDTH_FEATURES = sb("WIDTH_FEATURES", [D, S])
        m.HEAD = {8: sb("HEAD8", [D, 4]), 16: sb("HEAD16", [D, 2])}
        m.scratch = sb("scratch", [S, 2])
        m.PS = ctx.enter_context(nc.psum_tensor("PS", [128, 8, BANK], F32))
        m.s_weights = sem("weights")
        m.s_norm_a = sem("norm_parts")
        m.s_norm_b = sem("norm_rstd")
        m.norms = m.weight_loads = m.ctx_loads = m.mask_loads = m.preps = 0
        m.at = Signals(ctx, nc, "at", [
            "prep", "fold", "ctx0", "ctx1", "mask0", "mask1",
            "y", "yTps", "yT", "proj", "q", "k", "k_by_scalar", "v", "scores0", "scores1", "sfree0", "sfree1",
            "copied0", "copied1", "distance0", "distance1", "mx0", "mx1", "pv", "oT", "back",
            "rec", "O", "OTps", "OT", "out", "bias", "x", "T0", "T1", "xT", "PT0", "PT1", "PT2", "PT3",
            "P0", "P1", "P2", "P3", "passed", "r1", "t1", "r2", "r2cut", "abs0", "abs1", "abs2", "abs3",
            "y0", "yraw", "istat", "imv", "ivar", "irstd", "Oall", "tmp"])
        load_x(nc, m, t)
        for layer in (layer0_cross, layer0_experts, layer1_cross, layer1_experts, layer2_cross,
                      layer2_self, layer3_cross, layer3_experts):
            layer(nc, m, t)
            m.norms += 1


def load_x(nc, m, t):
    with ExitStack() as ctx:
        parts = 8
        s_x = [ctx.enter_context(nc.semaphore(f"x_in{n}")) for n in range(parts)]
        s_const = ctx.enter_context(nc.semaphore("const_in"))
        block = ctx.enter_context(nc.Block())
        consts = [(m.IDENT, "c_ident"), (m.WIDTH_TOKENS, "c_width_tokens"), (m.WIDTH_FEATURES, "c_width_features"),
                  (m.HEAD[8], "c_head8"), (m.HEAD[16], "c_head16")]

        @block.sync
        def _(sp):
            x = t["x"].rearrange("b s d -> s b d")
            for n in range(parts):
                c = slice(n * B // parts, (n + 1) * B // parts)
                sp.dma_start(m.X[:, c, :], x[:, c, :]).then_inc(s_x[n], 16)
            for dst, name in consts:
                sp.dma_start(dst[:, :], t[name]).then_inc(s_const, 16)
            sp.wait_ge(s_const, 16 * len(consts))

        @block.gpsimd
        def _(pool):
            pool.memset(m.MINUS_HALF[:, :], -0.5)
            pool.memset(m.scratch[:, :], 0.0)

        @block.vector
        def _(dve):
            dve.wait_ge(s_const, 16 * len(consts))
            dve.tensor_copy(m.IDENT_BF[:, :], m.IDENT[:, :])
            for b in range(B):
                if b % (B // parts) == 0:
                    dve.wait_ge(s_x[b // (B // parts)], 16)
                dve.bn_stats(m.STATS[:, b, :], m.X[:, b, :])


def layer1_cross(nc, m, t):
    n = "L1_xattn_"
    w = Named()
    w.Wq, w.Wk, w.Wv, w.Wo = t[n + "Wq"], t[n + "Wkv"][:, 0:D], t[n + "Wkv"][:, D:2 * D], t[n + "Wo"]
    w.bq, w.bk, w.bv, w.bo = t[n + "bq"], t[n + "bkv"][0:D], t[n + "bkv"][D:2 * D], t[n + "bo"]
    attention_layer(nc, m, 0, w, heads=16, keys=C, scale=8 ** -0.5, context=t["ctxT"])


def layer2_cross(nc, m, t):
    n = "L2_xattn_"
    w = Named()
    w.Wq, w.Wk, w.Wv, w.Wo = (t[n + f"W{c}T"] for c in "qkvo")
    w.bq, w.bk, w.bv, w.bo = (t[n + f"b{c}"] for c in "qkvo")
    attention_layer(nc, m, 1, w, heads=16, keys=C, scale=8 ** -0.5, context=t["ctxT"], mask=t["mask"])


def layer2_self(nc, m, t):
    n = "L2_ffn_"
    w = Named()
    w.Wq, w.Wk, w.Wv, w.Wo = (t[n + f"{c}_wT"] for c in "qkvo")
    w.bq, w.bk, w.bv, w.bo = (t[n + f"{c}_b"] for c in "qkvo")
    w.nw, w.nb = t[n + "norm_w"], t[n + "norm_b"]
    attention_layer(nc, m, 2, w, heads=8, keys=S, scale=D ** -0.5, inner=True)


def layer3_cross(nc, m, t):
    n = "L3_xattn_"
    w = Named()
    w.U, w.V = [t[n + f"U{c}T"] for c in "qkvo"], [t[n + f"V{c}T"] for c in "qkvo"]
    w.bq, w.bk, w.bv, w.bo = (t[n + f"b{c}"] for c in "qkvo")
    attention_layer(nc, m, 3, w, heads=16, keys=C, scale=8 ** -0.5, context=t["ctxT_reversed"], topk=64,
                    lowrank=True)



def laid_out(inputs):
    import numpy as np
    a = {n: np.asarray(v) for n, v in inputs.items()}
    ctx = a["ctx_1024"]
    out = {"x": a["x"], "ctxT": ctx.transpose(2, 0, 1), "ctxT_reversed": ctx[:, ::-1].transpose(2, 0, 1),
           "mask": a["mask_Bx1xSxS2_fk0"][:, 0].transpose(1, 0, 2), "q_masks": a["mask_BxS2_ik0"]}
    for n, v in a.items():
        if n[0:2] in ("L0", "L1", "L2", "L3"):
            out[n] = v
    out["L0_ffn_gate_w"] = a["L0_ffn_gate_w"].T
    for n in ("L0_ffn_w1", "L0_ffn_w3"):
        out[n] = a[n].transpose(1, 0, 2).reshape(D, -1)
    out["L0_ffn_w2"] = a["L0_ffn_w2"].reshape(8, 128, D).transpose(1, 0, 2)
    out["L1_ffn_gate_w"] = a["L1_ffn_gate_w"].T
    for n in ("L1_ffn_w1", "L1_ffn_w2", "L1_ffn_w3"):
        out[n] = a[n].transpose(2, 0, 1)
    for n in ("L1_ffn_b1", "L1_ffn_b2", "L1_ffn_sw1", "L1_ffn_sw2"):
        out[n] = a[n].T
    out["L1_ffn_sw3"] = a["L1_ffn_sw3"].reshape(D, 2, 128).transpose(2, 1, 0)
    out["L3_ffn_w1"] = a["L3_ffn_w1"].transpose(1, 0, 2)
    out["L3_ffn_w2"] = a["L3_ffn_w2"].reshape(32, 128, D).transpose(1, 0, 2)
    out["c_before"] = (np.arange(S)[:, None] < np.arange(S)[None, :]).astype(np.float32)
    out["c_slot0"] = (np.zeros((S, 1)) + np.arange(64)[None, :] * 128 + 1).astype(np.float32)
    for n in ("L2_xattn_Wq", "L2_xattn_Wk", "L2_xattn_Wv", "L2_xattn_Wo", "L2_ffn_q_w", "L2_ffn_k_w",
              "L2_ffn_v_w", "L2_ffn_o_w", "L3_xattn_Uq", "L3_xattn_Uk", "L3_xattn_Uv", "L3_xattn_Uo",
              "L3_xattn_Vq", "L3_xattn_Vk", "L3_xattn_Vv", "L3_xattn_Vo"):
        out[n + "T"] = out.pop(n).T
    f, tok = np.arange(D), np.arange(S)
    width = (f[None, :] < (D >> (tok[:, None] // 32))).astype(np.float32)
    out["c_ident"] = np.eye(S, dtype=np.float32)
    out["c_width_tokens"] = width
    out["c_width_features"] = width.T
    row, pair, expert = np.arange(72), np.arange(8), np.arange(8)
    half = 2 * pair[None, :, None] + (f // 64)[None, None, :]
    out["c_pick_pairs"] = ((row[:, None, None] % 16 == half) & (row[:, None, None] < 48)).astype(np.float32)
    mine = row[:, None] % 8 == expert[None, :]
    out["c_pick_weight"] = np.repeat((mine & (row[:, None] < 24))[:, :, None], D, 2).astype(np.float32)
    part = 24 + 8 * np.arange(3)
    out["c_pick_bias"] = (mine[:, None, :] & (row[:, None, None] // 8 * 8 == part[None, :, None])).astype(np.float32)
    for dh in (8, 16):
        out[f"c_head{dh}"] = ((f[:, None] % 32) // dh == np.arange(32 // dh)[None, :]).astype(np.float32)
    return out


def kernel(**inputs):
    import numpy as _np
    import concourse.bacc as _bacc
    from concourse import mybir as _mybir
    from concourse.bass_utils import run_bass_kernel_spmd as _run

    nc = _bacc.Bacc("TRN2", target_bir_lowering=False, num_devices=1)
    arrays, t = {}, {}
    for name, a in laid_out(inputs).items():
        a = _np.ascontiguousarray(a)
        arrays[f"in_{name}"] = a
        t[name] = nc.dram_tensor(f"in_{name}", a.shape, _mybir.dt.from_np(a.dtype), kind="ExternalInput").ap()
    t["out"] = nc.dram_tensor("out", (B, S, D), _mybir.dt.float32, kind="ExternalOutput").ap()
    program(nc, t)
    r = _run(nc, [arrays], core_ids=[0])
    return r.results[0]["out"]
```
